# Optimizing a Trainium2 kernel written in Bass

```python
import numpy as np
import jax
import jax.numpy as jnp

def _softmax(x, axis=-1):
    return jax.nn.softmax(x, axis=axis)

def _gelu(x):
    return jax.nn.gelu(x, approximate=True)

def _silu(x):
    return jax.nn.silu(x)

def _sigmoid(x):
    return jax.nn.sigmoid(x)

def _layernorm(x, axis=-1, eps=1e-05):
    m = jnp.mean(x, axis=axis, keepdims=True)
    v = jnp.var(x, axis=axis, keepdims=True)
    return (x - m) / jnp.sqrt(v + eps)

def _scatter_add(tgt, idx, src, axis=0):
    return tgt.at[idx].add(src)

def _segment_sum(src, seg, n):
    return jax.ops.segment_sum(src, seg, n)
kernel_name = 'mk_flamingo_gated_d1_seqx_r2_c97a7b'

def setup_inputs(seed: int=0):
    np.random.seed(seed)
    _w = jnp.asarray

    def _rec_inputs():
        import jax
        import jax.numpy as jnp
        _rk = jax.random.key(seed)
        x = -0.0002928 + 1 * jax.random.normal(jax.random.fold_in(_rk, 1), (8, 224, 512), jnp.float32)
        _lenS = 224 - jax.random.randint(jax.random.fold_in(_rk, 7), (8,), 0, max(1, 224 // 4) + 1, jnp.int32)
        _lenS2 = 750 - jax.random.randint(jax.random.fold_in(_rk, 8), (8,), 0, max(1, 750 // 4) + 1, jnp.int32)
        _ctx_1024P = jax.random.normal(jax.random.fold_in(_rk, 11), (8, 16, 512), jnp.float32)
        _ctx_1024c = jax.random.dirichlet(jax.random.fold_in(_rk, 511), 0.3 * jnp.ones((16,), jnp.float32), (8, 750))
        _ctx_1024t = jnp.einsum('bsk,bkd->bsd', _ctx_1024c, _ctx_1024P)
        _ctx_1024t = _ctx_1024t * jax.lax.rsqrt(jnp.mean(jnp.square(_ctx_1024t)) + 1e-12) * 0.953939
        ctx_1024 = -1.39393e-06 + 0.999914 * (_ctx_1024t + 0.3 * jax.random.normal(jax.random.fold_in(_rk, 611), (8, 750, 512), jnp.float32))
        _validS = jnp.arange(224)[None, :] < _lenS[:, None]
        _validS2 = jnp.arange(750)[None, :] < _lenS2[:, None]
        _causal = jnp.tril(jnp.ones((224, 224), dtype=bool))
        mask_Bx1xSxS2_ik0 = jnp.where(jnp.broadcast_to(_validS2[:, None, None, :], (8, 1, 224, 750)), 0, 1).astype(jnp.int32)
        _g = jax.random.normal(jax.random.fold_in(_rk, 9001), (2, 1), jnp.float32)
        _g = jnp.sign(_g) * jnp.maximum(jnp.abs(_g), 1.0) + (_g == 0) * 1.0
        g_xattn = _g[0]
        g_ffn = _g[1]
        return (x, ctx_1024, mask_Bx1xSxS2_ik0, g_xattn, g_ffn)
    x, ctx_1024, mask_Bx1xSxS2_ik0, g_xattn, g_ffn = _rec_inputs()

    def _L0_xattn_setup():
        import jax, jax.numpy as jnp
        import numpy as np
        D_MODEL = 512
        N_HEADS = 16
        D_K = D_MODEL // N_HEADS
        B, S = (2, 1024)

        def _rope_emb(seq_len, d_k):
            inv_freq = 1.0 / 10000.0 ** (jnp.arange(0, d_k, 2, dtype=jnp.float32) / d_k)
            t = jnp.arange(seq_len, dtype=jnp.float32)
            freqs = jnp.outer(t, inv_freq)
            return jnp.concatenate([freqs, freqs], axis=-1)

        def _rotate_half(x):
            x1, x2 = jnp.split(x, 2, axis=-1)
            return jnp.concatenate([-x2, x1], axis=-1)

        def _apply_rope(x, emb):
            return x * jnp.cos(emb)[None, None] + _rotate_half(x) * jnp.sin(emb)[None, None]
        key = jax.random.key(seed)
        ks = jax.random.split(key, 7)
        scale = 1.0 / np.sqrt(D_MODEL)
        q = jax.random.normal(ks[0], (B, S, D_MODEL), dtype=jnp.float32)
        k = jax.random.normal(ks[1], (B, S, D_MODEL), dtype=jnp.float32)
        v = jax.random.normal(ks[2], (B, S, D_MODEL), dtype=jnp.float32)
        W_q = jax.random.normal(ks[3], (D_MODEL, D_MODEL), dtype=jnp.float32) * scale
        W_k = jax.random.normal(ks[4], (D_MODEL, D_MODEL), dtype=jnp.float32) * scale
        W_v = jax.random.normal(ks[5], (D_MODEL, D_MODEL), dtype=jnp.float32) * scale
        W_o = jax.random.normal(ks[6], (D_MODEL, D_MODEL), dtype=jnp.float32) * scale
        mask = jnp.tril(jnp.ones((S, S), dtype=jnp.int32))[None, None]
        mask = jnp.broadcast_to(mask, (B, 1, S, S))
        return {'query': q, 'key': k, 'value': v, 'mask': mask, 'W_q': W_q, 'W_k': W_k, 'W_v': W_v, 'W_o': W_o}
    _L0_xattn_all = _L0_xattn_setup()
    _L0_xattn_in = {k: v for k, v in _L0_xattn_all.items() if k in ('W_q', 'W_k', 'W_v', 'W_o')}
    del _L0_xattn_all

    def _L0_ffn_setup():
        import jax, jax.numpy as jnp
        import numpy as np
        CAPACITY = 2
        B, S, D, E, I = (4, 2048, 512, 8, 2048)
        key = jax.random.key(seed)
        k0, k1, k2, k3, k4 = jax.random.split(key, 5)
        x = jax.random.normal(k0, (B, S, D), dtype=jnp.float32)
        gate_w = jax.random.normal(k1, (E, D), dtype=jnp.float32) * 0.006
        w_gate = jax.random.normal(k2, (E, I, D), dtype=jnp.float32) * (1.0 / np.sqrt(D))
        w_up = jax.random.normal(k3, (E, I, D), dtype=jnp.float32) * (1.0 / np.sqrt(D))
        w_down = jax.random.normal(k4, (E, D, I), dtype=jnp.float32) * (1.0 / np.sqrt(I))
        return {'x': x, 'gate_w': gate_w, 'w_gate': w_gate, 'w_up': w_up, 'w_down': w_down}
    _L0_ffn_all = _L0_ffn_setup()
    _L0_ffn_in = {k: v for k, v in _L0_ffn_all.items() if k in ('gate_w', 'w_gate', 'w_up', 'w_down')}
    del _L0_ffn_all
    return {'x': x, 'ctx_1024': ctx_1024, 'mask_Bx1xSxS2_ik0': mask_Bx1xSxS2_ik0, 'g_xattn': g_xattn, 'g_ffn': g_ffn, 'L0_xattn_W_q': _L0_xattn_in['W_q'], 'L0_xattn_W_k': _L0_xattn_in['W_k'], 'L0_xattn_W_v': _L0_xattn_in['W_v'], 'L0_xattn_W_o': _L0_xattn_in['W_o'], 'L0_ffn_gate_w': _L0_ffn_in['gate_w'], 'L0_ffn_w_gate': _L0_ffn_in['w_gate'], 'L0_ffn_w_up': _L0_ffn_in['w_up'], 'L0_ffn_w_down': _L0_ffn_in['w_down']}

def reference(x, ctx_1024, mask_Bx1xSxS2_ik0, g_xattn, g_ffn, L0_xattn_W_q, L0_xattn_W_k, L0_xattn_W_v, L0_xattn_W_o, L0_ffn_gate_w, L0_ffn_w_gate, L0_ffn_w_up, L0_ffn_w_down):
    import jax
    import jax.numpy as jnp

    def _L0_xattn_ref(query, key, value, mask, W_q, W_k, W_v, W_o):
        import jax, jax.numpy as jnp
        import numpy as np
        D_MODEL = 512
        N_HEADS = 16
        D_K = D_MODEL // N_HEADS
        B, S = (2, 1024)

        def _rope_emb(seq_len, d_k):
            inv_freq = 1.0 / 10000.0 ** (jnp.arange(0, d_k, 2, dtype=jnp.float32) / d_k)
            t = jnp.arange(seq_len, dtype=jnp.float32)
            freqs = jnp.outer(t, inv_freq)
            return jnp.concatenate([freqs, freqs], axis=-1)

        def _rotate_half(x):
            x1, x2 = jnp.split(x, 2, axis=-1)
            return jnp.concatenate([-x2, x1], axis=-1)

        def _apply_rope(x, emb):
            return x * jnp.cos(emb)[None, None] + _rotate_half(x) * jnp.sin(emb)[None, None]
        b = query.shape[0]

        def proj(x, W):
            y = jnp.einsum('bsd,ed->bse', x, W)
            return y.reshape(b, -1, N_HEADS, D_K).transpose(0, 2, 1, 3)
        Q = proj(query, W_q)
        K = proj(key, W_k)
        V = proj(value, W_v)
        emb_q = _rope_emb(Q.shape[2], D_K)
        emb_k = _rope_emb(K.shape[2], D_K)
        Q = _apply_rope(Q, emb_q)
        K = _apply_rope(K, emb_k)
        scores = jnp.einsum('bhqd,bhkd->bhqk', Q, K) / jnp.sqrt(jnp.float32(D_K))
        scores = jnp.where(mask == 0, jnp.float32(-jnp.inf), scores)
        attn = jax.nn.softmax(scores, axis=-1)
        ctx = jnp.einsum('bhqk,bhkd->bhqd', attn, V)
        ctx = ctx.transpose(0, 2, 1, 3).reshape(b, -1, D_MODEL)
        return jnp.einsum('bsd,ed->bse', ctx, W_o)

    def _L0_ffn_ref(x, gate_w, w_gate, w_up, w_down):
        import jax, jax.numpy as jnp
        import numpy as np
        CAPACITY = 2
        B, S, D = x.shape
        E = gate_w.shape[0]
        k = S // E * CAPACITY
        logits = jnp.einsum('bsd,ed->bse', x, gate_w)
        affinity = jax.nn.softmax(logits, axis=-1)
        affinity = jnp.transpose(affinity, (0, 2, 1))
        gating, idx = jax.lax.top_k(affinity, k)
        bidx = jnp.arange(B)[:, None, None]
        x_in = x[bidx, idx]
        h = jax.nn.silu(jnp.einsum('bekd,eid->beki', x_in, w_gate)) * jnp.einsum('bekd,eid->beki', x_in, w_up)
        x_e = jnp.einsum('beki,edi->bekd', h, w_down)
        out = jnp.zeros_like(x).at[bidx, idx].add(gating[..., None] * x_e)
        return out
    x = x + jnp.tanh(g_xattn[0]) * _L0_xattn_ref(_layernorm(x, axis=-1), ctx_1024, ctx_1024, mask_Bx1xSxS2_ik0, L0_xattn_W_q, L0_xattn_W_k, L0_xattn_W_v, L0_xattn_W_o)
    x = x + jnp.tanh(g_ffn[0]) * _L0_ffn_ref(_layernorm(x, axis=-1), L0_ffn_gate_w, L0_ffn_w_gate, L0_ffn_w_up, L0_ffn_w_down)
    return x

_drawn_inputs = setup_inputs


def setup_inputs(seed=0):
    import zlib

    import numpy as np

    out = dict(_drawn_inputs(seed))
    spreads = {}
    factors = {}
    for name, (base, spread) in spreads.items():
        noise = np.random.default_rng([zlib.crc32(name.encode()), seed]).standard_normal(out[name].shape)
        drawn = base * np.exp(spread * noise) if base else spread * noise
        out[name] = jnp.asarray(drawn.astype(out[name].dtype))
    for name, factor in factors.items():
        out[name] = (out[name] * factor).astype(out[name].dtype)
    return out
```

```python
from contextlib import ExitStack

import concourse.bass as bass
from concourse import mybir

F32 = mybir.dt.float32
F32R = mybir.dt.float32r
BF16 = mybir.dt.bfloat16
I32 = mybir.dt.int32
U32 = mybir.dt.uint32
ALU = mybir.AluOpType
ACT = mybir.ActivationFunctionType
AX_X = mybir.AxisListType.X
ds = bass.ds

B, S, D = 8, 224, 512
S2 = 750
H, DK = 16, 32
E, I = 8, 2048
TOPK = S // E * 2
P = 128
DC = D // P
QP, QC = 112, S // 112
KP, KC = 125, S2 // 125
KN = 376
SK = 2 * KN
HG, NG = 4, H // 4
VH = 8
VW = 2 * DK + 1
PAIR = 2 * S
SCALE = float(DK) ** -0.5
EPS = 1e-5
MASKED = -(2.0 ** 100)
SLOTS = B * TOPK
RP, RG = 2 * TOPK, B // 2
IC = I // P
UNIT = 2 * DC * P
GU, DU = IC, IC // 2
NU = GU + DU
NRAW = 4
LEAD = 3
WAYS = 32

C_ID = 0
C_COS = C_ID + P
C_SIN = C_COS + SK
C_KSEL = C_SIN + SK
C_ROW = C_KSEL + HG
C_END = C_ROW + B * TOPK

ROTATE = [(d + DK // 2) % DK for d in range(DK)]


def after(eng, sem, value):
    if not (isinstance(value, int) and value <= 0):
        eng.wait_ge(sem, value)


def program(nc, ctxT, x, maskq, maskt, wk, wv, wq, wo, gatew, gx, gf, wstream, consts, out):
    kd = nc.dram_tensor("k_split", (B, NG, 2, P, SK), F32, kind="Internal").ap()
    vd = nc.dram_tensor("v_split", (B, 2, KP, KC * VH * VW), F32, kind="Internal").ap()
    xn_rows = nc.dram_tensor("xn_rows", (B * S, D), F32, kind="Internal").ap()
    out_rows = out.rearrange("b s d -> (b s) d")

    with ExitStack() as top:
        def sem(name):
            return top.enter_context(nc.semaphore(name))

        def sb(stack, name, shape, dt=F32):
            return stack.enter_context(nc.sbuf_tensor(name, shape, dt))

        def ps(stack, name, shape, dt=F32):
            return stack.enter_context(nc.psum_tensor(name, shape, dt))

        cst = sb(top, "cst", [P, C_END])
        ident = cst[:, C_ID:C_ID + P]
        cos, sin = cst[:, C_COS:C_COS + SK], cst[:, C_SIN:C_SIN + SK]
        gate_all = sb(top, "gate_all", [E, B, TOPK])
        row_all = sb(top, "row_all", [E, B, TOPK])
        gains = sb(top, "gains", [P, 2])

        project_context(nc, sem, sb, ps, ctxT, wk, wv, gx, gf, consts, kd, vd, cst, ident, cos, sin, gains)
        attend(nc, sem, sb, ps, x, maskq, maskt, wq, wo, gatew, kd, vd, xn_rows, out, cst, ident,
               cos, sin, gains, gate_all, row_all)
        experts(nc, sem, sb, ps, wstream, xn_rows, out_rows, cst, ident, gains, gate_all, row_all)


def project_context(nc, sem, sb, ps, ctxT, wk, wv, gx, gf, consts, kd, vd, cst, ident, cos, sin, gains):
    with ExitStack() as st:
        wraw = sb(st, "wraw", [P, 2, DC, D])
        w_hi = sb(st, "w_hi", [P, 2, DC, D], F32R)
        w_lo = sb(st, "w_lo", [P, 2, DC, D], F32R)
        graw = sb(st, "graw", [P, 2])
        c_raw = [sb(st, f"c_raw{j}", [P, DC, S2]) for j in range(2)]
        c_hi = [sb(st, f"c_hi{j}", [P, DC, SK], F32R) for j in range(2)]
        c_lo = [sb(st, f"c_lo{j}", [P, DC, SK], F32R) for j in range(2)]
        k_raw = [sb(st, f"k_raw{j}", [P, SK]) for j in range(2)]
        k_cos = [sb(st, f"k_cos{j}", [P, SK]) for j in range(2)]
        k_rot = [sb(st, f"k_rot{j}", [P, SK]) for j in range(2)]
        k_split = [sb(st, f"k_split{j}", [P, 2, SK], F32R) for j in range(2)]
        v_out = sb(st, "v_out", [KP, 2, KC, VH, VW], F32R)
        k_ps = [ps(st, f"k_ps{j}", [P, 2, 512]) for j in range(2)]
        v_ps = [ps(st, f"v_ps{j}", [P, 512]) for j in range(4)]

        weights_in, consts_in, gains_in = sem("weights_in"), sem("consts_in"), sem("gains_in")
        gains_done = sem("gains_done")
        wsplit_hi, wsplit_lo, pads_set = sem("wsplit_hi"), sem("wsplit_lo"), sem("pads_set")
        ctx_in = [sem(f"ctx_in{j}") for j in range(2)]
        ctx_hi, ctx_lo = sem("ctx_hi"), [sem(f"ctx_lo{j}") for j in range(2)]
        k_made, v_made = sem("k_made"), [sem(f"v_made{j}") for j in range(2)]
        kraw_done = [sem(f"kraw_done{j}") for j in range(2)]
        kcos_done, krot_done, ksin_done, ksum_done = sem("kcos_done"), sem("krot_done"), sem("ksin_done"), sem("ksum_done")
        khi_done, klo_done = sem("khi_done"), [sem(f"klo_done{j}") for j in range(2)]
        vhi_done, vlo_done = sem("vhi_done"), [sem(f"vlo_done{j}") for j in range(4)]
        k_stored = [sem(f"k_stored{j}") for j in range(2)]
        v_stored = sem("v_stored")

        with nc.Block() as block:
            @block.sync
            def _(sp):
                def hold(s_, v_):
                    sp.wait_ge(s_, v_)
                    sp.nop(nofuse=True)

                sp.dma_start(wraw[:, 0], wk).then_inc(weights_in, 16)
                sp.dma_start(wraw[:, 1], wv).then_inc(weights_in, 16)
                sp.dma_start(graw[:, 0:1], gx).then_inc(gains_in, 16)
                sp.dma_start(graw[:, 1:2], gf).then_inc(gains_in, 16)
                with sp.Fori(0, B // 2) as i:
                    for j in range(2):
                        hold(ctx_lo[j], DC * i)
                        sp.dma_start(c_raw[j][:], ctxT[ds(2 * i + j, 1)].rearrange("o p c n -> p (o c) n")).then_inc(ctx_in[j], 16)

            @block.gpsimd
            def _(pool):
                pool.dma_start(cst[:], consts).then_inc(consts_in, 16)
                for j in range(2):
                    nc.gpsimd.memset(c_hi[j][:, :, S2:SK].bitcast(F32), 0.0)
                    nc.gpsimd.memset(c_lo[j][:, :, S2:SK].bitcast(F32), 0.0)
                nc.gpsimd.memset(v_out[:, :, :, :, 2 * DK:VW].bitcast(F32), 1.0).then_inc(pads_set, 1)
                pool.wait_ge(consts_in, 16)
                with pool.Fori(0, B // 2) as i:
                    for g in range(2 * NG):
                        pool.wait_ge(krot_done, 2 * NG * i + g + 1)
                        nc.gpsimd.tensor_tensor(k_rot[g % 2][:], k_rot[g % 2][:], sin, ALU.mult).then_inc(ksin_done, 1)

            @block.scalar
            def _(act):
                act.wait_ge(gains_in, 32)
                nc.scalar.activation(gains[:], graw[:], ACT.Tanh).then_inc(gains_done, 1)
                act.wait_ge(weights_in, 32)
                nc.scalar.activation(w_hi[:], wraw[:], ACT.Copy).then_inc(wsplit_hi, 1)

                def store_k(i, j, g):
                    act.wait_ge(klo_done[g % 2], NG * i + 2 * j + g // 2 + 1)
                    act.dma_start(kd[ds(2 * i + j, 1), g].rearrange("o h p n -> p (o h) n"), k_split[g % 2][:].bitcast(F32)).then_inc(k_stored[g % 2], 16)

                with act.Fori(0, B // 2) as i:
                    for j in range(2):
                        act.wait_ge(ctx_in[j], 16 * i + 16)
                        act.wait_ge(v_made[j], KC * i)
                        for c in range(DC):
                            nc.scalar.activation(c_hi[j][:, c, 0:S2], c_raw[j][:, c, :], ACT.Copy).then_inc(ctx_hi, 1)
                        for g in range(NG):
                            act.wait_ge(k_made, 2 * NG * i + NG * j + g + 1)
                            act.wait_ge(klo_done[g % 2], NG * i + 2 * j + g // 2)
                            nc.scalar.activation(k_raw[g % 2][:].rearrange("p (a n) -> p a n", a=2),
                                                 k_ps[g % 2][:, :, 0:KN], ACT.Copy).then_inc(kraw_done[g % 2], 1)
                            if g:
                                store_k(i, j, g - 1)
                            act.wait_ge(ksum_done, 2 * NG * i + NG * j + g + 1)
                            act.wait_ge(k_stored[g % 2], 16 * (NG * i + 2 * j + g // 2))
                            nc.scalar.activation(k_split[g % 2][:, 0], k_cos[g % 2][:], ACT.Copy).then_inc(khi_done, 1)
                        for c in range(KC):
                            act.wait_ge(v_made[j], KC * i + c + 1)
                            if c == 0:
                                act.wait_ge(v_stored, 32 * (2 * i + j))
                            nc.scalar.activation(v_out[:, :, c, :, 0:DK],
                                                 v_ps[(KC * j + c) % 4][0:KP, :].rearrange("p (a h d) -> p a h d", a=2, h=VH),
                                                 ACT.Copy).then_inc(vhi_done, 1)
                            if c == 0:
                                store_k(i, j, NG - 1)
                        for c in range(KC - 4, KC):
                            act.wait_ge(vlo_done[(KC * j + c) % 4], 3 * i + (KC * j + c) // 4 + 1)
                        for a in range(2):
                            act.dma_start(vd[ds(2 * i + j, 1), a].rearrange("o p n -> p (o n)"),
                                          v_out[:, a].bitcast(F32).rearrange("p c h w -> p (c h w)")).then_inc(v_stored, 16)
                for s in range(2):
                    act.wait_ge(k_stored[s], 16 * B * NG // 2)
                act.wait_ge(v_stored, 32 * B)

            @block.vector
            def _(dve):
                dve.wait_ge(wsplit_hi, 1)
                nc.vector.tensor_tensor(w_lo[:], wraw[:], w_hi[:], ALU.subtract).then_inc(wsplit_lo, 1)
                dve.wait_ge(pads_set, 1)
                dve.wait_ge(consts_in, 16)
                with dve.Fori(0, B // 2) as i:
                    for j in range(2):
                        for c in range(DC):
                            dve.wait_ge(ctx_hi, 2 * DC * i + DC * j + c + 1)
                            nc.vector.tensor_tensor(c_lo[j][:, c, 0:S2], c_raw[j][:, c, :], c_hi[j][:, c, 0:S2],
                                                    ALU.subtract).then_inc(ctx_lo[j], 1)
                        for g in range(NG):
                            n, s = 2 * NG * i + NG * j + g, g % 2
                            dve.wait_ge(kraw_done[s], NG * i + 2 * j + g // 2 + 1)
                            nc.vector.tensor_tensor(k_cos[s][:], k_raw[s][:], cos, ALU.mult).then_inc(kcos_done, 1)
                            nc.vector.stream_shuffle(k_rot[s][:], k_raw[s][:], ROTATE).then_inc(krot_done, 1)
                            dve.wait_ge(kcos_done, n + 1)
                            dve.wait_ge(ksin_done, n + 1)
                            nc.vector.tensor_tensor(k_cos[s][:], k_cos[s][:], k_rot[s][:], ALU.add).then_inc(ksum_done, 1)
                            dve.wait_ge(khi_done, n + 1)
                            nc.vector.tensor_tensor(k_split[s][:, 1], k_cos[s][:], k_split[s][:, 0], ALU.subtract).then_inc(klo_done[s], 1)
                        for c in range(KC):
                            q = (KC * j + c) % 4
                            dve.wait_ge(vhi_done, 2 * KC * i + KC * j + c + 1)
                            nc.vector.tensor_tensor(v_out[:, :, c, :, DK:2 * DK],
                                                    v_ps[q][0:KP, :].rearrange("p (a h d) -> p a h d", a=2, h=VH),
                                                    v_out[:, :, c, :, 0:DK], ALU.subtract).then_inc(vlo_done[q], 1)

            @block.tensor
            def _(pe):
                pe.wait_ge(wsplit_lo, 1)
                pe.wait_ge(pads_set, 1)
                with pe.Fori(0, B // 2) as i:
                    for j in range(2):
                        for g in range(NG):
                            pe.wait_ge(kraw_done[g % 2], NG * i + 2 * j + g // 2)
                            w = slice(g * P, g * P + P)
                            for n in range(2):
                                cols = slice(n * KN, n * KN + KN)
                                o = k_ps[g % 2][:, n, 0:KN]
                                for c in range(DC):
                                    if g == 0 and n == 0:
                                        pe.wait_ge(ctx_lo[j], DC * i + c + 1)
                                    nc.tensor.matmul(o, w_hi[:, 0, c, w], c_hi[j][:, c, cols], start=(c == 0), stop=False)
                                    nc.tensor.matmul(o, w_hi[:, 0, c, w], c_lo[j][:, c, cols], start=False, stop=False)
                                    mm = nc.tensor.matmul(o, w_lo[:, 0, c, w], c_hi[j][:, c, cols], start=False, stop=(c == DC - 1))
                            mm.then_inc(k_made, 1)
                        for k in range(KC):
                            pe.wait_ge(vlo_done[(KC * j + k) % 4], 3 * i + (KC * j + k) // 4)
                            rows = slice(k * KP, k * KP + KP)
                            o = v_ps[(KC * j + k) % 4][0:KP, :]
                            for c in range(DC):
                                nc.tensor.matmul(o, c_hi[j][:, c, rows], w_hi[:, 1, c, :], start=(c == 0), stop=False)
                                nc.tensor.matmul(o, c_hi[j][:, c, rows], w_lo[:, 1, c, :], start=False, stop=False)
                                mm = nc.tensor.matmul(o, c_lo[j][:, c, rows], w_hi[:, 1, c, :], start=False, stop=(c == DC - 1))
                            mm.then_inc(v_made[j], 1)


M_XT, M_Q, M_MAX = 0, 1, 2
M_GROUP = HG * QC + 1
M_Y = M_MAX + NG * M_GROUP
M_XNT, M_LOGIT, M_AFF, M_USES = M_Y + 1, M_Y + 2, M_Y + 3, M_Y + 4
assert M_USES % 2 == 0
NST = H * KC // 2
DVE_STEPS = 27


def max_use(g, hh, qc):
    return M_MAX + g * M_GROUP + hh * QC + qc


def neg_use(g):
    return M_MAX + g * M_GROUP + HG * QC


def attend(nc, sem, sb, ps, x, maskq, maskt, wq, wo, gatew, kd, vd, xn_rows, out, cst, ident,
           cos, sin, gains, gate_all, row_all):
    with ExitStack() as st:
        wq_sb, wo_sb = sb(st, "wq_sb", [P, DC, D]), sb(st, "wo_sb", [P, DC, D])
        gw_sb = sb(st, "gw_sb", [P, DC, E])
        identb = sb(st, "identb", [P, P], BF16)
        ks = [sb(st, f"ks{j}", [P, HG, SK], F32R) for j in range(2)]
        qs = sb(st, "qs", [P, H, S], F32R)
        vs = [sb(st, f"vs{j}", [KP, KC, VH, VW], F32R) for j in range(2)]
        mq_raw, mt_raw = sb(st, "mq_raw", [QP, QC, S2], I32), sb(st, "mt_raw", [KP, KC, S], I32)
        mq = sb(st, "mq", [QP, QC, SK])
        mt = sb(st, "mt", [KP, KC, S], BF16)
        x_t, x_res = sb(st, "x_t", [QP, QC, D]), sb(st, "x_res", [QP, QC, D])
        stats, mv, rstd = sb(st, "stats", [QP, QC, 6]), sb(st, "mv", [QP, QC, 2]), sb(st, "rstd", [QP, QC])
        var, minus_half = sb(st, "var", [QP, QC]), sb(st, "minus_half", [QP, QC])
        xn = sb(st, "xn", [QP, QC, D])
        xT = sb(st, "xT", [P, 2, 2 * S])
        q_raw, q_rot = sb(st, "q_raw", [P, NG, S]), sb(st, "q_rot", [P, NG, S])
        q_cos = sb(st, "q_cos", [P, NG, S])
        q_hi, q_lo = sb(st, "q_hi", [P, NG, S], F32R), sb(st, "q_lo", [P, NG, S], F32R)
        junk = [sb(st, f"junk{j}", [QP, SK]) for j in range(2)]
        mx = sb(st, "mx", [QP, QC, P])
        e_t = [sb(st, f"e_t{j}", [KP, PAIR]) for j in range(3)]
        p_hi = [sb(st, f"p_hi{j}", [KP, KC // 2, PAIR], F32R) for j in range(2)]
        p_lo = [sb(st, f"p_lo{j}", [KP, KC // 2, PAIR], F32R) for j in range(2)]
        c_a, c_b, c_s = (sb(st, n, [P, 2, PAIR]) for n in ("c_a", "c_b", "c_s"))
        cx = sb(st, "cx", [P, 2, PAIR])
        x2 = x_res
        x2o, xn2 = sb(st, "x2o", [QP, QC, D]), sb(st, "xn2", [QP, QC, D])
        flag = sb(st, "flag", [QP, 4, QC])
        lg, ex = sb(st, "lg", [QP, QC, E]), sb(st, "ex", [QP, QC, E])
        aff = sb(st, "aff", [QP, QC, E])
        lmax, lsum = sb(st, "lmax", [QP, QC]), sb(st, "lsum", [QP, QC])
        aff8 = [sb(st, f"aff8_{j}", [E, S]) for j in range(2)]
        top_v, top_i = sb(st, "top_v", [E, TOPK]), sb(st, "top_i", [E, TOPK], U32)

        m_ps = [ps(st, f"m_ps{j}", [P, 2, 512]) for j in range(2)]
        s_ps = [ps(st, f"s_ps{j}", [P, 512]) for j in range(2)]
        o_ps = [ps(st, f"o_ps{j}", [P, 512]) for j in range(2)]

        att_in, sel_set = sem("att_in"), sem("sel_set")
        x_in, mq_in, mt_in, xres_in = sem("x_in"), sem("mq_in"), sem("mt_in"), sem("xres_in")
        mq_done, mt_done = sem("mq_done"), sem("mt_done")
        ks_in, vs_in = [sem(f"ks_in{j}") for j in range(2)], [sem(f"vs_in{j}") for j in range(2)]
        qs_in = sem("qs_in")
        dve_step = sem("dve_step")
        mv_done, var_done, rstd_done = sem("mv_done"), sem("var_done"), sem("rstd_done")
        xn_done, xn2_done = sem("xn_done"), sem("xn2_done")
        m_made, m_free = sem("m_made"), [sem(f"m_free{j}") for j in range(2)]
        qrot_done, qcos_done, qsin_done, qsum_done = sem("qrot_done"), sem("qcos_done"), sem("qsin_done"), sem("qsum_done")
        qhi_done, qlo_done = sem("qhi_done"), sem("qlo_done")
        s_made = sem("s_made")
        exp_done = [[sem(f"exp_done{g}{j}") for j in range(2)] for g in range(2)]
        phi_done = sem("phi_done")
        plo_done = [sem(f"plo_done{j}") for j in range(3)]
        pv_done = [[sem(f"pv_done{a}{j}") for j in range(2)] for a in range(2)]
        copied = [sem(f"copied{j}") for j in range(4)]
        sums_copied = [sem(f"sums_copied{j}") for j in range(2)]
        recip_done, ab_done, cx_done = sem("recip_done"), sem("ab_done"), [sem(f"cx_done{j}") for j in range(2)]
        lsub_done, lexp_done, aff_done = sem("lsub_done"), sem("lexp_done"), sem("aff_done")
        x2o_done, rows_stored, out_stored = sem("x2o_done"), sem("rows_stored"), sem("out_stored")

        def made(b, u):
            return M_USES * b + u + 1

        def freed(b, u):
            return M_USES // 2 * b + u // 2 + 1

        def take_slot(pe, b, u):
            pe.wait_ge(m_free[u % 2], M_USES // 2 * b + u // 2)

        def exp_at(b, n):
            if n < 0:
                return exp_done[1][n % 2], NST // 4 * b
            g, k = n // (NST // NG), n % (NST // NG)
            return exp_done[g % 2][n % 2], NST // 4 * b + (NST // NG // 2) * (g // 2) + k // 2 + 1

        def pv_at(b, h):
            if h < 0:
                return pv_done[1][h % 2], VH // 2 * b
            return pv_done[h // VH][h % 2], VH // 2 * b + h % VH // 2 + 1

        with nc.Block() as block:
            @block.sync
            def _(sp):
                def hold(s_, v_):
                    sp.wait_ge(s_, v_)
                    sp.nop(nofuse=True)

                sp.dma_start(wq_sb[:], wq).then_inc(att_in, 16)
                sp.dma_start(wo_sb[:], wo).then_inc(att_in, 16)
                sp.dma_start(gw_sb[:], gatew).then_inc(att_in, 16)

                def load_k(b, g):
                    s_, v_ = exp_at(b, (g - 1) * HG * KC // 2 - 1) if g >= 2 else (exp_done[g % 2][1], NST // 4 * b)
                    hold(s_, v_)
                    for r, part in ((0, 0), (1, 1), (2, 0)):
                        sp.dma_start(ks[g % 2][r * WAYS:r * WAYS + WAYS].bitcast(F32),
                                     kd[ds(b, 1), g, part].rearrange("o (h d) n -> d (o h) n", d=DK)).then_inc(ks_in[g % 2], 16)

                def load_v(b, a):
                    hold(pv_done[a][0], VH // 2 * b)
                    hold(pv_done[a][1], VH // 2 * b)
                    sp.dma_start(vs[a][:].bitcast(F32).rearrange("p c h w -> p (c h w)"),
                                 vd[ds(b, 1), a].rearrange("o p n -> p (o n)")).then_inc(vs_in[a], 16)

                with sp.Fori(0, B) as b:
                    hold(xn_done, QC * b)
                    sp.dma_start(x_t[:], x[ds(b, 1)].rearrange("o p c n -> p (o c) n")).then_inc(x_in, 16)
                    hold(mq_done, b)
                    sp.dma_start(mq_raw[:], maskq[ds(b, 1)].rearrange("o p c n -> p (o c) n")).then_inc(mq_in, 16)
                    hold(mt_done, b)
                    sp.dma_start(mt_raw[:], maskt[ds(b, 1)].rearrange("o p c n -> p (o c) n")).then_inc(mt_in, 16)
                    load_k(b, 0)
                    load_k(b, 1)
                    load_v(b, 0)
                    hold(exp_done[1][1], NST // 4 * b)
                    hold(qlo_done, b + 1)
                    for r, part in ((0, q_hi), (1, q_hi), (2, q_lo)):
                        for hh in range(HG):
                            sp.dma_start(qs[r * WAYS:r * WAYS + WAYS, hh:H:HG, :].bitcast(F32),
                                         part[hh * DK:hh * DK + DK].bitcast(F32)).then_inc(qs_in, 16)
                    load_v(b, 1)
                    hold(xn2_done, QC * b)
                    sp.dma_start(x_res[:], x[ds(b, 1)].rearrange("o p c n -> p (o c) n")).then_inc(xres_in, 16)
                    load_k(b, 2)
                    load_k(b, 3)

            @block.gpsimd
            def _(pool):
                def hold(s_, v_):
                    pool.wait_ge(s_, v_)
                    pool.nop(nofuse=True)

                nc.gpsimd.memset(mq[:, :, S2:SK], MASKED).then_inc(sel_set, 1)
                nc.gpsimd.memset(mx[:], 0.0).then_inc(sel_set, 1)
                nc.gpsimd.memset(minus_half[:], -0.5).then_inc(sel_set, 1)
                hold(sel_set, 8)
                def root(b, which):
                    hold(mv_done, 2 * b + which + 1)
                    nc.gpsimd.tensor_scalar(var[:], mv[:, :, 1], EPS, None, ALU.add).then_inc(var_done, 1)
                    hold(var_done, 2 * b + which + 1)
                    nc.gpsimd.tensor_tensor(rstd[:], var[:], minus_half[:], ALU.pow).then_inc(rstd_done, 1)

                with pool.Fori(0, B) as b:
                    root(b, 0)
                    hold(mq_in, 16 * b + 16)
                    hold(xn2_done, QC * b)
                    nc.gpsimd.tensor_scalar(mq[:, :, 0:S2], mq_raw[:], 0, MASKED, ALU.is_equal, ALU.mult).then_inc(mq_done, 1)
                    hold(mt_in, 16 * b + 16)
                    hold(exp_done[1][1], NST // 4 * b)
                    nc.gpsimd.tensor_scalar(mt[:], mt_raw[:], 0, MASKED, ALU.is_equal, ALU.mult).then_inc(mt_done, 1)
                    hold(qrot_done, b + 1)
                    nc.gpsimd.tensor_tensor(q_rot[:], q_rot[:], sin[:, None, 0:S].broadcast_to((P, NG, S)), ALU.mult).then_inc(qsin_done, 1)
                    for a in range(2):
                        for j in range(4):
                            hold(copied[j], 2 * b + a + 1)
                        nc.gpsimd.tensor_tensor(c_a[:, a], c_a[:, a], c_b[:, a], ALU.add).then_inc(ab_done, 1)
                    hold(x2o_done, QC * b + QC)
                    pool.dma_start(out[ds(b, 1)].rearrange("o (c p) n -> p (o c) n", c=QC), x2o[:]).then_inc(out_stored, 16)
                    root(b, 1)
                    hold(xn2_done, QC * b + QC)
                    pool.dma_start(xn_rows.rearrange("(b c p) n -> b p c n", b=B, c=QC)[ds(b, 1)].rearrange("o p c n -> p (o c) n"),
                                   xn2[:]).then_inc(rows_stored, 16)
                pool.wait_ge(out_stored, 16 * B)
                pool.wait_ge(rows_stored, 16 * B)

            @block.scalar
            def _(act):
                for j in range(2):
                    nc.scalar.activation(ks[j][3 * WAYS:P], cst[3 * WAYS:P, C_KSEL:C_KSEL + HG, None].broadcast_to((WAYS, HG, SK)),
                                         ACT.Copy).then_inc(sel_set, 1)
                nc.scalar.activation(identb[:], ident, ACT.Copy).then_inc(sel_set, 1)

                def neg_max(b, g):
                    u = neg_use(g)
                    act.wait_ge(m_made, made(b, u))
                    nc.scalar.activation(qs[3 * WAYS:P, g * HG:g * HG + HG, :],
                                         m_ps[u % 2][3 * WAYS:P, 0:1, 0:S].broadcast_to((WAYS, HG, S)),
                                         ACT.Copy, scale=-1.0).then_inc(m_free[u % 2], 1)

                def exps(b, h):
                    for pc in range(KC // 2):
                        n = h * (KC // 2) + pc
                        act.wait_ge(s_made, NST * b + n + 1)
                        act.wait_ge(plo_done[pc], H * b + h)
                        s_, v_ = exp_at(b, n)
                        nc.scalar.activation(e_t[pc][:], s_ps[n % 2][0:KP, 0:PAIR], ACT.Exp, scale=SCALE).then_inc(s_, 1)
                        act.wait_ge(s_, v_)
                        if pc == 0:
                            act.wait_ge(*pv_at(b, h - 2))
                        nc.scalar.activation(p_hi[h % 2][:, pc], e_t[pc][:], ACT.Copy).then_inc(phi_done, 1)

                def copy_ctx(b, q):
                    a, j = q // 4, q % 4
                    act.wait_ge(*pv_at(b, 2 * q + 1))
                    if j == 0:
                        act.wait_ge(cx_done[a], b)
                    rows = slice(j * WAYS, j * WAYS + WAYS)
                    nc.scalar.activation(c_a[rows, a], o_ps[q % 2][0:DK, 0:PAIR], ACT.Copy)
                    nc.scalar.activation(c_b[rows, a], o_ps[q % 2][DK:2 * DK, 0:PAIR], ACT.Copy).then_inc(copied[q % 4], 1)

                with act.Fori(0, B) as b:
                    act.wait_ge(m_made, made(b, M_XT))
                    nc.scalar.activation(xT[:], m_ps[M_XT % 2][:, :, 0:2 * S], ACT.Copy).then_inc(m_free[M_XT % 2], 1)
                    act.wait_ge(m_made, made(b, M_Q))
                    nc.scalar.activation(q_raw[:].rearrange("p (a c) s -> p a (c s)", a=2), m_ps[M_Q % 2][:, :, 0:2 * S], ACT.Copy).then_inc(m_free[M_Q % 2], 1)
                    act.wait_ge(qsum_done, b + 1)
                    act.wait_ge(qs_in, 16 * 12 * b)
                    nc.scalar.activation(q_hi[:], q_cos[:], ACT.Copy).then_inc(qhi_done, 1)
                    neg_max(b, 0)
                    for g in range(NG):
                        for hh in range(HG):
                            exps(b, g * HG + hh)
                            if hh == 2:
                                copy_ctx(b, 2 * g)
                        if g < NG - 1:
                            neg_max(b, g + 1)
                        copy_ctx(b, 2 * g + 1)
                    act.wait_ge(m_made, made(b, M_XNT))
                    nc.scalar.activation(xT[:], m_ps[M_XNT % 2][:, :, 0:2 * S], ACT.Copy).then_inc(m_free[M_XNT % 2], 1)
                    act.wait_ge(lsub_done, b + 1)
                    nc.scalar.activation(ex[:], lg[:], ACT.Exp).then_inc(lexp_done, 1)

            @block.vector
            def _(dve):
                nc.vector.memset(o_ps[0][:], 1.0).then_inc(sel_set, 1)
                nc.vector.memset(o_ps[1][:], 1.0).then_inc(sel_set, 1)
                dve.wait_ge(sel_set, 8)
                steps = [0]

                def hold(s_, v_):
                    dve.wait_ge(s_, v_)
                    dve.nop(nofuse=True)

                def step(b, ins, alone=False):
                    ins.then_inc(dve_step, 1)
                    steps[0] += 1
                    dve.wait_ge(dve_step, DVE_STEPS * b + steps[0])
                    if alone:
                        dve.nop(nofuse=True)

                def norm(b, which, src, dst, done):
                    for c in range(QC):
                        ins = nc.vector.bn_stats(stats[:, c], src[:, c])
                    step(b, ins, alone=True)
                    for c in range(QC):
                        ins = nc.vector.bn_aggr(mv[:, c], stats[:, c])
                    ins.then_inc(mv_done, 1)
                    dve.wait_ge(rstd_done, 2 * b + which + 1)
                    for c in range(QC):
                        nc.vector.tensor_scalar(dst[:, c], src[:, c], mv[:, c, 0:1], rstd[:, c:c + 1],
                                                ALU.subtract, ALU.mult).then_inc(done, 1)

                def maxima(b, g, hh):
                    for qc in range(QC):
                        u = max_use(g, hh, qc)
                        dve.wait_ge(m_made, made(b, u))
                        hold(m_free[u % 2], freed(b, u) - 1)
                        nc.vector.tensor_tensor_reduce(junk[u % 2][:].rearrange("p (a n) -> p a n", a=2), m_ps[u % 2][0:QP, :, 0:KN],
                                                       mq[:, qc].rearrange("p (a n) -> p a n", a=2), 1.0, -3e38, ALU.add, ALU.max,
                                                       mx[:, qc, 3 * WAYS + hh:3 * WAYS + hh + 1]).then_inc(m_free[u % 2], 1)

                def split_low(b, h):
                    for pc in range(KC // 2):
                        dve.wait_ge(phi_done, NST * b + h * (KC // 2) + pc + 1)
                        nc.vector.tensor_tensor(p_lo[h % 2][:, pc], e_t[pc][:], p_hi[h % 2][:, pc], ALU.subtract).then_inc(plo_done[pc], 1)

                def copy_sums(b, q):
                    a, j = q // 4, q % 4
                    hold(copied[q % 4], 2 * b + a + 1)
                    nc.vector.stream_shuffle(c_s[j * WAYS:j * WAYS + WAYS, a], o_ps[q % 2][2 * DK:3 * DK, 0:PAIR],
                                             [0] * WAYS).then_inc(sums_copied[q % 2], 1)

                def normalise(b, a):
                    for j in range(2):
                        dve.wait_ge(sums_copied[j], 4 * b + 2 * a + 2)
                    nc.vector.reciprocal(c_s[:, a], c_s[:, a]).then_inc(recip_done, 1)
                    dve.wait_ge(recip_done, 2 * b + a + 1)
                    dve.wait_ge(ab_done, 2 * b + a + 1)
                    nc.vector.tensor_tensor(cx[:, a], c_a[:, a], c_s[:, a], ALU.mult).then_inc(cx_done[a], 1)

                with dve.Fori(0, B) as b:
                    dve.wait_ge(x_in, 16 * b + 16)
                    norm(b, 0, x_t, xn, xn_done)
                    dve.wait_ge(m_free[M_Q % 2], freed(b, M_Q))
                    nc.vector.tensor_tensor(q_cos[:], q_raw[:], cos[:, None, 0:S].broadcast_to((P, NG, S)), ALU.mult).then_inc(qcos_done, 1)
                    nc.vector.stream_shuffle(q_rot[:], q_raw[:], ROTATE).then_inc(qrot_done, 1)
                    dve.wait_ge(qcos_done, b + 1)
                    dve.wait_ge(qsin_done, b + 1)
                    nc.vector.tensor_tensor(q_cos[:], q_cos[:], q_rot[:], ALU.add).then_inc(qsum_done, 1)
                    dve.wait_ge(qhi_done, b + 1)
                    nc.vector.tensor_tensor(q_lo[:], q_cos[:], q_hi[:], ALU.subtract).then_inc(qlo_done, 1)
                    dve.wait_ge(mq_done, b + 1)
                    for hh in range(HG):
                        maxima(b, 0, hh)
                    for g in range(NG):
                        for hh in range(HG):
                            if g < NG - 1:
                                if hh == 0:
                                    dve.wait_ge(m_made, made(b, neg_use(g)))
                                maxima(b, g + 1, hh)
                            split_low(b, g * HG + hh)
                            if hh == 2:
                                copy_sums(b, 2 * g)
                        copy_sums(b, 2 * g + 1)
                        if g % 2:
                            normalise(b, g // 2)
                    dve.wait_ge(xres_in, 16 * b + 16)
                    dve.wait_ge(m_made, made(b, M_Y))
                    nc.vector.scalar_tensor_tensor(out=x2[:], in0=m_ps[M_Y % 2][0:QP], scalar=gains[0:QP, 0:1], in1=x_res[:],
                                                   op0=ALU.mult, op1=ALU.add).then_inc(m_free[M_Y % 2], 1)
                    dve.wait_ge(m_free[max_use(NG - 1, 0, 1) % 2], freed(b, max_use(NG - 1, 0, 1)))
                    step(b, nc.vector.tensor_scalar(flag[:, 0], mx[:, :, 3 * WAYS], MASKED / 2, None, ALU.is_lt))
                    step(b, nc.vector.tensor_scalar(flag[:, 1], flag[:, 0], -1.0, 1.0, ALU.mult, ALU.add))
                    step(b, nc.vector.reciprocal(flag[:, 2], flag[:, 1]))
                    step(b, nc.vector.tensor_scalar(flag[:, 3], flag[:, 2], 0.0, None, ALU.mult))
                    dve.wait_ge(m_free[M_Y % 2], freed(b, M_Y))
                    dve.wait_ge(out_stored, 16 * b)
                    dve.wait_ge(rows_stored, 16 * b)
                    for c in range(QC):
                        nc.vector.tensor_scalar(x2o[:, c], x2[:, c], flag[:, 3, c:c + 1], None, ALU.add).then_inc(x2o_done, 1)
                    norm(b, 1, x2, xn2, xn2_done)
                    dve.wait_ge(m_made, made(b, M_LOGIT))
                    nc.vector.tensor_copy(lg[:], m_ps[M_LOGIT % 2][0:QP, 0, 0:QC * E].rearrange("p (c e) -> p c e", c=QC)).then_inc(m_free[M_LOGIT % 2], 1)
                    dve.wait_ge(m_free[M_LOGIT % 2], freed(b, M_LOGIT))
                    step(b, nc.vector.tensor_reduce(lmax[:], lg[:], AX_X, ALU.max))
                    nc.vector.tensor_tensor(lg[:], lg[:], lmax[:].rearrange("p (c o) -> p c o", o=1).broadcast_to((QP, QC, E)), ALU.subtract).then_inc(lsub_done, 1)
                    dve.wait_ge(lexp_done, b + 1)
                    step(b, nc.vector.tensor_reduce(lsum[:], ex[:], AX_X, ALU.add))
                    step(b, nc.vector.reciprocal(lsum[:], lsum[:]))
                    step(b, nc.vector.tensor_tensor(aff[:], ex[:], lsum[:].rearrange("p (c o) -> p c o", o=1).broadcast_to((QP, QC, E)), ALU.mult))
                    for c in range(QC):
                        step(b, nc.vector.tensor_scalar(flag[:, 1, c:c + 1], flag[:, 0, c:c + 1], 4.0, None, ALU.mult))
                        nc.vector.tensor_scalar(aff[:, c], aff[:, c], flag[:, 1, c:c + 1], None, ALU.add).then_inc(aff_done, 1)
                    dve.wait_ge(m_made, made(b, M_AFF))
                    nc.vector.tensor_copy(aff8[0][:], m_ps[M_AFF % 2][0:E, 0, 0:S]).then_inc(m_free[M_AFF % 2], 1)
                    hold(m_free[M_AFF % 2], freed(b, M_AFF))
                    for r in range(TOPK // 8):
                        v8, i8 = top_v[:, 8 * r:8 * r + 8], top_i[:, 8 * r:8 * r + 8]
                        step(b, nc.vector.max(v8, aff8[r % 2][:]), alone=True)
                        nc.vector.max_index(i8, v8, aff8[r % 2][:])
                        step(b, nc.vector.match_replace(aff8[(r + 1) % 2][:], v8, aff8[r % 2][:], -1.0), alone=True)
                    nc.vector.tensor_copy(gate_all[:, ds(b, 1), :].rearrange("e o k -> e (o k)"), top_v[:])
                    step(b, nc.vector.tensor_copy(row_all[:, ds(b, 1), :].rearrange("e o k -> e (o k)"), top_i[:]))
                    assert steps[0] == DVE_STEPS, steps[0]

            @block.tensor
            def _(pe):
                pe.wait_ge(att_in, 48)
                pe.wait_ge(sel_set, 8)

                def transposes(b, u, src, ready, n_ready):
                    take_slot(pe, b, u)
                    pe.wait_ge(ready, n_ready)
                    for c in range(DC):
                        for qc in range(QC):
                            a = c % 2 * S + qc * QP
                            mm = nc.tensor.transpose(m_ps[u % 2][:, c // 2, a:a + QP], src[:, qc, c * P:c * P + P], ident[0:QP, 0:QP])
                    mm.then_inc(m_made, 1)

                def scores(b, g, hh):
                    for qc in range(QC):
                        u = max_use(g, hh, qc)
                        take_slot(pe, b, u)
                        for n in range(2):
                            mm = nc.tensor.matmul(m_ps[u % 2][0:QP, n, 0:KN], qs[0:3 * WAYS, g * HG + hh, qc * QP:qc * QP + QP],
                                                  ks[g % 2][0:3 * WAYS, hh, n * KN:n * KN + KN], start=True, stop=True)
                        mm.then_inc(m_made, 1)

                def transpose_max(b, g):
                    u = neg_use(g)
                    take_slot(pe, b, u)
                    for j in range(2):
                        last = max_use(g, HG - 1, QC - 1 - j)
                        pe.wait_ge(m_free[last % 2], freed(b, last))
                    for qc in range(QC):
                        mm = nc.tensor.transpose(m_ps[u % 2][:, 0, qc * QP:qc * QP + QP], mx[:, qc, :], ident[0:QP, 0:QP])
                    mm.then_inc(m_made, 1)

                def scores_t(b, h):
                    g, hh = h // HG, h % HG
                    for pc in range(KC // 2):
                        n = h * (KC // 2) + pc
                        s_, v_ = exp_at(b, n - 2)
                        pe.wait_ge(s_, v_)
                        o = s_ps[n % 2][0:KP, 0:PAIR]
                        nc.tensor.matmul(o, identb[0:KP, 0:KP], mt[:, 2 * pc:2 * pc + 2, :].rearrange("p c s -> p (c s)"), start=True, stop=False)
                        for k in range(2):
                            c = 2 * pc + k
                            mm = nc.tensor.matmul(o[:, k * S:k * S + S], ks[g % 2][:, hh, c * KP:c * KP + KP], qs[:, h, :],
                                                  start=False, stop=(k == 1))
                        mm.then_inc(s_made, 1)

                def values(b, h):
                    if h % VH == 0:
                        pe.wait_ge(vs_in[h // VH], 16 * b + 16)
                    if h % 2 == 0:
                        pe.wait_ge(sums_copied[h // 2 % 2], 4 * b + h // 4)
                    o = o_ps[h // 2 % 2][0:VW, h % 2 * S:h % 2 * S + S]
                    for c in range(KC):
                        if c % 2 == 0:
                            pe.wait_ge(plo_done[c // 2], H * b + h + 1)
                        w = vs[h // VH][:, c, h % VH, :]
                        k = slice(c % 2 * S, c % 2 * S + S)
                        nc.tensor.matmul(o, w, p_hi[h % 2][:, c // 2, k], start=(c == 0), stop=False)
                        mm = nc.tensor.matmul(o, w, p_lo[h % 2][:, c // 2, k], start=False, stop=(c == KC - 1))
                    mm.then_inc(pv_done[h // VH][h % 2], 1)

                with pe.Fori(0, B) as b:
                    transposes(b, M_XT, xn, xn_done, QC * b + QC)
                    take_slot(pe, b, M_Q)
                    pe.wait_ge(m_free[M_XT % 2], freed(b, M_XT))
                    for g in range(NG):
                        for c in range(DC):
                            mm = nc.tensor.matmul(m_ps[M_Q % 2][:, g // 2, g % 2 * S:g % 2 * S + S], wq_sb[:, c, g * P:g * P + P],
                                                  xT[:, c // 2, c % 2 * S:c % 2 * S + S], start=(c == 0), stop=(c == DC - 1))
                    mm.then_inc(m_made, 1)
                    pe.wait_ge(qs_in, 16 * 12 * (b + 1))
                    pe.wait_ge(ks_in[0], 48 * (2 * b + 1))
                    for hh in range(HG):
                        scores(b, 0, hh)
                    transpose_max(b, 0)
                    pe.wait_ge(mt_done, b + 1)
                    pe.wait_ge(m_free[neg_use(0) % 2], freed(b, neg_use(0)))
                    for g in range(NG):
                        for hh in range(HG):
                            if g < NG - 1:
                                if hh == 0:
                                    pe.wait_ge(ks_in[(g + 1) % 2], 48 * (2 * b + (g + 1) // 2 + 1))
                                scores(b, g + 1, hh)
                            scores_t(b, g * HG + hh)
                            if hh:
                                values(b, g * HG + hh - 1)
                        if g < NG - 1:
                            transpose_max(b, g + 1)
                        values(b, g * HG + HG - 1)
                        if g < NG - 1:
                            u = neg_use(g + 1)
                            pe.wait_ge(m_free[u % 2], freed(b, u))
                    take_slot(pe, b, M_Y)
                    for a in range(2):
                        pe.wait_ge(cx_done[a], b + 1)
                    for qc in range(QC):
                        for t in range(2):
                            for a in range(2):
                                mm = nc.tensor.matmul(m_ps[M_Y % 2][0:QP, qc, :], cx[:, a, t * S + qc * QP:t * S + qc * QP + QP],
                                                      wo_sb[:, 2 * t + a, :], start=(t == 0 and a == 0), stop=(t == 1 and a == 1))
                    mm.then_inc(m_made, 1)
                    transposes(b, M_XNT, xn2, xn2_done, QC * b + QC)
                    take_slot(pe, b, M_LOGIT)
                    pe.wait_ge(m_free[M_XNT % 2], freed(b, M_XNT))
                    for qc in range(QC):
                        for c in range(DC):
                            mm = nc.tensor.matmul(m_ps[M_LOGIT % 2][0:QP, 0, qc * E:qc * E + E],
                                                  xT[:, c // 2, c % 2 * S + qc * QP:c % 2 * S + qc * QP + QP],
                                                  gw_sb[:, c, :], start=(c == 0), stop=(c == DC - 1))
                    mm.then_inc(m_made, 1)
                    take_slot(pe, b, M_AFF)
                    pe.wait_ge(aff_done, QC * b + QC)
                    for qc in range(QC):
                        mm = nc.tensor.transpose(m_ps[M_AFF % 2][0:E, 0, qc * QP:qc * QP + QP], aff[:, qc, :], ident[0:QP, 0:QP])
                    mm.then_inc(m_made, 1)


def experts(nc, sem, sb, ps, wstream, xn_rows, out_rows, cst, ident, gains, gate_all, row_all):
    with ExitStack() as st:
        w_raw = [sb(st, f"w_raw{j}", [P, UNIT]) for j in range(NRAW)]
        w_hi = [sb(st, f"ws_hi{j}", [P, UNIT], F32R) for j in range(NRAW)]
        w_lo = [sb(st, f"ws_lo{j}", [P, UNIT], F32R) for j in range(NRAW)]
        rows_f = sb(st, "rows_f", [E, SLOTS])
        gate_t = sb(st, "gate_t", [RP, E, RG])
        idx_t = sb(st, "idx_t", [RP, E, RG], U32)
        gather_i, scatter_i = sb(st, "gather_i", [RP, RG], U32), sb(st, "scatter_i", [RP, RG], U32)
        xg = sb(st, "xg", [RP, RG, D])
        xs_hi, xs_lo = sb(st, "xs_hi", [P, DC, SLOTS], F32R), sb(st, "xs_lo", [P, DC, SLOTS], F32R)
        silu = [sb(st, f"silu{j}", [P, SLOTS]) for j in range(2)]
        hid = [sb(st, f"hid{j}", [P, SLOTS]) for j in range(2)]
        h_hi, h_lo = sb(st, "h_hi", [P, IC, SLOTS], F32R), sb(st, "h_lo", [P, IC, SLOTS], F32R)
        y_sb = sb(st, "y_sb", [RP, RG, D])
        gu_ps = [ps(st, f"gu_ps{j}", [P, 512]) for j in range(4)]
        y_ps = [ps(st, f"y_ps{j}", [P, 512]) for j in range(RG)]

        w_in = [sem(f"w_in{j}") for j in range(NRAW)]
        whi_done, wlo_done = sem("whi_done"), [sem(f"wlo_done{j}") for j in range(NRAW)]
        w_used = sem("w_used")
        rows_ready, turned, gates_ready, idx_ready = sem("rows_ready"), sem("turned"), sem("gates_ready"), sem("idx_ready")
        gidx_done, sidx_done = sem("gidx_done"), sem("sidx_done")
        gathered, x_turned, xhi_done, xlo_done = sem("gathered"), sem("x_turned"), sem("xhi_done"), sem("xlo_done")
        silu_done, hid_done = sem("silu_done"), [sem(f"hid_done{j}") for j in range(2)]
        hhi_done, hlo_done = sem("hhi_done"), sem("hlo_done")
        y_act, y_dve, scattered = sem("y_act"), sem("y_dve"), sem("scattered")

        def ahead(e, u):
            return (e, u + LEAD) if u + LEAD < NU else (e + 1, u + LEAD - NU)

        def raw_uses(e, u):
            return NU // NRAW * e + u // NRAW

        with nc.Block() as block:
            @block.sync
            def _(sp):
                def hold(s_, v_):
                    sp.wait_ge(s_, v_)
                    sp.nop(nofuse=True)

                with sp.Fori(0, E) as e:
                    for u in range(NU):
                        s = u % NRAW
                        hold(wlo_done[s], raw_uses(e, u))
                        sp.dma_start(w_raw[s][:], wstream[ds(NU * e + u, 1)].rearrange("o p n -> p (o n)")).then_inc(w_in[s], 16)

            @block.gpsimd
            def _(pool):
                def hold(s_, v_):
                    pool.wait_ge(s_, v_)
                    pool.nop(nofuse=True)

                def gather(e):
                    hold(x_turned, e)
                    hold(gathered, 16 * RG * e)
                    nc.gpsimd.tensor_copy(gather_i[:], idx_t[:, ds(e, 1), :].rearrange("p o g -> p (o g)")).then_inc(gidx_done, 1)
                    hold(gidx_done, e + 1)
                    for g in range(RG):
                        pool.indirect_dma_start(xg[:, g, :], None, xn_rows, bass.IndirectOffsetOnAxis(gather_i[:, g:g + 1], 0)).then_inc(gathered, 16)

                def scatter(e):
                    hold(scattered, 16 * RG * e)
                    nc.gpsimd.tensor_copy(scatter_i[:], idx_t[:, ds(e, 1), :].rearrange("p o g -> p (o g)")).then_inc(sidx_done, 1)
                    hold(sidx_done, e + 1)
                    hold(y_act, RG // 2 * (e + 1))
                    hold(y_dve, RG // 2 * (e + 1))
                    for g in range(RG):
                        pool.indirect_dma_start(out_rows, bass.IndirectOffsetOnAxis(scatter_i[:, g:g + 1], 0), y_sb[:, g, :], None,
                                                compute_op=ALU.add).then_inc(scattered, 16)

                pool.wait_ge(idx_ready, 1)
                gather(0)
                with pool.Fori(0, E - 1) as e:
                    gather(e + 1)
                    scatter(e)
                scatter(E - 1)
                pool.wait_ge(scattered, 16 * RG * E)

            @block.scalar
            def _(act):
                def split_w(e, u):
                    s = u % NRAW
                    act.wait_ge(w_in[s], 16 * (raw_uses(e, u) + 1))
                    after(act, w_used, NU * e + u - NRAW + 1)
                    nc.scalar.activation(w_hi[s][:], w_raw[s][:], ACT.Copy).then_inc(whi_done, 1)

                def split_x(e):
                    act.wait_ge(x_turned, e + 1)
                    for c in range(DC):
                        nc.scalar.activation(xs_hi[:, c], gu_ps[c][:, 0:SLOTS], ACT.Copy).then_inc(xhi_done, 1)

                def expert(e, last):
                    for u in range(NU):
                        if not (last and u + LEAD >= NU):
                            split_w(*ahead(e, u))
                        if u < GU:
                            act.wait_ge(w_used, NU * e + u + 1)
                            nc.scalar.activation(silu[u % 2][:], gu_ps[u % 2 * 2][:, 0:SLOTS], ACT.Silu).then_inc(silu_done, 1)
                            act.wait_ge(hid_done[u % 2], GU // 2 * e + u // 2 + 1)
                            nc.scalar.activation(h_hi[:, u], hid[u % 2][:], ACT.Copy).then_inc(hhi_done, 1)
                        if u == GU + 1 and not last:
                            split_x(e + 1)
                    act.wait_ge(scattered, 16 * RG * e)
                    act.wait_ge(w_used, NU * (e + 1))
                    act.nop(nofuse=True)
                    for g in range(RG // 2):
                        nc.scalar.activation(y_sb[:, g], y_ps[g][0:RP, :], ACT.Copy,
                                             scale=gate_t[:, ds(e, 1), g:g + 1].rearrange("p o g -> p (o g)")).then_inc(y_act, 1)

                for u in range(LEAD):
                    split_w(0, u)
                split_x(0)
                act.wait_ge(gates_ready, 1)
                with act.Fori(0, E - 1) as e:
                    expert(e, False)
                expert(E - 1, True)

            @block.vector
            def _(dve):
                def split_w(e, u):
                    s = u % NRAW
                    dve.wait_ge(whi_done, NU * e + u + 1)
                    nc.vector.tensor_tensor(w_lo[s][:], w_raw[s][:], w_hi[s][:], ALU.subtract).then_inc(wlo_done[s], 1)

                def split_x(e):
                    for c in range(DC):
                        dve.wait_ge(xhi_done, DC * e + c + 1)
                        nc.vector.tensor_tensor(xs_lo[:, c], gu_ps[c][:, 0:SLOTS], xs_hi[:, c], ALU.subtract).then_inc(xlo_done, 1)

                def expert(e, last):
                    for u in range(NU):
                        if not (last and u + LEAD >= NU):
                            split_w(*ahead(e, u))
                        if u < GU:
                            dve.wait_ge(silu_done, GU * e + u + 1)
                            nc.vector.tensor_tensor(hid[u % 2][:], silu[u % 2][:], gu_ps[u % 2 * 2 + 1][:, 0:SLOTS],
                                                    ALU.mult).then_inc(hid_done[u % 2], 1)
                            dve.wait_ge(hhi_done, GU * e + u + 1)
                            nc.vector.tensor_tensor(h_lo[:, u], hid[u % 2][:], h_hi[:, u], ALU.subtract).then_inc(hlo_done, 1)
                        if u == GU + 1 and not last:
                            split_x(e + 1)
                    dve.wait_ge(scattered, 16 * RG * e)
                    dve.wait_ge(w_used, NU * (e + 1))
                    for g in range(RG // 2, RG):
                        nc.vector.tensor_scalar(y_sb[:, g], y_ps[g][0:RP, :], gate_t[:, ds(e, 1), g:g + 1].rearrange("p o g -> p (o g)"),
                                                None, ALU.mult).then_inc(y_dve, 1)

                nc.vector.tensor_tensor(rows_f[:], row_all[:].rearrange("e b k -> e (b k)"), cst[0:E, C_ROW:C_ROW + SLOTS],
                                        ALU.add).then_inc(rows_ready, 1)
                for u in range(LEAD):
                    split_w(0, u)
                dve.wait_ge(turned, 1)
                nc.vector.tensor_scalar(gate_t[:].rearrange("p e g -> p g e"), gu_ps[0][0:RP, 0:RG * E].rearrange("p (g e) -> p g e", g=RG),
                                        gains[0:RP, 1:2], None, ALU.mult).then_inc(gates_ready, 1)
                nc.vector.tensor_copy(idx_t[:].rearrange("p e g -> p g e"),
                                      gu_ps[0][0:RP, RG * E:2 * RG * E].rearrange("p (g e) -> p g e", g=RG)).then_inc(idx_ready, 1)
                split_x(0)
                dve.wait_ge(gates_ready, 1)
                with dve.Fori(0, E - 1) as e:
                    expert(e, False)
                expert(E - 1, True)

            @block.tensor
            def _(pe):
                def turn_rows(e):
                    pe.wait_ge(gathered, 16 * RG * (e + 1))
                    for c in range(DC):
                        for g in range(RG):
                            mm = nc.tensor.transpose(gu_ps[c][:, g * RP:g * RP + RP], xg[:, g, c * P:c * P + P], ident[0:RP, 0:RP])
                    mm.then_inc(x_turned, 1)

                def gate_up(e, u):
                    s = u % NRAW
                    pe.wait_ge(wlo_done[s], raw_uses(e, u) + 1)
                    pe.wait_ge(hid_done[u % 2], GU // 2 * e + u // 2)
                    if u == 0:
                        pe.wait_ge(xlo_done, DC * (e + 1))
                    for k in range(2):
                        o = gu_ps[u % 2 * 2 + k][:, 0:SLOTS]
                        for c in range(DC):
                            w = slice((k * DC + c) * P, (k * DC + c + 1) * P)
                            nc.tensor.matmul(o, w_hi[s][:, w], xs_hi[:, c], start=(c == 0), stop=False)
                            nc.tensor.matmul(o, w_hi[s][:, w], xs_lo[:, c], start=False, stop=False)
                            mm = nc.tensor.matmul(o, w_lo[s][:, w], xs_hi[:, c], start=False, stop=(c == DC - 1))
                    mm.then_inc(w_used, 1)

                def down(e, v):
                    s = (GU + v) % NRAW
                    pe.wait_ge(wlo_done[s], raw_uses(e, GU + v) + 1)
                    pe.wait_ge(hlo_done, GU * e + 2 * v + 2)
                    if v == 0:
                        pe.wait_ge(y_act, RG // 2 * e)
                        pe.wait_ge(y_dve, RG // 2 * e)
                    for k in range(2):
                        i, w = 2 * v + k, slice(k * D, k * D + D)
                        for g in range(RG):
                            o, r = y_ps[g][0:RP, :], slice(g * RP, g * RP + RP)
                            nc.tensor.matmul(o, h_hi[:, i, r], w_hi[s][:, w], start=(i == 0), stop=False)
                            nc.tensor.matmul(o, h_hi[:, i, r], w_lo[s][:, w], start=False, stop=False)
                            mm = nc.tensor.matmul(o, h_lo[:, i, r], w_hi[s][:, w], start=False, stop=(i == IC - 1))
                    mm.then_inc(w_used, 1)

                def expert(e, last):
                    for u in range(GU):
                        gate_up(e, u)
                    for v in range(DU):
                        down(e, v)
                        if v == 1 and not last:
                            for j in range(2):
                                pe.wait_ge(hid_done[j], GU // 2 * (e + 1))
                            turn_rows(e + 1)

                pe.wait_ge(rows_ready, 1)
                for g in range(RG):
                    nc.tensor.transpose(gu_ps[0][0:RP, g * E:g * E + E], gate_all[:].rearrange("e b k -> e (b k)")[:, g * RP:g * RP + RP],
                                        ident[0:E, 0:E])
                for g in range(RG):
                    mm = nc.tensor.transpose(gu_ps[0][0:RP, (RG + g) * E:(RG + g) * E + E], rows_f[:, g * RP:g * RP + RP], ident[0:E, 0:E])
                mm.then_inc(turned, 1)
                pe.wait_ge(idx_ready, 1)
                turn_rows(0)
                with pe.Fori(0, E - 1) as e:
                    expert(e, False)
                expert(E - 1, True)


def kernel(x, ctx_1024, mask_Bx1xSxS2_ik0, g_xattn, g_ffn, L0_xattn_W_q, L0_xattn_W_k, L0_xattn_W_v, L0_xattn_W_o,
           L0_ffn_gate_w, L0_ffn_w_gate, L0_ffn_w_up, L0_ffn_w_down):
    import numpy as np
    import concourse.bacc as bacc
    from concourse.bass_utils import run_bass_kernel_spmd

    f = np.float32
    arr = np.asarray

    consts = np.zeros((P, C_END), f)
    consts[:, C_ID:C_ID + P] = np.eye(P, dtype=f)
    inv_freq = (f(1.0) / f(10000.0) ** (np.arange(0, DK, 2, dtype=f) / f(DK))).astype(f)
    angles = np.outer(np.arange(S2, dtype=f), inv_freq).astype(f)
    angles = np.concatenate([angles, angles], axis=1).T
    sign = np.where(np.arange(DK) < DK // 2, f(-1), f(1))[:, None]
    consts[:, C_COS:C_COS + S2] = np.tile(np.cos(angles), (P // DK, 1))
    consts[:, C_SIN:C_SIN + S2] = np.tile(np.sin(angles) * sign, (P // DK, 1))
    consts[3 * WAYS:3 * WAYS + HG, C_KSEL:C_KSEL + HG] = np.eye(HG, dtype=f)
    consts[0:E, C_ROW:] = np.repeat(np.arange(B) * S, TOPK)[None]

    def columns(w):
        return arr(w).T.reshape(DC, P, -1).transpose(1, 0, 2)

    wo = arr(L0_xattn_W_o).T.reshape(2, 4, 2, DK, D).transpose(1, 3, 2, 0, 4).reshape(P, DC, D)
    ctxT = arr(ctx_1024).transpose(0, 2, 1).reshape(B, DC, P, S2).transpose(0, 2, 1, 3)
    mask = arr(mask_Bx1xSxS2_ik0).reshape(B, S, S2)
    maskq = mask.reshape(B, QC, QP, S2).transpose(0, 2, 1, 3)
    maskt = mask.transpose(0, 2, 1).reshape(B, KC, KP, S).transpose(0, 2, 1, 3)
    wg, wu, wd = arr(L0_ffn_w_gate), arr(L0_ffn_w_up), arr(L0_ffn_w_down)
    wstream = np.empty((E, NU, P, UNIT), f)
    for k, w in ((0, wg), (1, wu)):
        wstream[:, 0:GU].reshape(E, GU, P, 2, DC, P)[:, :, :, k] = w.reshape(E, IC, P, DC, P).transpose(0, 1, 4, 3, 2)
    wstream[:, GU:] = wd.transpose(0, 2, 1).reshape(E, DU, 2, P, D).transpose(0, 1, 3, 2, 4).reshape(E, DU, P, UNIT)

    arrays = {
        "ctxT": ctxT, "x_rows": arr(x).reshape(B, QC, QP, D).transpose(0, 2, 1, 3), "maskq": maskq, "maskt": maskt,
        "wk": columns(L0_xattn_W_k), "wv": columns(L0_xattn_W_v), "wq": columns(L0_xattn_W_q), "wo": wo,
        "gatew": columns(L0_ffn_gate_w), "gx": np.broadcast_to(arr(g_xattn), (P, 1)), "gf": np.broadcast_to(arr(g_ffn), (P, 1)),
        "wstream": wstream.reshape(E * NU, P, UNIT), "consts": consts,
    }
    arrays = {n: np.ascontiguousarray(a) for n, a in arrays.items()}
    nc = bacc.Bacc("TRN2", target_bir_lowering=False, num_devices=1)
    args = [nc.dram_tensor(n, a.shape, mybir.dt.from_np(a.dtype), kind="ExternalInput").ap() for n, a in arrays.items()]
    out = nc.dram_tensor("out", (B, S, D), F32, kind="ExternalOutput").ap()
    (ctxT_, x_, mq_, mt_, wk_, wv_, wq_, wo_, gw_, gx_, gf_, ws_, cs_) = args
    program(nc, ctxT_, x_, mq_, mt_, wk_, wv_, wq_, wo_, gw_, gx_, gf_, ws_, cs_, out)
    r = run_bass_kernel_spmd(nc, [arrays], core_ids=[0])
    return r.results[0]["out"]
```

```python
from contextlib import ExitStack

import concourse.bass as bass
from concourse import mybir

F32 = mybir.dt.float32
F32R = mybir.dt.float32r
BF16 = mybir.dt.bfloat16
I32 = mybir.dt.int32
U32 = mybir.dt.uint32
ALU = mybir.AluOpType
ACT = mybir.ActivationFunctionType
AX_X = mybir.AxisListType.X
ds = bass.ds

B, S, D = 8, 224, 512
S2 = 750
H, DK = 16, 32
E, I = 8, 2048
TOPK = S // E * 2
P = 128
DC = D // P
QP, QC = 112, S // 112
KP, KC = 125, S2 // 125
KN = 376
SK = 2 * KN
HG, NG = 4, H // 4
VH = 8
VW = 2 * DK + 1
PAIR = 2 * S
SCALE = float(DK) ** -0.5
EPS = 1e-5
MASKED = -(2.0 ** 100)
SLOTS = B * TOPK
RP, RG = 2 * TOPK, B // 2
IC = I // P
UNIT = 2 * DC * P
GU, DU = IC, IC // 2
NU = GU + DU
NRAW = 4
LEAD = 3
WAYS = 32

C_ID = 0
C_COS = C_ID + P
C_SIN = C_COS + SK
C_KSEL = C_SIN + SK
C_ROW = C_KSEL + HG
C_END = C_ROW + B * TOPK

ROTATE = [(d + DK // 2) % DK for d in range(DK)]


def after(eng, sem, value):
    if not (isinstance(value, int) and value <= 0):
        eng.wait_ge(sem, value)


def program(nc, ctxT, x, maskq, maskt, wk, wv, wq, wo, gatew, gx, gf, wstream, consts, out):
    kd = nc.dram_tensor("k_split", (B, NG, 2, P, SK), F32, kind="Internal").ap()
    vd = nc.dram_tensor("v_split", (B, 2, KP, KC * VH * VW), F32, kind="Internal").ap()
    xn_rows = nc.dram_tensor("xn_rows", (B * S, D), F32, kind="Internal").ap()
    out_rows = out.rearrange("b s d -> (b s) d")

    with ExitStack() as top:
        def sem(name):
            return top.enter_context(nc.semaphore(name))

        def sb(stack, name, shape, dt=F32):
            return stack.enter_context(nc.sbuf_tensor(name, shape, dt))

        def ps(stack, name, shape, dt=F32):
            return stack.enter_context(nc.psum_tensor(name, shape, dt))

        cst = sb(top, "cst", [P, C_END])
        ident = cst[:, C_ID:C_ID + P]
        cos, sin = cst[:, C_COS:C_COS + SK], cst[:, C_SIN:C_SIN + SK]
        gate_all = sb(top, "gate_all", [E, B, TOPK])
        row_all = sb(top, "row_all", [E, B, TOPK])
        gains = sb(top, "gains", [P, 2])

        project_context(nc, sem, sb, ps, ctxT, wk, wv, gx, gf, consts, kd, vd, cst, ident, cos, sin, gains)
        attend(nc, sem, sb, ps, x, maskq, maskt, wq, wo, gatew, kd, vd, xn_rows, out, cst, ident,
               cos, sin, gains, gate_all, row_all)
        experts(nc, sem, sb, ps, wstream, xn_rows, out_rows, cst, ident, gains, gate_all, row_all)


def project_context(nc, sem, sb, ps, ctxT, wk, wv, gx, gf, consts, kd, vd, cst, ident, cos, sin, gains):
    with ExitStack() as st:
        wraw = sb(st, "wraw", [P, 2, DC, D])
        w_hi = sb(st, "w_hi", [P, 2, DC, D], F32R)
        w_lo = sb(st, "w_lo", [P, 2, DC, D], F32R)
        graw = sb(st, "graw", [P, 2])
        c_raw = [sb(st, f"c_raw{j}", [P, DC, S2]) for j in range(2)]
        c_hi = [sb(st, f"c_hi{j}", [P, DC, SK], F32R) for j in range(2)]
        c_lo = [sb(st, f"c_lo{j}", [P, DC, SK], F32R) for j in range(2)]
        k_raw = [sb(st, f"k_raw{j}", [P, SK]) for j in range(2)]
        k_cos = [sb(st, f"k_cos{j}", [P, SK]) for j in range(2)]
        k_rot = [sb(st, f"k_rot{j}", [P, SK]) for j in range(2)]
        k_split = [sb(st, f"k_split{j}", [P, 2, SK], F32R) for j in range(2)]
        v_out = sb(st, "v_out", [KP, 2, KC, VH, VW], F32R)
        k_ps = [ps(st, f"k_ps{j}", [P, 2, 512]) for j in range(2)]
        v_ps = [ps(st, f"v_ps{j}", [P, 512]) for j in range(4)]

        weights_in, consts_in, gains_in = sem("weights_in"), sem("consts_in"), sem("gains_in")
        gains_done = sem("gains_done")
        wsplit_hi, wsplit_lo, pads_set = sem("wsplit_hi"), sem("wsplit_lo"), sem("pads_set")
        ctx_in = [sem(f"ctx_in{j}") for j in range(2)]
        ctx_hi, ctx_lo = sem("ctx_hi"), [sem(f"ctx_lo{j}") for j in range(2)]
        k_made, v_made = sem("k_made"), [sem(f"v_made{j}") for j in range(2)]
        kraw_done = [sem(f"kraw_done{j}") for j in range(2)]
        kcos_done, krot_done, ksin_done, ksum_done = sem("kcos_done"), sem("krot_done"), sem("ksin_done"), sem("ksum_done")
        khi_done, klo_done = sem("khi_done"), [sem(f"klo_done{j}") for j in range(2)]
        vhi_done, vlo_done = sem("vhi_done"), [sem(f"vlo_done{j}") for j in range(4)]
        k_stored = [sem(f"k_stored{j}") for j in range(2)]
        v_stored = sem("v_stored")

        with nc.Block() as block:
            @block.sync
            def _(sp):
                def hold(s_, v_):
                    sp.wait_ge(s_, v_)
                    sp.nop(nofuse=True)

                sp.dma_start(wraw[:, 0], wk).then_inc(weights_in, 16)
                sp.dma_start(wraw[:, 1], wv).then_inc(weights_in, 16)
                sp.dma_start(graw[:, 0:1], gx).then_inc(gains_in, 16)
                sp.dma_start(graw[:, 1:2], gf).then_inc(gains_in, 16)

                def load_ctx(i, j):
                    if not isinstance(i, int):
                        hold(ctx_lo[j], DC * i)
                    sp.dma_start(c_raw[j][:], ctxT[ds(2 * i + j, 1)].rearrange("o p c n -> p (o c) n")).then_inc(ctx_in[j], 16)

                for j in range(2):
                    load_ctx(0, j)
                with sp.Fori(1, B // 2) as i:
                    for j in range(2):
                        load_ctx(i, j)

            @block.gpsimd
            def _(pool):
                pool.dma_start(cst[:], consts).then_inc(consts_in, 16)
                for j in range(2):
                    nc.gpsimd.memset(c_hi[j][:, :, S2:SK].bitcast(F32), 0.0)
                    nc.gpsimd.memset(c_lo[j][:, :, S2:SK].bitcast(F32), 0.0)
                nc.gpsimd.memset(v_out[:, :, :, :, 2 * DK:VW].bitcast(F32), 1.0).then_inc(pads_set, 1)
                pool.wait_ge(consts_in, 16)
                with pool.Fori(0, B // 2) as i:
                    for g in range(2 * NG):
                        pool.wait_ge(krot_done, 2 * NG * i + g + 1)
                        nc.gpsimd.tensor_tensor(k_rot[g % 2][:], k_rot[g % 2][:], sin, ALU.mult).then_inc(ksin_done, 1)

            @block.scalar
            def _(act):
                act.wait_ge(gains_in, 32)
                nc.scalar.activation(gains[:], graw[:], ACT.Tanh).then_inc(gains_done, 1)
                act.wait_ge(weights_in, 32)
                nc.scalar.activation(w_hi[:], wraw[:], ACT.Copy).then_inc(wsplit_hi, 1)

                def split_ctx(i, j):
                    act.wait_ge(ctx_in[j], 16 * i + 16)
                    after(act, v_made[j], KC * i)
                    for c in range(DC):
                        nc.scalar.activation(c_hi[j][:, c, 0:S2], c_raw[j][:, c, :], ACT.Copy).then_inc(ctx_hi, 1)

                def copy_k(i, j, g):
                    act.wait_ge(k_made, 2 * NG * i + NG * j + g + 1)
                    after(act, klo_done[g % 2], NG * i + 2 * j + g // 2)
                    nc.scalar.activation(k_raw[g % 2][:].rearrange("p (a n) -> p a n", a=2),
                                         k_ps[g % 2][:, :, 0:KN], ACT.Copy).then_inc(kraw_done[g % 2], 1)

                def high_k(i, j, g):
                    act.wait_ge(ksum_done, 2 * NG * i + NG * j + g + 1)
                    after(act, k_stored[g % 2], 16 * (NG * i + 2 * j + g // 2))
                    nc.scalar.activation(k_split[g % 2][:, 0], k_cos[g % 2][:], ACT.Copy).then_inc(khi_done, 1)

                def store_k(i, j, g):
                    act.wait_ge(klo_done[g % 2], NG * i + 2 * j + g // 2 + 1)
                    act.dma_start(kd[ds(2 * i + j, 1), g].rearrange("o h p n -> p (o h) n"), k_split[g % 2][:].bitcast(F32)).then_inc(k_stored[g % 2], 16)

                def high_v(i, j, c):
                    act.wait_ge(v_made[j], KC * i + c + 1)
                    if c == 0:
                        after(act, v_stored, 32 * (2 * i + j))
                    nc.scalar.activation(v_out[:, :, c, :, 0:DK],
                                         v_ps[(KC * j + c) % 4][0:KP, :].rearrange("p (a h d) -> p a h d", a=2, h=VH),
                                         ACT.Copy).then_inc(vhi_done, 1)

                def store_v(i, j):
                    for c in range(KC - 4, KC):
                        act.wait_ge(vlo_done[(KC * j + c) % 4], 3 * i + (KC * j + c) // 4 + 1)
                    for a in range(2):
                        act.dma_start(vd[ds(2 * i + j, 1), a].rearrange("o p n -> p (o n)"),
                                      v_out[:, a].bitcast(F32).rearrange("p c h w -> p (c h w)")).then_inc(v_stored, 16)

                def pair(i, last):
                    for j in range(2):
                        copy_k(i, j, 0)
                        for g in range(1, NG):
                            copy_k(i, j, g)
                            high_k(i, j, g - 1)
                            if g > 1:
                                store_k(i, j, g - 2)
                        high_v(i, j, 0)
                        high_k(i, j, NG - 1)
                        store_k(i, j, NG - 2)
                        high_v(i, j, 1)
                        store_k(i, j, NG - 1)
                        if not (last and j):
                            split_ctx(*((i, 1) if j == 0 else (i + 1, 0)))
                        for c in range(2, KC):
                            high_v(i, j, c)
                        store_v(i, j)

                split_ctx(0, 0)
                pair(0, False)
                with act.Fori(1, B // 2 - 1) as i:
                    pair(i, False)
                pair(B // 2 - 1, True)
                for s in range(2):
                    act.wait_ge(k_stored[s], 16 * B * NG // 2)
                act.wait_ge(v_stored, 32 * B)

            @block.vector
            def _(dve):
                dve.wait_ge(wsplit_hi, 1)
                nc.vector.tensor_tensor(w_lo[:], wraw[:], w_hi[:], ALU.subtract).then_inc(wsplit_lo, 1)
                dve.wait_ge(pads_set, 1)
                dve.wait_ge(consts_in, 16)

                def low_ctx(i, j):
                    for c in range(DC):
                        dve.wait_ge(ctx_hi, 2 * DC * i + DC * j + c + 1)
                        nc.vector.tensor_tensor(c_lo[j][:, c, 0:S2], c_raw[j][:, c, :], c_hi[j][:, c, 0:S2],
                                                ALU.subtract).then_inc(ctx_lo[j], 1)

                def rotate(i, j, g):
                    s = g % 2
                    dve.wait_ge(kraw_done[s], NG * i + 2 * j + g // 2 + 1)
                    dve.nop(nofuse=True)
                    nc.vector.stream_shuffle(k_rot[s][:], k_raw[s][:], ROTATE).then_inc(krot_done, 1)
                    nc.vector.tensor_tensor(k_cos[s][:], k_raw[s][:], cos, ALU.mult).then_inc(kcos_done, 1)

                def sum_k(i, j, g):
                    n, s = 2 * NG * i + NG * j + g, g % 2
                    dve.wait_ge(kcos_done, n + 1)
                    dve.wait_ge(ksin_done, n + 1)
                    nc.vector.tensor_tensor(k_cos[s][:], k_cos[s][:], k_rot[s][:], ALU.add).then_inc(ksum_done, 1)

                def low_k(i, j, g):
                    s = g % 2
                    dve.wait_ge(khi_done, 2 * NG * i + NG * j + g + 1)
                    nc.vector.tensor_tensor(k_split[s][:, 1], k_cos[s][:], k_split[s][:, 0], ALU.subtract).then_inc(klo_done[s], 1)

                def low_v(i, j, c):
                    q = (KC * j + c) % 4
                    dve.wait_ge(vhi_done, 2 * KC * i + KC * j + c + 1)
                    nc.vector.tensor_tensor(v_out[:, :, c, :, DK:2 * DK],
                                            v_ps[q][0:KP, :].rearrange("p (a h d) -> p a h d", a=2, h=VH),
                                            v_out[:, :, c, :, 0:DK], ALU.subtract).then_inc(vlo_done[q], 1)

                def pair(i, last):
                    for j in range(2):
                        rotate(i, j, 0)
                        for g in range(1, NG):
                            sum_k(i, j, g - 1)
                            rotate(i, j, g)
                            low_k(i, j, g - 1)
                        sum_k(i, j, NG - 1)
                        low_v(i, j, 0)
                        low_k(i, j, NG - 1)
                        low_v(i, j, 1)
                        if not (last and j):
                            low_ctx(*((i, 1) if j == 0 else (i + 1, 0)))
                        for c in range(2, KC):
                            low_v(i, j, c)

                low_ctx(0, 0)
                pair(0, False)
                with dve.Fori(1, B // 2 - 1) as i:
                    pair(i, False)
                pair(B // 2 - 1, True)

            @block.tensor
            def _(pe):
                pe.wait_ge(wsplit_lo, 1)
                pe.wait_ge(pads_set, 1)

                def pair(i):
                    for j in range(2):
                        for g in range(NG):
                            after(pe, kraw_done[g % 2], NG * i + 2 * j + g // 2)
                            w = slice(g * P, g * P + P)
                            for n in range(2):
                                cols = slice(n * KN, n * KN + KN)
                                o = k_ps[g % 2][:, n, 0:KN]
                                for c in range(DC):
                                    if g == 0 and n == 0:
                                        pe.wait_ge(ctx_lo[j], DC * i + c + 1)
                                    nc.tensor.matmul(o, w_hi[:, 0, c, w], c_hi[j][:, c, cols], start=(c == 0), stop=False)
                                    nc.tensor.matmul(o, w_hi[:, 0, c, w], c_lo[j][:, c, cols], start=False, stop=False)
                                    mm = nc.tensor.matmul(o, w_lo[:, 0, c, w], c_hi[j][:, c, cols], start=False, stop=(c == DC - 1))
                            mm.then_inc(k_made, 1)
                        for k in range(KC):
                            after(pe, vlo_done[(KC * j + k) % 4], 3 * i + (KC * j + k) // 4)
                            rows = slice(k * KP, k * KP + KP)
                            o = v_ps[(KC * j + k) % 4][0:KP, :]
                            for c in range(DC):
                                nc.tensor.matmul(o, c_hi[j][:, c, rows], w_hi[:, 1, c, :], start=(c == 0), stop=False)
                                nc.tensor.matmul(o, c_hi[j][:, c, rows], w_lo[:, 1, c, :], start=False, stop=False)
                                mm = nc.tensor.matmul(o, c_lo[j][:, c, rows], w_hi[:, 1, c, :], start=False, stop=(c == DC - 1))
                            mm.then_inc(v_made[j], 1)

                pair(0)
                with pe.Fori(1, B // 2) as i:
                    pair(i)



M_GROUP = HG * QC + 1
M_USES = NG * M_GROUP
assert M_USES % 2 == 0
NST = H * KC // 2
KSLOTS = 2 * HG
F_XT, F_Q, F_USES = 0, 2, 4
R_Y, R_XNT, R_LOGIT, R_AFF, R_USES = 0, 2, 4, 5, 6
ROUNDS = TOPK // 8


def head_of(turn):
    return HG * (turn % HG) + turn // HG


def max_use(h, qc):
    return h // HG * M_GROUP + h % HG * QC + qc


def neg_use(g):
    return g * M_GROUP + HG * QC


def attend(nc, sem, sb, ps, x, maskq, maskt, wq, wo, gatew, kd, vd, xn_rows, out, cst, ident,
           cos, sin, gains, gate_all, row_all):
    with ExitStack() as st:
        wq_sb, wo_sb = sb(st, "wq_sb", [P, DC, D]), sb(st, "wo_sb", [P, DC, D])
        gw_sb = sb(st, "gw_sb", [P, DC, E])
        identb = sb(st, "identb", [P, P], BF16)
        ks = sb(st, "ks", [P, KSLOTS, SK], F32R)
        qs = sb(st, "qs", [P, H, S], F32R)
        vs = [sb(st, f"vs{j}", [KP, KC, VH, VW], F32R) for j in range(2)]
        mq_raw, mt_raw = sb(st, "mq_raw", [QP, QC, S2], I32), sb(st, "mt_raw", [KP, KC, S], I32)
        mq = sb(st, "mq", [QP, QC, SK])
        mt = sb(st, "mt", [KP, KC, S], BF16)
        x_t, x_res = sb(st, "x_t", [QP, QC, D]), sb(st, "x_res", [QP, QC, D])
        stats, mv, rstd = sb(st, "stats", [QP, QC, 6]), sb(st, "mv", [QP, 2, QC, 2]), sb(st, "rstd", [QP, 2, QC])
        var, minus_half = sb(st, "var", [QP, QC]), sb(st, "minus_half", [QP, QC])
        xn = sb(st, "xn", [QP, QC, D])
        xT = sb(st, "xT", [P, 2, 2 * S])
        q_raw, q_rot = sb(st, "q_raw", [P, NG, S]), sb(st, "q_rot", [P, NG, S])
        q_cos = sb(st, "q_cos", [P, NG, S])
        q_hi, q_lo = sb(st, "q_hi", [P, NG, S], F32R), sb(st, "q_lo", [P, NG, S], F32R)
        junk = [sb(st, f"junk{j}", [QP, SK]) for j in range(2)]
        mx = sb(st, "mx", [QP, 2, QC, P])
        e_t = [sb(st, f"e_t{j}", [KP, PAIR]) for j in range(3)]
        p_hi = [sb(st, f"p_hi{j}", [KP, KC // 2, PAIR], F32R) for j in range(2)]
        p_lo = [sb(st, f"p_lo{j}", [KP, KC // 2, PAIR], F32R) for j in range(2)]
        c_a, c_b, c_s = (sb(st, n, [P, 2, PAIR]) for n in ("c_a", "c_b", "c_s"))
        cx = sb(st, "cx", [P, 2, PAIR])
        x2 = x_res
        x2o, xn2 = sb(st, "x2o", [QP, QC, D]), sb(st, "xn2", [QP, QC, D])
        flag = sb(st, "flag", [QP, 4, QC])
        lg, ex = sb(st, "lg", [QP, QC, E]), sb(st, "ex", [QP, QC, E])
        aff = sb(st, "aff", [QP, QC, E])
        lmax, lsum = sb(st, "lmax", [QP, QC]), sb(st, "lsum", [QP, QC])
        aff8 = [sb(st, f"aff8_{j}", [E, S]) for j in range(2)]
        top_v, top_i = sb(st, "top_v", [E, TOPK]), sb(st, "top_i", [E, TOPK], U32)

        m_ps = [ps(st, f"m_ps{j}", [P, 2, 512]) for j in range(2)]
        s_ps = [ps(st, f"s_ps{j}", [P, 512]) for j in range(2)]
        o_ps, w_ps = ps(st, "o_ps", [P, 512]), ps(st, "w_ps", [P, 512])

        att_in, sel_set = sem("att_in"), sem("sel_set")
        x_in, mq_in, mt_in, xres_in = sem("x_in"), sem("mq_in"), sem("mt_in"), sem("xres_in")
        mq_done, mt_done = sem("mq_done"), sem("mt_done")
        ks_in = [sem(f"ks_in{j}") for j in range(KSLOTS // 2)]
        vs_in = [sem(f"vs_in{j}") for j in range(2)]
        qs_in = [sem(f"qs_in{j}") for j in range(NG)]
        ahead_step, rest_step, flag_step, ctx_step = sem("ahead_step"), sem("rest_step"), sem("flag_step"), sem("ctx_step")
        soft_step = sem("soft_step")
        mv_done = [sem(f"mv_done{j}") for j in range(2)]
        var_done, rstd_done = sem("var_done"), [sem(f"rstd_done{j}") for j in range(2)]
        xn_done, xn2_done = sem("xn_done"), sem("xn2_done")
        m_made, m_free = sem("m_made"), [sem(f"m_free{j}") for j in range(2)]
        ahead_made, ahead_free = sem("ahead_made"), sem("ahead_free")
        rest_made, rest_free = sem("rest_made"), sem("rest_free")
        qrot_done, qcos_done, qsin_done, qsum_done = sem("qrot_done"), sem("qcos_done"), sem("qsin_done"), sem("qsum_done")
        qhi_done, qlo_done = sem("qhi_done"), sem("qlo_done")
        s_made = sem("s_made")
        exp_done = [[sem(f"exp_done{g}{j}") for j in range(2)] for g in range(2)]
        phi_done = sem("phi_done")
        plo_done = [sem(f"plo_done{j}") for j in range(3)]
        pv_done = [[sem(f"pv_done{a}{j}") for j in range(2)] for a in range(2)]
        copied = sem("copied")
        ab_done, cx_done = sem("ab_done"), [sem(f"cx_done{j}") for j in range(2)]
        x2_done = sem("x2_done")
        lsub_done, lexp_done, aff_done = sem("lsub_done"), sem("lexp_done"), sem("aff_done")
        x2o_done, rows_stored, out_stored = sem("x2o_done"), sem("rows_stored"), sem("out_stored")

        def made(b, u):
            return M_USES * b + u + 1

        def freed(b, u):
            return M_USES // 2 * b + u // 2 + 1

        def exp_at(b, h, pc):
            if pc < 0:
                h, pc = h - 1, pc + KC // 2
            if h < 0:
                b, h = b - 1, h + H
            g, k = h // HG, h % HG * (KC // 2) + pc
            return exp_done[g % 2][(h * (KC // 2) + pc) % 2], NST // 4 * b + (HG * KC // 4) * (g // 2) + k // 2 + 1

        def pv_at(b, h):
            if h < 0:
                b, h = b - 1, h + H
            return pv_done[h // VH][h % 2], VH // 2 * b + h % VH // 2 + 1

        def every_batch(engine, start, body, end):
            start()
            body(0, True, False)
            with engine.Fori(1, B - 1) as b:
                body(b, False, False)
            body(B - 1, False, True)
            end()

        with nc.Block() as block:
            @block.sync
            def _(sp):
                def hold(s_, v_):
                    if not (isinstance(v_, int) and v_ <= 0):
                        sp.wait_ge(s_, v_)
                        sp.nop(nofuse=True)

                def load_k(b, h):
                    hold(*exp_at(b, h + 1 - KSLOTS, KC // 2 - 1))
                    g, k, s = h // HG, h % HG, h % KSLOTS
                    for r, part in ((0, 0), (1, 1), (2, 0)):
                        sp.dma_start(ks[r * WAYS:r * WAYS + WAYS, s:s + 2].bitcast(F32),
                                     kd[ds(b, 1), k:k + 2, part, g * DK:g * DK + DK].rearrange("o g d n -> d (o g) n")).then_inc(ks_in[s // 2], 16)

                def load_v(b, a):
                    hold(pv_done[a][0], VH // 2 * b)
                    hold(pv_done[a][1], VH // 2 * b)
                    sp.dma_start(vs[a][:].bitcast(F32).rearrange("p c h w -> p (c h w)"),
                                 vd[ds(b, 1), a].rearrange("o p n -> p (o n)")).then_inc(vs_in[a], 16)

                def stack_q(b, g):
                    hold(qlo_done, b + 1)
                    hold(*exp_at(b - 1, g * HG + HG - 1, KC // 2 - 1))
                    for r, part in ((0, q_hi), (1, q_hi), (2, q_lo)):
                        sp.dma_start(qs[r * WAYS:r * WAYS + WAYS, g * HG:g * HG + HG, :].bitcast(F32),
                                     part[g * DK:g * DK + DK].bitcast(F32)).then_inc(qs_in[g], 16)

                def load_x(b):
                    hold(xn_done, QC * b)
                    sp.dma_start(x_t[:], x[ds(b, 1)].rearrange("o p c n -> p (o c) n")).then_inc(x_in, 16)

                def load_mq(b):
                    hold(mq_done, QC * b)
                    sp.dma_start(mq_raw[:], maskq[ds(b, 1)].rearrange("o p c n -> p (o c) n")).then_inc(mq_in, 16)

                def load_mt(b):
                    hold(mt_done, KC // 2 * b)
                    sp.dma_start(mt_raw[:], maskt[ds(b, 1)].rearrange("o p c n -> p (o c) n")).then_inc(mt_in, 16)

                def load_res(b):
                    hold(rest_free, R_USES * b + 1)
                    sp.dma_start(x_res[:], x[ds(b, 1)].rearrange("o p c n -> p (o c) n")).then_inc(xres_in, 16)

                def start():
                    load_x(0)
                    sp.dma_start(wq_sb[:], wq).then_inc(att_in, 16)
                    load_mq(0)
                    load_k(0, 0)
                    load_k(0, 2)
                    load_mt(0)
                    load_k(0, 4)
                    load_v(0, 0)
                    sp.dma_start(wo_sb[:], wo).then_inc(att_in, 16)
                    sp.dma_start(gw_sb[:], gatew).then_inc(att_in, 16)
                    for g in range(NG):
                        stack_q(0, g)

                def body(b, first, last):
                    if not last:
                        load_x(b + 1)
                    if not first:
                        load_res(b - 1)
                    if not last:
                        load_mq(b + 1)
                    for t in range(0, H, 2):
                        if t + 6 < H:
                            load_k(b, t + 6)
                        elif not last:
                            load_k(b + 1, t + 6 - H)
                        if t == 0 and not first:
                            stack_q(b, NG - 1)
                        if t == 2:
                            load_v(b, 1)
                            if not last:
                                load_mt(b + 1)
                        if t == 8 and not last:
                            stack_q(b + 1, 0)
                            stack_q(b + 1, 1)
                        if t == 10 and not last:
                            load_v(b + 1, 0)
                        if t == 12 and not last:
                            stack_q(b + 1, 2)

                every_batch(sp, start, body, lambda: load_res(B - 1))

            @block.gpsimd
            def _(pool):
                def hold(s_, v_):
                    if not (isinstance(v_, int) and v_ <= 0):
                        pool.wait_ge(s_, v_)
                        pool.nop(nofuse=True)

                def root(b, which, before):
                    hold(mv_done[which], b + 1)
                    nc.gpsimd.tensor_scalar(var[:], mv[:, which, :, 1], EPS, None, ALU.add).then_inc(var_done, 1)
                    hold(var_done, before + 1)
                    nc.gpsimd.tensor_tensor(rstd[:, which], var[:], minus_half[:], ALU.pow).then_inc(rstd_done[which], 1)

                def mask_queries(b):
                    hold(mq_in, 16 * b + 16)
                    for qc in range(QC):
                        u = max_use(H - 1, qc)
                        hold(m_free[u % 2], freed(b - 1, u))
                        nc.gpsimd.tensor_scalar(mq[:, qc, 0:S2], mq_raw[:, qc], 0, MASKED, ALU.is_equal, ALU.mult).then_inc(mq_done, 1)

                def mask_keys(b):
                    hold(mt_in, 16 * b + 16)
                    for pc in range(KC // 2):
                        hold(*exp_at(b - 1, H - 1, pc))
                        k = slice(2 * pc, 2 * pc + 2)
                        nc.gpsimd.tensor_scalar(mt[:, k], mt_raw[:, k], 0, MASKED, ALU.is_equal, ALU.mult).then_inc(mt_done, 1)

                def sines(b):
                    hold(qrot_done, b + 1)
                    nc.gpsimd.tensor_tensor(q_rot[:], q_rot[:], sin[:, None, 0:S].broadcast_to((P, NG, S)), ALU.mult).then_inc(qsin_done, 1)

                def add_parts(b, a):
                    hold(copied, H // 2 * b + 4 * a + 4)
                    nc.gpsimd.tensor_tensor(c_a[:, a], c_a[:, a], c_b[:, a], ALU.add).then_inc(ab_done, 1)

                def split_low(b, h):
                    hold(phi_done, NST * b + h * (KC // 2) + KC // 2)
                    nc.gpsimd.tensor_tensor(p_lo[h % 2][:, KC // 2 - 1], e_t[KC // 2 - 1][:], p_hi[h % 2][:, KC // 2 - 1],
                                            ALU.subtract).then_inc(plo_done[KC // 2 - 1], 1)

                def store_out(b):
                    hold(x2o_done, QC * b + QC)
                    pool.dma_start(out[ds(b, 1)].rearrange("o (c p) n -> p (o c) n", c=QC), x2o[:]).then_inc(out_stored, 16)

                def store_rows(b):
                    hold(xn2_done, QC * b + QC)
                    pool.dma_start(xn_rows.rearrange("(b c p) n -> b p c n", b=B, c=QC)[ds(b, 1)].rearrange("o p c n -> p (o c) n"),
                                   xn2[:]).then_inc(rows_stored, 16)

                def start():
                    nc.gpsimd.memset(mq[:, :, S2:SK], MASKED).then_inc(sel_set, 1)
                    nc.gpsimd.memset(mx[:], 0.0).then_inc(sel_set, 1)
                    nc.gpsimd.memset(minus_half[:], -0.5).then_inc(sel_set, 1)
                    hold(sel_set, 7)
                    root(0, 0, 0)
                    mask_queries(0)
                    sines(0)
                    mask_keys(0)

                def body(b, first, last):
                    for t in range(H):
                        split_low(b, t)
                        if not last:
                            if t == 0:
                                root(b + 1, 0, b + 1 if first else 2 * b)
                            if t == 5:
                                sines(b + 1)
                            if t == 11:
                                mask_queries(b + 1)
                            if t == 15:
                                mask_keys(b + 1)
                        if not first:
                            if t == 1:
                                add_parts(b - 1, 1)
                            if t == 6:
                                store_out(b - 1)
                                root(b - 1, 1, 2 * B - 2 if last else 2 * b + 1)
                            if t == 7:
                                store_rows(b - 1)
                        if t == 9:
                            add_parts(b, 0)

                def end():
                    add_parts(B - 1, 1)
                    store_out(B - 1)
                    root(B - 1, 1, 2 * B - 1)
                    store_rows(B - 1)
                    pool.wait_ge(out_stored, 16 * B)
                    pool.wait_ge(rows_stored, 16 * B)

                every_batch(pool, start, body, end)

            @block.scalar
            def _(act):
                def copy_rows(n, free, sems):
                    for s_, v_ in sems:
                        after(act, s_, v_)
                    nc.scalar.activation(xT[:, n], w_ps[:, 0:2 * S], ACT.Copy).then_inc(free, 1)

                def x_columns(b, n):
                    copy_rows(n, ahead_free, ((ahead_made, F_USES * b + F_XT + n + 1), (rest_free, R_USES * (b - 2) + 1)))

                def x2_columns(b, n):
                    copy_rows(n, rest_free, ((rest_made, R_USES * b + R_XNT + n + 1),))

                def queries(b, n):
                    act.wait_ge(ahead_made, F_USES * b + F_Q + n + 1)
                    nc.scalar.activation(q_raw[:, 2 * n:2 * n + 2].rearrange("p c s -> p (c s)"), w_ps[:, 0:2 * S], ACT.Copy).then_inc(ahead_free, 1)

                def high_q(b):
                    act.wait_ge(qsum_done, b + 1)
                    for g in range(NG):
                        after(act, qs_in[g], 48 * b)
                    nc.scalar.activation(q_hi[:], q_cos[:], ACT.Copy).then_inc(qhi_done, 1)

                def neg_max(b, g):
                    u = neg_use(g)
                    act.wait_ge(m_made, made(b, u))
                    nc.scalar.activation(qs[3 * WAYS:P, g * HG:g * HG + HG, :],
                                         m_ps[u % 2][3 * WAYS:P, 0:1, 0:S].broadcast_to((WAYS, HG, S)),
                                         ACT.Copy, scale=-1.0).then_inc(m_free[u % 2], 1)

                def exp(b, h, pc):
                    n = h * (KC // 2) + pc
                    act.wait_ge(s_made, NST * b + n + 1)
                    after(act, plo_done[pc], H * b + h)
                    nc.scalar.activation(e_t[pc][:], s_ps[n % 2][0:KP, 0:PAIR], ACT.Exp, scale=SCALE).then_inc(exp_at(b, h, pc)[0], 1)

                def high(b, h, pc):
                    act.wait_ge(*exp_at(b, h, pc))
                    if pc == 0:
                        after(act, *pv_at(b, h - 2))
                    nc.scalar.activation(p_hi[h % 2][:, pc], e_t[pc][:], ACT.Copy).then_inc(phi_done, 1)

                def copy_ctx(b, q):
                    a, j = q // 4, q % 4
                    act.wait_ge(*pv_at(b, 2 * q + 1))
                    if j == 0:
                        after(act, cx_done[a], b)
                    rows = slice(j * WAYS, j * WAYS + WAYS)
                    nc.scalar.activation(c_a[rows, a], o_ps[0:DK, 0:PAIR], ACT.Copy)
                    nc.scalar.activation(c_b[rows, a], o_ps[DK:2 * DK, 0:PAIR], ACT.Copy)
                    nc.scalar.activation(c_s[rows, a], o_ps[2 * DK:3 * DK, 0:PAIR], ACT.Copy).then_inc(copied, 1)

                def logit_exp(b):
                    act.wait_ge(lsub_done, b + 1)
                    nc.scalar.activation(ex[:], lg[:], ACT.Exp).then_inc(lexp_done, 1)

                def start():
                    for j in range(2):
                        nc.scalar.activation(ks[3 * WAYS:P, j * HG:j * HG + HG], cst[3 * WAYS:P, C_KSEL:C_KSEL + HG, None].broadcast_to((WAYS, HG, SK)),
                                             ACT.Copy).then_inc(sel_set, 1)
                    nc.scalar.activation(identb[:], ident, ACT.Copy).then_inc(sel_set, 1)
                    for n in range(2):
                        x_columns(0, n)
                    for n in range(2):
                        queries(0, n)
                    high_q(0)
                    neg_max(0, 0)

                def body(b, first, last):
                    for t in range(H):
                        if t == 11 and not first:
                            logit_exp(b - 1)
                        exp(b, t, 0)
                        exp(b, t, 1)
                        high(b, t, 0)
                        exp(b, t, 2)
                        high(b, t, 1)
                        high(b, t, 2)
                        if t == 0 and not first:
                            copy_ctx(b - 1, 7)
                        if t and t % 2 == 0:
                            copy_ctx(b, t // 2 - 1)
                        if not last:
                            if t in (1, 2):
                                x_columns(b + 1, t - 1)
                            if t in (3, 4):
                                queries(b + 1, t - 3)
                            if t == 7:
                                high_q(b + 1)
                        if not first and t in (8, 9):
                            x2_columns(b - 1, t - 8)
                        if t % HG == HG - 1 and t < H - 1:
                            neg_max(b, t // HG + 1)
                        if t == H - 1 and not last:
                            neg_max(b + 1, 0)

                def end():
                    copy_ctx(B - 1, 7)
                    for n in range(2):
                        x2_columns(B - 1, n)
                    logit_exp(B - 1)

                every_batch(act, start, body, end)

            @block.vector
            def _(dve):
                def hold(s_, v_):
                    if not (isinstance(v_, int) and v_ <= 0):
                        dve.wait_ge(s_, v_)
                        dve.nop(nofuse=True)

                def done(ins, s_, value, alone=False):
                    ins.then_inc(s_, 1)
                    dve.wait_ge(s_, value)
                    if alone:
                        dve.nop(nofuse=True)

                def moments(b, which, src):
                    for c in range(QC):
                        ins = nc.vector.bn_stats(stats[:, c], src[:, c])
                    done(ins, ahead_step if which == 0 else rest_step, b + 1, alone=True)
                    for c in range(QC):
                        ins = nc.vector.bn_aggr(mv[:, which, c], stats[:, c])
                    ins.then_inc(mv_done[which], 1)

                def norm(b, which, src, dst, s_):
                    dve.wait_ge(rstd_done[which], b + 1)
                    dve.wait_ge(mv_done[which], b + 1)
                    for c in range(QC):
                        nc.vector.tensor_scalar(dst[:, c], src[:, c], mv[:, which, c, 0:1], rstd[:, which, c:c + 1],
                                                ALU.subtract, ALU.mult).then_inc(s_, 1)

                def maxima(b, h):
                    if h == 0:
                        dve.wait_ge(mq_done, QC * (b + 1))
                    g, hh = h // HG, h % HG
                    if hh == 0:
                        g_, b_ = (g - 2, b) if g >= 2 else (g + 2, b - 1)
                        after(dve, m_made, made(b_, neg_use(g_)))
                    for qc in range(QC):
                        u = max_use(h, qc)
                        dve.wait_ge(m_made, made(b, u))
                        hold(m_free[u % 2], freed(b, u) - 1)
                        nc.vector.tensor_tensor_reduce(junk[u % 2][:].rearrange("p (a n) -> p a n", a=2), m_ps[u % 2][0:QP, :, 0:KN],
                                                       mq[:, qc].rearrange("p (a n) -> p a n", a=2), 1.0, -3e38, ALU.add, ALU.max,
                                                       mx[:, g % 2, qc, 3 * WAYS + hh:3 * WAYS + hh + 1]).then_inc(m_free[u % 2], 1)

                def split_low(b, h):
                    for pc in range(KC // 2 - 1):
                        dve.wait_ge(phi_done, NST * b + h * (KC // 2) + pc + 1)
                        nc.vector.tensor_tensor(p_lo[h % 2][:, pc], e_t[pc][:], p_hi[h % 2][:, pc], ALU.subtract).then_inc(plo_done[pc], 1)

                def normalise(b, a):
                    hold(copied, H // 2 * b + 4 * a + 4)
                    done(nc.vector.stream_shuffle(cx[:, a], c_s[:, a], [0] * WAYS), ctx_step, 4 * b + 2 * a + 1)
                    done(nc.vector.reciprocal(c_s[:, a], cx[:, a]), ctx_step, 4 * b + 2 * a + 2)
                    dve.wait_ge(ab_done, 2 * b + a + 1)
                    nc.vector.tensor_tensor(cx[:, a], c_a[:, a], c_s[:, a], ALU.mult).then_inc(cx_done[a], 1)

                def rotate(b):
                    dve.wait_ge(ahead_free, F_USES * (b + 1))
                    nc.vector.tensor_tensor(q_cos[:], q_raw[:], cos[:, None, 0:S].broadcast_to((P, NG, S)), ALU.mult).then_inc(qcos_done, 1)
                    nc.vector.stream_shuffle(q_rot[:], q_raw[:], ROTATE).then_inc(qrot_done, 1)

                def sum_q(b):
                    dve.wait_ge(qcos_done, b + 1)
                    dve.wait_ge(qsin_done, b + 1)
                    nc.vector.tensor_tensor(q_cos[:], q_cos[:], q_rot[:], ALU.add).then_inc(qsum_done, 1)

                def low_q(b):
                    dve.wait_ge(qhi_done, b + 1)
                    nc.vector.tensor_tensor(q_lo[:], q_cos[:], q_hi[:], ALU.subtract).then_inc(qlo_done, 1)

                def flags(b):
                    for qc in range(QC):
                        u = max_use(H - 1, qc)
                        dve.wait_ge(m_free[u % 2], freed(b, u))
                    done(nc.vector.tensor_scalar(flag[:, 0], mx[:, (NG - 1) % 2, :, 3 * WAYS], MASKED / 2, None, ALU.is_lt), flag_step, 5 * b + 1)
                    done(nc.vector.tensor_scalar(flag[:, 1], flag[:, 0], -1.0, 1.0, ALU.mult, ALU.add), flag_step, 5 * b + 2)
                    done(nc.vector.reciprocal(flag[:, 2], flag[:, 1]), flag_step, 5 * b + 3)
                    done(nc.vector.tensor_scalar(flag[:, 3], flag[:, 2], 0.0, None, ALU.mult), flag_step, 5 * b + 4)
                    done(nc.vector.tensor_scalar(flag[:, 1], flag[:, 0], -4.0, None, ALU.mult), flag_step, 5 * b + 5)

                def residual(b, c):
                    dve.wait_ge(xres_in, 16 * b + 16)
                    dve.wait_ge(rest_made, R_USES * b + R_Y + c + 1)
                    nc.vector.scalar_tensor_tensor(out=x2[:, c], in0=w_ps[0:QP, :], scalar=gains[0:QP, 0:1], in1=x_res[:, c],
                                                   op0=ALU.mult, op1=ALU.add).then_inc(rest_free, 1)

                def x2_out(b):
                    dve.wait_ge(rest_free, R_USES * b + R_Y + 3)
                    for c in range(QC):
                        nc.vector.tensor_scalar(x2o[:, c], x2[:, c], flag[:, 3, c:c + 1], None, ALU.add).then_inc(x2o_done, 1)
                    dve.nop(nofuse=True)
                    moments(b, 1, x2)

                def norm_2(b):
                    norm(b, 1, x2, xn2, xn2_done)

                def logits(b):
                    dve.wait_ge(rest_made, R_USES * b + R_LOGIT + 1)
                    nc.vector.tensor_copy(lg[:], w_ps[0:QP, 0:QC * E].rearrange("p (c e) -> p c e", c=QC)).then_inc(rest_free, 1)
                    dve.wait_ge(rest_free, R_USES * b + R_LOGIT + 2)
                    done(nc.vector.tensor_reduce(lmax[:], lg[:], AX_X, ALU.max), soft_step, SOFT * b + 1)
                    nc.vector.tensor_tensor(lg[:], lg[:], lmax[:].rearrange("p (c o) -> p c o", o=1).broadcast_to((QP, QC, E)), ALU.subtract).then_inc(lsub_done, 1)

                def affinity(b):
                    dve.wait_ge(lexp_done, b + 1)
                    done(nc.vector.tensor_reduce(lsum[:], ex[:], AX_X, ALU.add), soft_step, SOFT * b + 2)
                    done(nc.vector.reciprocal(lsum[:], lsum[:]), soft_step, SOFT * b + 3)
                    done(nc.vector.tensor_tensor(aff[:], ex[:], lsum[:].rearrange("p (c o) -> p c o", o=1).broadcast_to((QP, QC, E)), ALU.mult), soft_step, SOFT * b + 4)
                    for c in range(QC):
                        nc.vector.tensor_scalar(aff[:, c], aff[:, c], flag[:, 1, c:c + 1], None, ALU.add).then_inc(aff_done, 1)

                def rounds(b, which):
                    if 0 in which:
                        dve.wait_ge(rest_made, R_USES * b + R_AFF + 1)
                        nc.vector.tensor_copy(aff8[0][:], w_ps[0:E, 0:S]).then_inc(rest_free, 1)
                        hold(rest_free, R_USES * b + R_AFF + 2)
                    for r in which:
                        v8, i8 = top_v[:, 8 * r:8 * r + 8], top_i[:, 8 * r:8 * r + 8]
                        done(nc.vector.max(v8, aff8[r % 2][:]), soft_step, SOFT * b + 5 + 2 * r, alone=True)
                        nc.vector.max_index(i8, v8, aff8[r % 2][:])
                        done(nc.vector.match_replace(aff8[(r + 1) % 2][:], v8, aff8[r % 2][:], -8.0), soft_step, SOFT * b + 6 + 2 * r, alone=True)
                    if ROUNDS - 1 in which:
                        dve.wait_ge(out_stored, 16 * (b + 1))
                        dve.wait_ge(rows_stored, 16 * (b + 1))
                        nc.vector.tensor_copy(gate_all[:, ds(b, 1), :].rearrange("e o k -> e (o k)"), top_v[:])
                        done(nc.vector.tensor_copy(row_all[:, ds(b, 1), :].rearrange("e o k -> e (o k)"), top_i[:]), soft_step, SOFT * (b + 1))

                SOFT = 5 + 2 * ROUNDS

                def start():
                    nc.vector.memset(o_ps[:], 1.0).then_inc(sel_set, 1)
                    nc.vector.memset(flag[:], 0.0).then_inc(rest_free, 1)
                    dve.wait_ge(sel_set, 7)
                    dve.wait_ge(x_in, 16)
                    moments(0, 0, x_t)
                    norm(0, 0, x_t, xn, xn_done)
                    rotate(0)
                    sum_q(0)
                    low_q(0)
                    for h in range(HG):
                        maxima(0, h)

                def body(b, first, last):
                    for t in range(H):
                        if t + HG < H:
                            maxima(b, t + HG)
                        elif not last:
                            maxima(b + 1, t + HG - H)
                        split_low(b, t)
                        if not last:
                            if t == 0:
                                dve.wait_ge(x_in, 16 * (b + 2))
                                moments(b + 1, 0, x_t)
                                dve.wait_ge(ahead_made, F_USES * (b + 1))
                                norm(b + 1, 0, x_t, xn, xn_done)
                            if t == 5:
                                rotate(b + 1)
                            if t == 6:
                                sum_q(b + 1)
                            if t == 7:
                                low_q(b + 1)
                        if not first:
                            if t == 2:
                                normalise(b - 1, 1)
                            if t in (5, 6):
                                residual(b - 1, t - 5)
                            if t == 6:
                                x2_out(b - 1)
                            if t == 7:
                                norm_2(b - 1)
                            if t == 10:
                                logits(b - 1)
                            if t == 11:
                                affinity(b - 1)
                            if t == 13:
                                rounds(b - 1, (0, 1))
                            if t == 14:
                                rounds(b - 1, (2, 3))
                            if t == 15:
                                rounds(b - 1, (4, 5, 6))
                        if t == 10:
                            normalise(b, 0)
                        if t == 12:
                            flags(b)

                def end():
                    b = B - 1
                    normalise(b, 1)
                    residual(b, 0)
                    residual(b, 1)
                    x2_out(b)
                    norm_2(b)
                    logits(b)
                    affinity(b)
                    rounds(b, range(ROUNDS))

                every_batch(dve, start, body, end)

            @block.tensor
            def _(pe):
                def take_slot(b, u):
                    after(pe, m_free[u % 2], freed(b, u) - 1)

                def turn(src, n, s_):
                    for c in range(2 * n, 2 * n + 2):
                        for qc in range(QC):
                            a = c % 2 * S + qc * QP
                            mm = nc.tensor.transpose(w_ps[:, a:a + QP], src[:, qc, c * P:c * P + P], ident[0:QP, 0:QP])
                    mm.then_inc(s_, 1)

                def turn_x(b, n):
                    if n == 0:
                        pe.wait_ge(rest_free, 1 if isinstance(b, int) and b < 2 else R_USES * (b - 2) + 1)
                    else:
                        pe.wait_ge(ahead_free, F_USES * b + F_XT + n)
                    pe.wait_ge(xn_done, QC * (b + 1))
                    turn(xn, n, ahead_made)

                def project_q(b, n):
                    pe.wait_ge(ahead_free, F_USES * b + F_Q + n)
                    for g in range(2 * n, 2 * n + 2):
                        for c in range(DC):
                            mm = nc.tensor.matmul(w_ps[:, g % 2 * S:g % 2 * S + S], wq_sb[:, c, g * P:g * P + P],
                                                  xT[:, c // 2, c % 2 * S:c % 2 * S + S], start=(c == 0), stop=(c == DC - 1))
                    mm.then_inc(ahead_made, 1)

                def project_out(b, qc, last):
                    if qc == 0:
                        pe.wait_ge(ahead_free, F_USES * (B if last else b + 3))
                    pe.wait_ge(rest_free, R_USES * b + R_Y + qc + 1)
                    for a in range(2):
                        pe.wait_ge(cx_done[a], b + 1)
                    for t in range(2):
                        for a in range(2):
                            mm = nc.tensor.matmul(w_ps[0:QP, :], cx[:, a, t * S + qc * QP:t * S + qc * QP + QP],
                                                  wo_sb[:, 2 * t + a, :], start=(t == 0 and a == 0), stop=(t == 1 and a == 1))
                    mm.then_inc(rest_made, 1)

                def turn_x2(b, n):
                    pe.wait_ge(rest_free, R_USES * b + R_XNT + n + 1)
                    pe.wait_ge(xn2_done, QC * (b + 1))
                    turn(xn2, n, rest_made)

                def logits(b):
                    pe.wait_ge(rest_free, R_USES * b + R_LOGIT + 1)
                    for qc in range(QC):
                        for c in range(DC):
                            mm = nc.tensor.matmul(w_ps[0:QP, qc * E:qc * E + E],
                                                  xT[:, c // 2, c % 2 * S + qc * QP:c % 2 * S + qc * QP + QP],
                                                  gw_sb[:, c, :], start=(c == 0), stop=(c == DC - 1))
                    mm.then_inc(rest_made, 1)

                def turn_affinity(b):
                    pe.wait_ge(rest_free, R_USES * b + R_AFF + 1)
                    pe.wait_ge(aff_done, QC * (b + 1))
                    for qc in range(QC):
                        mm = nc.tensor.transpose(w_ps[0:E, qc * QP:qc * QP + QP], aff[:, qc, :], ident[0:QP, 0:QP])
                    mm.then_inc(rest_made, 1)

                def scores(b, h):
                    if h % HG == 0:
                        pe.wait_ge(qs_in[h // HG], 48 * (b + 1))
                    if h % 2 == 0:
                        pe.wait_ge(ks_in[h // 2 % HG], 48 * (2 * b + h // KSLOTS + 1))
                    for qc in range(QC):
                        u = max_use(h, qc)
                        take_slot(b, u)
                        for n in range(2):
                            mm = nc.tensor.matmul(m_ps[u % 2][0:QP, n, 0:KN], qs[0:3 * WAYS, h, qc * QP:qc * QP + QP],
                                                  ks[0:3 * WAYS, h % KSLOTS, n * KN:n * KN + KN], start=True, stop=True)
                        mm.then_inc(m_made, 1)

                def transpose_max(b, g):
                    u = neg_use(g)
                    take_slot(b, u)
                    for j in range(2):
                        last = max_use(g * HG + HG - 1, QC - 1 - j)
                        pe.wait_ge(m_free[last % 2], freed(b, last))
                    for qc in range(QC):
                        mm = nc.tensor.transpose(m_ps[u % 2][:, 0, qc * QP:qc * QP + QP], mx[:, g % 2, qc, :], ident[0:QP, 0:QP])
                    mm.then_inc(m_made, 1)

                def scores_t(b, h):
                    if h % HG == 0:
                        u = neg_use(h // HG)
                        pe.wait_ge(m_free[u % 2], freed(b, u))
                    for pc in range(KC // 2):
                        n = h * (KC // 2) + pc
                        after(pe, *exp_at(b, h, pc - 2))
                        if h == 0:
                            pe.wait_ge(mt_done, KC // 2 * b + pc + 1)
                        o = s_ps[n % 2][0:KP, 0:PAIR]
                        nc.tensor.matmul(o, identb[0:KP, 0:KP], mt[:, 2 * pc:2 * pc + 2, :].rearrange("p c s -> p (c s)"), start=True, stop=False)
                        for k in range(2):
                            c = 2 * pc + k
                            mm = nc.tensor.matmul(o[:, k * S:k * S + S], ks[:, h % KSLOTS, c * KP:c * KP + KP], qs[:, h, :],
                                                  start=False, stop=(k == 1))
                        mm.then_inc(s_made, 1)

                def values(b, h):
                    if h % VH == 0:
                        pe.wait_ge(vs_in[h // VH], 16 * b + 16)
                    if h % 2 == 0:
                        after(pe, copied, H // 2 * b + h // 2)
                    o = o_ps[0:VW, h % 2 * S:h % 2 * S + S]
                    for c in range(KC):
                        if c % 2 == 0:
                            pe.wait_ge(plo_done[c // 2], H * b + h + 1)
                        w = vs[h // VH][:, c, h % VH, :]
                        k = slice(c % 2 * S, c % 2 * S + S)
                        nc.tensor.matmul(o, w, p_hi[h % 2][:, c // 2, k], start=(c == 0), stop=False)
                        mm = nc.tensor.matmul(o, w, p_lo[h % 2][:, c // 2, k], start=False, stop=(c == KC - 1))
                    mm.then_inc(pv_done[h // VH][h % 2], 1)

                def start():
                    pe.wait_ge(sel_set, 7)
                    for n in range(2):
                        turn_x(0, n)
                    pe.wait_ge(att_in, 48)
                    for n in range(2):
                        project_q(0, n)
                    for h in range(HG):
                        scores(0, h)
                    transpose_max(0, 0)

                def body(b, first, last):
                    for t in range(H):
                        if t + HG < H:
                            scores(b, t + HG)
                        elif not last:
                            scores(b + 1, t + HG - H)
                        scores_t(b, t)
                        if t:
                            values(b, t - 1)
                        elif not first:
                            values(b - 1, H - 1)
                        if not last:
                            if t in (1, 2):
                                turn_x(b + 1, t - 1)
                            if t in (3, 4):
                                project_q(b + 1, t - 3)
                        if not first:
                            if t in (5, 6):
                                project_out(b - 1, t - 5, last)
                            if t in (8, 9):
                                turn_x2(b - 1, t - 8)
                            if t == 10:
                                logits(b - 1)
                            if t == 12:
                                turn_affinity(b - 1)
                        if t % HG == HG - 1 and t < H - 1:
                            transpose_max(b, t // HG + 1)
                        if t == H - 1 and not last:
                            transpose_max(b + 1, 0)

                def end():
                    b = B - 1
                    values(b, H - 1)
                    for qc in range(QC):
                        project_out(b, qc, True)
                    for n in range(2):
                        turn_x2(b, n)
                    logits(b)
                    turn_affinity(b)

                every_batch(pe, start, body, end)


def experts(nc, sem, sb, ps, wstream, xn_rows, out_rows, cst, ident, gains, gate_all, row_all):
    with ExitStack() as st:
        w_raw = [sb(st, f"w_raw{j}", [P, UNIT]) for j in range(NRAW)]
        w_hi = [sb(st, f"ws_hi{j}", [P, UNIT], F32R) for j in range(NRAW)]
        w_lo = [sb(st, f"ws_lo{j}", [P, UNIT], F32R) for j in range(NRAW)]
        rows_f = sb(st, "rows_f", [E, SLOTS])
        gate_t = sb(st, "gate_t", [RP, E, RG])
        idx_t = sb(st, "idx_t", [RP, E, RG], U32)
        gather_i, scatter_i = sb(st, "gather_i", [RP, RG], U32), sb(st, "scatter_i", [RP, RG], U32)
        xg = sb(st, "xg", [RP, RG, D])
        xs_hi, xs_lo = sb(st, "xs_hi", [P, DC, SLOTS], F32R), sb(st, "xs_lo", [P, DC, SLOTS], F32R)
        silu = [sb(st, f"silu{j}", [P, SLOTS]) for j in range(2)]
        hid = [sb(st, f"hid{j}", [P, SLOTS]) for j in range(2)]
        h_hi, h_lo = sb(st, "h_hi", [P, IC, SLOTS], F32R), sb(st, "h_lo", [P, IC, SLOTS], F32R)
        y_sb = sb(st, "y_sb", [RP, RG, D])
        gu_ps = [ps(st, f"gu_ps{j}", [P, 512]) for j in range(4)]
        y_ps = [ps(st, f"y_ps{j}", [P, 512]) for j in range(RG)]

        w_in = [sem(f"w_in{j}") for j in range(NRAW)]
        whi_done, wlo_done = sem("whi_done"), [sem(f"wlo_done{j}") for j in range(NRAW)]
        w_used = sem("w_used")
        rows_ready, turned, gates_ready, idx_ready = sem("rows_ready"), sem("turned"), sem("gates_ready"), sem("idx_ready")
        gidx_done, sidx_done = sem("gidx_done"), sem("sidx_done")
        gathered, x_turned, xhi_done, xlo_done = sem("gathered"), sem("x_turned"), sem("xhi_done"), sem("xlo_done")
        silu_done, hid_done = sem("silu_done"), [sem(f"hid_done{j}") for j in range(2)]
        hhi_done, hlo_done = sem("hhi_done"), sem("hlo_done")
        y_act, y_dve, scattered = sem("y_act"), sem("y_dve"), sem("scattered")

        def ahead(e, u):
            return (e, u + LEAD) if u + LEAD < NU else (e + 1, u + LEAD - NU)

        def raw_uses(e, u):
            return NU // NRAW * e + u // NRAW

        with nc.Block() as block:
            @block.sync
            def _(sp):
                def hold(s_, v_):
                    sp.wait_ge(s_, v_)
                    sp.nop(nofuse=True)

                def load(e, u):
                    s = u % NRAW
                    if not (isinstance(e, int) and u < NRAW):
                        hold(wlo_done[s], raw_uses(e, u))
                    sp.dma_start(w_raw[s][:], wstream[ds(NU * e + u, 1)].rearrange("o p n -> p (o n)")).then_inc(w_in[s], 16)

                for u in range(NU):
                    load(0, u)
                with sp.Fori(1, E) as e:
                    for u in range(NU):
                        load(e, u)

            @block.gpsimd
            def _(pool):
                def hold(s_, v_):
                    if not (isinstance(v_, int) and v_ <= 0):
                        pool.wait_ge(s_, v_)
                        pool.nop(nofuse=True)

                def gather(e):
                    hold(x_turned, e)
                    hold(gathered, 16 * RG * e)
                    nc.gpsimd.tensor_copy(gather_i[:], idx_t[:, ds(e, 1), :].rearrange("p o g -> p (o g)")).then_inc(gidx_done, 1)
                    hold(gidx_done, e + 1)
                    for g in range(RG):
                        pool.indirect_dma_start(xg[:, g, :], None, xn_rows, bass.IndirectOffsetOnAxis(gather_i[:, g:g + 1], 0)).then_inc(gathered, 16)

                def scatter(e):
                    hold(scattered, 16 * RG * e)
                    nc.gpsimd.tensor_copy(scatter_i[:], idx_t[:, ds(e, 1), :].rearrange("p o g -> p (o g)")).then_inc(sidx_done, 1)
                    hold(sidx_done, e + 1)
                    hold(y_act, RG // 2 * (e + 1))
                    hold(y_dve, RG // 2 * (e + 1))
                    for g in range(RG):
                        pool.indirect_dma_start(out_rows, bass.IndirectOffsetOnAxis(scatter_i[:, g:g + 1], 0), y_sb[:, g, :], None,
                                                compute_op=ALU.add).then_inc(scattered, 16)

                pool.wait_ge(idx_ready, 1)
                gather(0)
                gather(1)
                scatter(0)
                with pool.Fori(1, E - 1) as e:
                    gather(e + 1)
                    scatter(e)
                scatter(E - 1)
                pool.wait_ge(scattered, 16 * RG * E)

            @block.scalar
            def _(act):
                def split_w(e, u):
                    s = u % NRAW
                    act.wait_ge(w_in[s], 16 * (raw_uses(e, u) + 1))
                    after(act, w_used, NU * e + u - NRAW + 1)
                    nc.scalar.activation(w_hi[s][:], w_raw[s][:], ACT.Copy).then_inc(whi_done, 1)

                def split_x(e):
                    act.wait_ge(x_turned, e + 1)
                    for c in range(DC):
                        nc.scalar.activation(xs_hi[:, c], gu_ps[c][:, 0:SLOTS], ACT.Copy).then_inc(xhi_done, 1)

                def expert(e, last):
                    for u in range(NU):
                        if not (last and u + LEAD >= NU):
                            split_w(*ahead(e, u))
                        if u < GU:
                            act.wait_ge(w_used, NU * e + u + 1)
                            nc.scalar.activation(silu[u % 2][:], gu_ps[u % 2 * 2][:, 0:SLOTS], ACT.Silu).then_inc(silu_done, 1)
                            act.wait_ge(hid_done[u % 2], GU // 2 * e + u // 2 + 1)
                            nc.scalar.activation(h_hi[:, u], hid[u % 2][:], ACT.Copy).then_inc(hhi_done, 1)
                        if u == GU + 1 and not last:
                            split_x(e + 1)
                    after(act, scattered, 16 * RG * e)
                    act.wait_ge(w_used, NU * (e + 1))
                    act.nop(nofuse=True)
                    for g in range(RG // 2):
                        nc.scalar.activation(y_sb[:, g], y_ps[g][0:RP, :], ACT.Copy,
                                             scale=gate_t[:, ds(e, 1), g:g + 1].rearrange("p o g -> p (o g)")).then_inc(y_act, 1)

                for u in range(LEAD):
                    split_w(0, u)
                split_x(0)
                act.wait_ge(gates_ready, 1)
                expert(0, False)
                with act.Fori(1, E - 1) as e:
                    expert(e, False)
                expert(E - 1, True)

            @block.vector
            def _(dve):
                def split_w(e, u):
                    s = u % NRAW
                    dve.wait_ge(whi_done, NU * e + u + 1)
                    nc.vector.tensor_tensor(w_lo[s][:], w_raw[s][:], w_hi[s][:], ALU.subtract).then_inc(wlo_done[s], 1)

                def split_x(e):
                    for c in range(DC):
                        dve.wait_ge(xhi_done, DC * e + c + 1)
                        nc.vector.tensor_tensor(xs_lo[:, c], gu_ps[c][:, 0:SLOTS], xs_hi[:, c], ALU.subtract).then_inc(xlo_done, 1)

                def expert(e, last):
                    for u in range(NU):
                        if not (last and u + LEAD >= NU):
                            split_w(*ahead(e, u))
                        if u < GU:
                            dve.wait_ge(silu_done, GU * e + u + 1)
                            nc.vector.tensor_tensor(hid[u % 2][:], silu[u % 2][:], gu_ps[u % 2 * 2 + 1][:, 0:SLOTS],
                                                    ALU.mult).then_inc(hid_done[u % 2], 1)
                            dve.wait_ge(hhi_done, GU * e + u + 1)
                            nc.vector.tensor_tensor(h_lo[:, u], hid[u % 2][:], h_hi[:, u], ALU.subtract).then_inc(hlo_done, 1)
                        if u == GU + 1 and not last:
                            split_x(e + 1)
                    after(dve, scattered, 16 * RG * e)
                    dve.wait_ge(w_used, NU * (e + 1))
                    for g in range(RG // 2, RG):
                        nc.vector.tensor_scalar(y_sb[:, g], y_ps[g][0:RP, :], gate_t[:, ds(e, 1), g:g + 1].rearrange("p o g -> p (o g)"),
                                                None, ALU.mult).then_inc(y_dve, 1)

                nc.vector.tensor_tensor(rows_f[:], row_all[:].rearrange("e b k -> e (b k)"), cst[0:E, C_ROW:C_ROW + SLOTS],
                                        ALU.add).then_inc(rows_ready, 1)
                for u in range(LEAD):
                    split_w(0, u)
                dve.wait_ge(turned, 1)
                nc.vector.tensor_scalar(gate_t[:].rearrange("p e g -> p g e"), gu_ps[0][0:RP, 0:RG * E].rearrange("p (g e) -> p g e", g=RG),
                                        gains[0:RP, 1:2], None, ALU.mult).then_inc(gates_ready, 1)
                nc.vector.tensor_copy(idx_t[:].rearrange("p e g -> p g e"),
                                      gu_ps[0][0:RP, RG * E:2 * RG * E].rearrange("p (g e) -> p g e", g=RG)).then_inc(idx_ready, 1)
                split_x(0)
                dve.wait_ge(gates_ready, 1)
                expert(0, False)
                with dve.Fori(1, E - 1) as e:
                    expert(e, False)
                expert(E - 1, True)

            @block.tensor
            def _(pe):
                def turn_rows(e):
                    pe.wait_ge(gathered, 16 * RG * (e + 1))
                    for c in range(DC):
                        for g in range(RG):
                            mm = nc.tensor.transpose(gu_ps[c][:, g * RP:g * RP + RP], xg[:, g, c * P:c * P + P], ident[0:RP, 0:RP])
                    mm.then_inc(x_turned, 1)

                def gate_up(e, u):
                    s = u % NRAW
                    pe.wait_ge(wlo_done[s], raw_uses(e, u) + 1)
                    after(pe, hid_done[u % 2], GU // 2 * e + u // 2)
                    if u == 0:
                        pe.wait_ge(xlo_done, DC * (e + 1))
                    for k in range(2):
                        o = gu_ps[u % 2 * 2 + k][:, 0:SLOTS]
                        for c in range(DC):
                            w = slice((k * DC + c) * P, (k * DC + c + 1) * P)
                            nc.tensor.matmul(o, w_hi[s][:, w], xs_hi[:, c], start=(c == 0), stop=False)
                            nc.tensor.matmul(o, w_hi[s][:, w], xs_lo[:, c], start=False, stop=False)
                            mm = nc.tensor.matmul(o, w_lo[s][:, w], xs_hi[:, c], start=False, stop=(c == DC - 1))
                    mm.then_inc(w_used, 1)

                def down(e, v):
                    s = (GU + v) % NRAW
                    pe.wait_ge(wlo_done[s], raw_uses(e, GU + v) + 1)
                    pe.wait_ge(hlo_done, GU * e + 2 * v + 2)
                    if v == 0:
                        after(pe, y_act, RG // 2 * e)
                        after(pe, y_dve, RG // 2 * e)
                    for k in range(2):
                        i, w = 2 * v + k, slice(k * D, k * D + D)
                        for g in range(RG):
                            o, r = y_ps[g][0:RP, :], slice(g * RP, g * RP + RP)
                            nc.tensor.matmul(o, h_hi[:, i, r], w_hi[s][:, w], start=(i == 0), stop=False)
                            nc.tensor.matmul(o, h_hi[:, i, r], w_lo[s][:, w], start=False, stop=False)
                            mm = nc.tensor.matmul(o, h_lo[:, i, r], w_hi[s][:, w], start=False, stop=(i == IC - 1))
                    mm.then_inc(w_used, 1)

                def expert(e, last):
                    for u in range(GU):
                        gate_up(e, u)
                    for v in range(DU):
                        down(e, v)
                        if v == 1 and not last:
                            for j in range(2):
                                pe.wait_ge(hid_done[j], GU // 2 * (e + 1))
                            turn_rows(e + 1)

                pe.wait_ge(rows_ready, 1)
                for g in range(RG):
                    nc.tensor.transpose(gu_ps[0][0:RP, g * E:g * E + E], gate_all[:].rearrange("e b k -> e (b k)")[:, g * RP:g * RP + RP],
                                        ident[0:E, 0:E])
                for g in range(RG):
                    mm = nc.tensor.transpose(gu_ps[0][0:RP, (RG + g) * E:(RG + g) * E + E], rows_f[:, g * RP:g * RP + RP], ident[0:E, 0:E])
                mm.then_inc(turned, 1)
                pe.wait_ge(idx_ready, 1)
                turn_rows(0)
                expert(0, False)
                with pe.Fori(1, E - 1) as e:
                    expert(e, False)
                expert(E - 1, True)


def kernel(x, ctx_1024, mask_Bx1xSxS2_ik0, g_xattn, g_ffn, L0_xattn_W_q, L0_xattn_W_k, L0_xattn_W_v, L0_xattn_W_o,
           L0_ffn_gate_w, L0_ffn_w_gate, L0_ffn_w_up, L0_ffn_w_down):
    import numpy as np
    import concourse.bacc as bacc
    from concourse.bass_utils import run_bass_kernel_spmd

    f = np.float32
    arr = np.asarray

    consts = np.zeros((P, C_END), f)
    consts[:, C_ID:C_ID + P] = np.eye(P, dtype=f)
    inv_freq = (f(1.0) / f(10000.0) ** (np.arange(0, DK, 2, dtype=f) / f(DK))).astype(f)
    angles = np.outer(np.arange(S2, dtype=f), inv_freq).astype(f)
    angles = np.concatenate([angles, angles], axis=1).T
    sign = np.where(np.arange(DK) < DK // 2, f(-1), f(1))[:, None]
    consts[:, C_COS:C_COS + S2] = np.tile(np.cos(angles), (P // DK, 1))
    consts[:, C_SIN:C_SIN + S2] = np.tile(np.sin(angles) * sign, (P // DK, 1))
    consts[3 * WAYS:3 * WAYS + HG, C_KSEL:C_KSEL + HG] = np.eye(HG, dtype=f)
    consts[0:E, C_ROW:] = np.repeat(np.arange(B) * S, TOPK)[None]

    def columns(w):
        return arr(w).T.reshape(DC, P, -1).transpose(1, 0, 2)

    turns = [head_of(h) for h in range(H)]
    wv = arr(L0_xattn_W_v).reshape(H, DK, D)[turns].reshape(D, D)
    wo = arr(L0_xattn_W_o).T.reshape(H, DK, D)[turns].reshape(2, 4, 2, DK, D).transpose(1, 3, 2, 0, 4).reshape(P, DC, D)
    ctxT = arr(ctx_1024).transpose(0, 2, 1).reshape(B, DC, P, S2).transpose(0, 2, 1, 3)
    mask = arr(mask_Bx1xSxS2_ik0).reshape(B, S, S2)
    maskq = mask.reshape(B, QC, QP, S2).transpose(0, 2, 1, 3)
    maskt = mask.transpose(0, 2, 1).reshape(B, KC, KP, S).transpose(0, 2, 1, 3)
    wg, wu, wd = arr(L0_ffn_w_gate), arr(L0_ffn_w_up), arr(L0_ffn_w_down)
    wstream = np.empty((E, NU, P, UNIT), f)
    for k, w in ((0, wg), (1, wu)):
        wstream[:, 0:GU].reshape(E, GU, P, 2, DC, P)[:, :, :, k] = w.reshape(E, IC, P, DC, P).transpose(0, 1, 4, 3, 2)
    wstream[:, GU:] = wd.transpose(0, 2, 1).reshape(E, DU, 2, P, D).transpose(0, 1, 3, 2, 4).reshape(E, DU, P, UNIT)

    arrays = {
        "ctxT": ctxT, "x_rows": arr(x).reshape(B, QC, QP, D).transpose(0, 2, 1, 3), "maskq": maskq, "maskt": maskt,
        "wk": columns(L0_xattn_W_k), "wv": columns(wv), "wq": columns(L0_xattn_W_q), "wo": wo,
        "gatew": columns(L0_ffn_gate_w), "gx": np.broadcast_to(arr(g_xattn), (P, 1)), "gf": np.broadcast_to(arr(g_ffn), (P, 1)),
        "wstream": wstream.reshape(E * NU, P, UNIT), "consts": consts,
    }
    arrays = {n: np.ascontiguousarray(a) for n, a in arrays.items()}
    nc = bacc.Bacc("TRN2", target_bir_lowering=False, num_devices=1)
    args = [nc.dram_tensor(n, a.shape, mybir.dt.from_np(a.dtype), kind="ExternalInput").ap() for n, a in arrays.items()]
    out = nc.dram_tensor("out", (B, S, D), F32, kind="ExternalOutput").ap()
    (ctxT_, x_, mq_, mt_, wk_, wv_, wq_, wo_, gw_, gx_, gf_, ws_, cs_) = args
    program(nc, ctxT_, x_, mq_, mt_, wk_, wv_, wq_, wo_, gw_, gx_, gf_, ws_, cs_, out)
    r = run_bass_kernel_spmd(nc, [arrays], core_ids=[0])
    return r.results[0]["out"]
```

```python
from contextlib import ExitStack

import concourse.bass as bass
from concourse import mybir

F32 = mybir.dt.float32
F32R = mybir.dt.float32r
BF16 = mybir.dt.bfloat16
I32 = mybir.dt.int32
U32 = mybir.dt.uint32
ALU = mybir.AluOpType
ACT = mybir.ActivationFunctionType
AX_X = mybir.AxisListType.X
ds = bass.ds

B, S, D = 8, 224, 512
S2 = 750
H, DK = 16, 32
E, I = 8, 2048
TOPK = S // E * 2
P = 128
DC = D // P
QP, QC = 112, S // 112
KP, KC = 125, S2 // 125
KN = 376
SK = 2 * KN
HG, NG = 4, H // 4
VH = 8
VW = 2 * DK + 1
PAIR = 2 * S
SCALE = float(DK) ** -0.5
EPS = 1e-5
MASKED = -(2.0 ** 100)
SLOTS = B * TOPK
RP, RG = 2 * TOPK, B // 2
IC = I // P
UNIT = 2 * DC * P
GU, DU = IC, IC // 2
NU = GU + DU
NRAW = 4
LEAD = 3
WAYS = 32

C_ID = 0
C_COS = C_ID + P
C_SIN = C_COS + S
C_KSEL = C_SIN + S
C_ROW = C_KSEL + HG
C_END = C_ROW + B * TOPK

ROTATE = [(d + DK // 2) % DK for d in range(DK)]


def after(eng, sem, value):
    if not (isinstance(value, int) and value <= 0):
        eng.wait_ge(sem, value)


def program(nc, ctxT, x, maskq, maskt, wk, wv, wq, wo, gatew, gx, gf, wstream, consts, rotations, out):
    kd = nc.dram_tensor("k_split", (B, NG, 2, P, SK), F32, kind="Internal").ap()
    vd = nc.dram_tensor("v_split", (B, 2, KP, KC * VH * VW), F32, kind="Internal").ap()
    xn_rows = nc.dram_tensor("xn_rows", (B * S, D), F32, kind="Internal").ap()
    out_rows = out.rearrange("b s d -> (b s) d")

    with ExitStack() as top:
        def sem(name):
            return top.enter_context(nc.semaphore(name))

        def sb(stack, name, shape, dt=F32):
            return stack.enter_context(nc.sbuf_tensor(name, shape, dt))

        def ps(stack, name, shape, dt=F32):
            return stack.enter_context(nc.psum_tensor(name, shape, dt))

        cst = sb(top, "cst", [P, C_END])
        ident = cst[:, C_ID:C_ID + P]
        cos, sin = cst[:, C_COS:C_COS + S], cst[:, C_SIN:C_SIN + S]
        gate_all = sb(top, "gate_all", [E, B, TOPK])
        row_all = sb(top, "row_all", [E, B, TOPK])
        gains = sb(top, "gains", [P, 2])

        wq_sb, wq_in = sb(top, "wq_sb", [P, DC, D]), sem("wq_in")

        project_context(nc, sem, sb, ps, ctxT, wk, wv, wq, wq_sb, wq_in, gx, gf, consts, rotations, kd, vd, cst, gains)
        attend(nc, sem, sb, ps, x, maskq, maskt, wq_sb, wq_in, wo, gatew, kd, vd, xn_rows, out, cst, ident,
               cos, sin, gains, gate_all, row_all)
        experts(nc, sem, sb, ps, wstream, xn_rows, out_rows, cst, ident, gains, gate_all, row_all)


def project_context(nc, sem, sb, ps, ctxT, wk, wv, wq, wq_sb, wq_in, gx, gf, consts, rotations, kd, vd, cst, gains):
    with ExitStack() as st:
        wraw = sb(st, "wraw", [P, 2, DC, D])
        w_hi = sb(st, "w_hi", [P, 2, DC, D], F32R)
        w_lo = sb(st, "w_lo", [P, 2, DC, D], F32R)
        graw = sb(st, "graw", [P, 2])
        rot = sb(st, "rot", [P, 2, SK])
        cos, sin = rot[:, 0], rot[:, 1]
        c_raw = [sb(st, f"c_raw{j}", [P, DC, S2]) for j in range(2)]
        c_hi = [sb(st, f"c_hi{j}", [P, DC, SK], F32R) for j in range(2)]
        c_lo = [sb(st, f"c_lo{j}", [P, DC, SK], F32R) for j in range(2)]
        k_raw = [sb(st, f"k_raw{j}", [P, SK]) for j in range(2)]
        k_cos = [sb(st, f"k_cos{j}", [P, SK]) for j in range(2)]
        k_rot = [sb(st, f"k_rot{j}", [P, SK]) for j in range(2)]
        k_split = [sb(st, f"k_split{j}", [P, 2, SK], F32R) for j in range(2)]
        v_out = sb(st, "v_out", [KP, 2, KC, VH, VW], F32R)
        k_ps = [ps(st, f"k_ps{j}", [P, 2, 512]) for j in range(2)]
        v_ps = [ps(st, f"v_ps{j}", [P, 512]) for j in range(4)]

        weights_in, consts_in, gains_in = [sem(f"weights_in{k}") for k in range(2)], sem("consts_in"), sem("gains_in")
        gains_done = sem("gains_done")
        wsplit_hi, wsplit_lo, pads_set = sem("wsplit_hi"), sem("wsplit_lo"), sem("pads_set")
        ctx_in = [sem(f"ctx_in{j}") for j in range(2)]
        ctx_hi, ctx_lo = sem("ctx_hi"), [sem(f"ctx_lo{j}") for j in range(2)]
        k_made, v_made = sem("k_made"), [sem(f"v_made{j}") for j in range(2)]
        kraw_done = [sem(f"kraw_done{j}") for j in range(2)]
        kcos_done, krot_done, ksin_done, ksum_done = sem("kcos_done"), sem("krot_done"), sem("ksin_done"), sem("ksum_done")
        khi_done, klo_done = sem("khi_done"), [sem(f"klo_done{j}") for j in range(2)]
        vhi_done, vlo_done = sem("vhi_done"), [sem(f"vlo_done{j}") for j in range(4)]
        k_stored = [sem(f"k_stored{j}") for j in range(2)]
        v_stored = sem("v_stored")

        with nc.Block() as block:
            @block.sync
            def _(sp):
                def hold(s_, v_):
                    sp.wait_ge(s_, v_)
                    sp.nop(nofuse=True)

                sp.dma_start(wraw[:, 0], wk).then_inc(weights_in[0], 16)

                def load_ctx(i, j):
                    if not isinstance(i, int):
                        hold(ctx_lo[j], DC * i)
                    sp.dma_start(c_raw[j][:], ctxT[ds(2 * i + j, 1)].rearrange("o p c n -> p (o c) n")).then_inc(ctx_in[j], 16)

                load_ctx(0, 0)
                sp.dma_start(wraw[:, 1], wv).then_inc(weights_in[1], 16)
                sp.dma_start(graw[:, 0:1], gx).then_inc(gains_in, 16)
                sp.dma_start(graw[:, 1:2], gf).then_inc(gains_in, 16)
                load_ctx(0, 1)
                with sp.Fori(1, B // 2) as i:
                    for j in range(2):
                        load_ctx(i, j)
                sp.dma_start(wq_sb[:], wq).then_inc(wq_in, 16)

            @block.gpsimd
            def _(pool):
                pool.dma_start(cst[:], consts).then_inc(consts_in, 16)
                pool.dma_start(rot[:], rotations).then_inc(consts_in, 16)
                for j in range(2):
                    nc.gpsimd.memset(c_hi[j][:, :, S2:SK].bitcast(F32), 0.0)
                    nc.gpsimd.memset(c_lo[j][:, :, S2:SK].bitcast(F32), 0.0)
                nc.gpsimd.memset(v_out[:, :, :, :, 2 * DK:VW].bitcast(F32), 1.0).then_inc(pads_set, 1)
                pool.wait_ge(consts_in, 32)
                with pool.Fori(0, B // 2) as i:
                    for g in range(2 * NG):
                        pool.wait_ge(krot_done, 2 * NG * i + g + 1)
                        nc.gpsimd.tensor_tensor(k_rot[g % 2][:], k_rot[g % 2][:], sin, ALU.mult).then_inc(ksin_done, 1)

            @block.scalar
            def _(act):
                def high_w(k, c):
                    nc.scalar.activation(w_hi[:, k, c], wraw[:, k, c], ACT.Copy).then_inc(wsplit_hi, 1)

                def split_ctx(i, j):
                    act.wait_ge(ctx_in[j], 16 * i + 16)
                    after(act, v_made[j], KC * i)
                    for c in range(DC):
                        nc.scalar.activation(c_hi[j][:, c, 0:S2], c_raw[j][:, c, :], ACT.Copy).then_inc(ctx_hi, 1)

                def copy_k(i, j, g):
                    act.wait_ge(k_made, 2 * NG * i + NG * j + g + 1)
                    after(act, klo_done[g % 2], NG * i + 2 * j + g // 2)
                    nc.scalar.activation(k_raw[g % 2][:].rearrange("p (a n) -> p a n", a=2),
                                         k_ps[g % 2][:, :, 0:KN], ACT.Copy).then_inc(kraw_done[g % 2], 1)

                def high_k(i, j, g):
                    act.wait_ge(ksum_done, 2 * NG * i + NG * j + g + 1)
                    after(act, k_stored[g % 2], 16 * (NG * i + 2 * j + g // 2))
                    nc.scalar.activation(k_split[g % 2][:, 0], k_cos[g % 2][:], ACT.Copy).then_inc(khi_done, 1)

                def store_k(i, j, g):
                    act.wait_ge(klo_done[g % 2], NG * i + 2 * j + g // 2 + 1)
                    act.dma_start(kd[ds(2 * i + j, 1), g].rearrange("o h p n -> p (o h) n"), k_split[g % 2][:].bitcast(F32)).then_inc(k_stored[g % 2], 16)

                def high_v(i, j, c):
                    act.wait_ge(v_made[j], KC * i + c + 1)
                    if c == 0:
                        after(act, v_stored, 16 * KC * (2 * i + j))
                    nc.scalar.activation(v_out[:, :, c, :, 0:DK],
                                         v_ps[(KC * j + c) % 4][0:KP, :].rearrange("p (a h d) -> p a h d", a=2, h=VH),
                                         ACT.Copy).then_inc(vhi_done, 1)

                def store_v(i, j, c):
                    act.wait_ge(vlo_done[(KC * j + c) % 4], 3 * i + (KC * j + c) // 4 + 1)
                    act.dma_start(vd[ds(2 * i + j, 1)].rearrange("o a p (c n) -> p (o a) c n", c=KC)[:, :, c],
                                  v_out[:, :, c].bitcast(F32).rearrange("p a h w -> p a (h w)")).then_inc(v_stored, 16)

                def pair(i, last):
                    for j in range(2):
                        copy_k(i, j, 0)
                        for g in range(1, NG):
                            copy_k(i, j, g)
                            high_k(i, j, g - 1)
                            if g > 1:
                                store_k(i, j, g - 2)
                        high_v(i, j, 0)
                        high_k(i, j, NG - 1)
                        store_k(i, j, NG - 2)
                        high_v(i, j, 1)
                        store_k(i, j, NG - 1)
                        store_v(i, j, 0)
                        if not (last and j):
                            split_ctx(*((i, 1) if j == 0 else (i + 1, 0)))
                        for c in range(2, KC):
                            high_v(i, j, c)
                            store_v(i, j, c - 1)
                        store_v(i, j, KC - 1)

                act.wait_ge(weights_in[0], 16)
                for c in range(DC):
                    high_w(0, c)
                split_ctx(0, 0)
                act.wait_ge(weights_in[1], 16)
                for c in range(DC):
                    high_w(1, c)
                act.wait_ge(gains_in, 32)
                nc.scalar.activation(gains[:], graw[:], ACT.Tanh).then_inc(gains_done, 1)
                pair(0, False)
                with act.Fori(1, B // 2 - 1) as i:
                    pair(i, False)
                pair(B // 2 - 1, True)
                for s in range(2):
                    act.wait_ge(k_stored[s], 16 * B * NG // 2)
                act.wait_ge(v_stored, 16 * KC * B)

            @block.vector
            def _(dve):
                def low_w(k, c):
                    dve.wait_ge(wsplit_hi, DC * k + c + 1)
                    nc.vector.tensor_tensor(w_lo[:, k, c], wraw[:, k, c], w_hi[:, k, c], ALU.subtract).then_inc(wsplit_lo, 1)


                def low_ctx(i, j):
                    for c in range(DC):
                        dve.wait_ge(ctx_hi, 2 * DC * i + DC * j + c + 1)
                        nc.vector.tensor_tensor(c_lo[j][:, c, 0:S2], c_raw[j][:, c, :], c_hi[j][:, c, 0:S2],
                                                ALU.subtract).then_inc(ctx_lo[j], 1)

                def rotate(i, j, g):
                    s = g % 2
                    dve.wait_ge(kraw_done[s], NG * i + 2 * j + g // 2 + 1)
                    dve.nop(nofuse=True)
                    nc.vector.stream_shuffle(k_rot[s][:], k_raw[s][:], ROTATE).then_inc(krot_done, 1)
                    nc.vector.tensor_tensor(k_cos[s][:], k_raw[s][:], cos, ALU.mult).then_inc(kcos_done, 1)

                def sum_k(i, j, g):
                    n, s = 2 * NG * i + NG * j + g, g % 2
                    dve.wait_ge(kcos_done, n + 1)
                    dve.wait_ge(ksin_done, n + 1)
                    nc.vector.tensor_tensor(k_cos[s][:], k_cos[s][:], k_rot[s][:], ALU.add).then_inc(ksum_done, 1)

                def low_k(i, j, g):
                    s = g % 2
                    dve.wait_ge(khi_done, 2 * NG * i + NG * j + g + 1)
                    nc.vector.tensor_tensor(k_split[s][:, 1], k_cos[s][:], k_split[s][:, 0], ALU.subtract).then_inc(klo_done[s], 1)

                def low_v(i, j, c):
                    q = (KC * j + c) % 4
                    dve.wait_ge(vhi_done, 2 * KC * i + KC * j + c + 1)
                    nc.vector.tensor_tensor(v_out[:, :, c, :, DK:2 * DK],
                                            v_ps[q][0:KP, :].rearrange("p (a h d) -> p a h d", a=2, h=VH),
                                            v_out[:, :, c, :, 0:DK], ALU.subtract).then_inc(vlo_done[q], 1)

                def pair(i, last):
                    for j in range(2):
                        rotate(i, j, 0)
                        for g in range(1, NG):
                            sum_k(i, j, g - 1)
                            rotate(i, j, g)
                            low_k(i, j, g - 1)
                        sum_k(i, j, NG - 1)
                        low_v(i, j, 0)
                        low_k(i, j, NG - 1)
                        low_v(i, j, 1)
                        if not (last and j):
                            low_ctx(*((i, 1) if j == 0 else (i + 1, 0)))
                        for c in range(2, KC):
                            low_v(i, j, c)

                for c in range(DC):
                    low_w(0, c)
                dve.wait_ge(pads_set, 1)
                low_ctx(0, 0)
                for c in range(DC):
                    low_w(1, c)
                dve.wait_ge(consts_in, 32)
                pair(0, False)
                with dve.Fori(1, B // 2 - 1) as i:
                    pair(i, False)
                pair(B // 2 - 1, True)

            @block.tensor
            def _(pe):
                pe.wait_ge(wsplit_lo, DC)
                pe.wait_ge(pads_set, 1)

                def pair(i):
                    for j in range(2):
                        for g in range(NG):
                            after(pe, kraw_done[g % 2], NG * i + 2 * j + g // 2)
                            w = slice(g * P, g * P + P)
                            for n in range(2):
                                cols = slice(n * KN, n * KN + KN)
                                o = k_ps[g % 2][:, n, 0:KN]
                                for c in range(DC):
                                    if g == 0 and n == 0:
                                        pe.wait_ge(ctx_lo[j], DC * i + c + 1)
                                    nc.tensor.matmul(o, w_hi[:, 0, c, w], c_hi[j][:, c, cols], start=(c == 0), stop=False)
                                    nc.tensor.matmul(o, w_hi[:, 0, c, w], c_lo[j][:, c, cols], start=False, stop=False)
                                    mm = nc.tensor.matmul(o, w_lo[:, 0, c, w], c_hi[j][:, c, cols], start=False, stop=(c == DC - 1))
                            mm.then_inc(k_made, 1)
                        if isinstance(i, int) and j == 0:
                            pe.wait_ge(wsplit_lo, 2 * DC)
                        for k in range(KC):
                            after(pe, vlo_done[(KC * j + k) % 4], 3 * i + (KC * j + k) // 4)
                            rows = slice(k * KP, k * KP + KP)
                            o = v_ps[(KC * j + k) % 4][0:KP, :]
                            for c in range(DC):
                                nc.tensor.matmul(o, c_hi[j][:, c, rows], w_hi[:, 1, c, :], start=(c == 0), stop=False)
                                nc.tensor.matmul(o, c_hi[j][:, c, rows], w_lo[:, 1, c, :], start=False, stop=False)
                                mm = nc.tensor.matmul(o, c_lo[j][:, c, rows], w_hi[:, 1, c, :], start=False, stop=(c == DC - 1))
                            mm.then_inc(v_made[j], 1)

                pair(0)
                with pe.Fori(1, B // 2) as i:
                    pair(i)



M_GROUP = HG * QC + 1
M_USES = NG * M_GROUP
assert M_USES % 2 == 0
NST = H * KC // 2
KSLOTS = 2 * HG
F_XT, F_Q, F_USES = 0, 2, 4
R_Y, R_XNT, R_LOGIT, R_AFF, R_USES = 0, 2, 4, 5, 6
ROUNDS = TOPK // 8
MLEAD = HG + 1


def head_of(turn):
    return HG * (turn % HG) + turn // HG


def max_use(h, qc):
    return h // HG * M_GROUP + h % HG * QC + qc


def neg_use(g):
    return g * M_GROUP + HG * QC


def attend(nc, sem, sb, ps, x, maskq, maskt, wq_sb, wq_in, wo, gatew, kd, vd, xn_rows, out, cst, ident,
           cos, sin, gains, gate_all, row_all):
    with ExitStack() as st:
        wo_sb = sb(st, "wo_sb", [P, DC, D])
        gw_sb = sb(st, "gw_sb", [P, DC, E])
        identb = sb(st, "identb", [P, P], BF16)
        ks = sb(st, "ks", [P, KSLOTS, SK], F32R)
        qs = sb(st, "qs", [P, H, S], F32R)
        vs = [sb(st, f"vs{j}", [KP, KC, VH, VW], F32R) for j in range(2)]
        mq_raw, mt_raw = sb(st, "mq_raw", [QP, QC, S2], I32), sb(st, "mt_raw", [KP, KC, S], I32)
        mq = sb(st, "mq", [QP, QC, SK])
        mt = [sb(st, f"mt{j}", [KP, KC, S], BF16) for j in range(2)]
        x_t, x_res = sb(st, "x_t", [QP, QC, D]), sb(st, "x_res", [QP, QC, D])
        stats, mv, rstd = sb(st, "stats", [QP, QC, 6]), sb(st, "mv", [QP, 2, QC, 2]), sb(st, "rstd", [QP, 2, QC])
        var, minus_half = sb(st, "var", [QP, QC]), sb(st, "minus_half", [QP, QC])
        xn = sb(st, "xn", [QP, QC, D])
        xT = sb(st, "xT", [P, 2, 2 * S])
        q_raw, q_rot = sb(st, "q_raw", [P, NG, S]), sb(st, "q_rot", [P, NG, S])
        q_cos = sb(st, "q_cos", [P, NG, S])
        q_hi, q_lo = sb(st, "q_hi", [P, NG, S], F32R), sb(st, "q_lo", [P, NG, S], F32R)
        junk = [sb(st, f"junk{j}", [QP, SK]) for j in range(2)]
        mx = sb(st, "mx", [QP, 2, QC, P])
        e_t = [[sb(st, f"e_t{j}_{pc}", [KP, PAIR]) for pc in range(KC // 2)] for j in range(2)]
        p_hi = [sb(st, f"p_hi{j}", [KP, KC // 2, PAIR], F32R) for j in range(2)]
        p_lo = [sb(st, f"p_lo{j}", [KP, KC // 2, PAIR], F32R) for j in range(2)]
        c_a, c_b, c_s = (sb(st, n, [P, 2, PAIR]) for n in ("c_a", "c_b", "c_s"))
        cx = sb(st, "cx", [P, 2, PAIR])
        x2 = x_res
        x2o, xn2 = sb(st, "x2o", [QP, QC, D]), sb(st, "xn2", [QP, QC, D])
        flag = sb(st, "flag", [QP, 4, QC])
        lg, ex = sb(st, "lg", [QP, QC, E]), sb(st, "ex", [QP, QC, E])
        aff = sb(st, "aff", [QP, QC, E])
        lmax, lsum = sb(st, "lmax", [QP, QC]), sb(st, "lsum", [QP, QC])
        aff8 = [sb(st, f"aff8_{j}", [E, S]) for j in range(2)]
        top_v, top_i = sb(st, "top_v", [E, TOPK]), sb(st, "top_i", [E, TOPK], U32)

        m_ps = [ps(st, f"m_ps{j}", [P, 2, 512]) for j in range(2)]
        s_ps = [ps(st, f"s_ps{j}", [P, 512]) for j in range(2)]
        o_ps, w_ps = ps(st, "o_ps", [P, 512]), ps(st, "w_ps", [P, 512])

        att_in, sel_set, fill_set = sem("att_in"), sem("sel_set"), sem("fill_set")
        x_in, mq_in, mt_in, xres_in = sem("x_in"), sem("mq_in"), sem("mt_in"), sem("xres_in")
        mq_done, mt_done = sem("mq_done"), sem("mt_done")
        ks_in = [sem(f"ks_in{j}") for j in range(KSLOTS // 2)]
        vs_in = [sem(f"vs_in{j}") for j in range(2)]
        qs_in = [sem(f"qs_in{j}") for j in range(NG)]
        ahead_step, rest_step, flag_step, spread_done = sem("ahead_step"), sem("rest_step"), sem("flag_step"), sem("spread_done")
        soft_step = sem("soft_step")
        mv_done = [sem(f"mv_done{j}") for j in range(2)]
        var_done, rstd_done = sem("var_done"), [sem(f"rstd_done{j}") for j in range(2)]
        xn_done, xn2_done = sem("xn_done"), sem("xn2_done")
        m_made, m_free = sem("m_made"), [sem(f"m_free{j}") for j in range(2)]
        ahead_made, ahead_free = sem("ahead_made"), sem("ahead_free")
        rest_made, rest_free = sem("rest_made"), sem("rest_free")
        qrot_done, qcos_done, qsin_done, qsum_done = sem("qrot_done"), sem("qcos_done"), sem("qsin_done"), sem("qsum_done")
        qhi_done, qlo_done = sem("qhi_done"), sem("qlo_done")
        s_made = sem("s_made")
        exp_done = [[sem(f"exp_done{g}{j}") for j in range(2)] for g in range(2)]
        phi_done = [sem(f"phi_done{j}") for j in range(3)]
        plo_done = [sem(f"plo_done{j}") for j in range(3)]
        pv_done = [[sem(f"pv_done{a}{j}") for j in range(2)] for a in range(2)]
        copied = sem("copied")
        ab_done, cx_done = sem("ab_done"), [sem(f"cx_done{j}") for j in range(2)]
        recip_done = sem("recip_done")
        lsub_done, lexp_done, aff_done = sem("lsub_done"), sem("lexp_done"), sem("aff_done")
        x2o_done, rows_stored, out_stored = sem("x2o_done"), sem("rows_stored"), sem("out_stored")

        def made(b, u):
            return M_USES * b + u + 1

        def freed(b, u):
            return M_USES // 2 * b + u // 2 + 1

        def exp_at(b, h, pc):
            if pc < 0:
                h, pc = h - 1, pc + KC // 2
            if h < 0:
                b, h = b - 1, h + H
            g, k = h // HG, h % HG * (KC // 2) + pc
            return exp_done[g % 2][(h * (KC // 2) + pc) % 2], NST // 4 * b + (HG * KC // 4) * (g // 2) + k // 2 + 1

        def pv_at(b, h):
            if h < 0:
                b, h = b - 1, h + H
            return pv_done[h // VH][h % 2], VH // 2 * b + h % VH // 2 + 1

        def every_batch(engine, start, body, end):
            start()
            body(0, 0, True, False)
            with engine.Fori(0, B // 2 - 1) as i:
                for j in range(2):
                    body(2 * i + 1 + j, (1 + j) % 2, False, False)
            body(B - 1, (B - 1) % 2, False, True)
            end()

        with nc.Block() as block:
            @block.sync
            def _(sp):
                def hold(s_, v_):
                    if not (isinstance(v_, int) and v_ <= 0):
                        sp.wait_ge(s_, v_)
                        sp.nop(nofuse=True)

                def load_k(b, h):
                    hold(*exp_at(b, h + 1 - KSLOTS, KC // 2 - 1))
                    g, k, s = h // HG, h % HG, h % KSLOTS
                    for r, part in ((0, 0), (1, 1), (2, 0)):
                        sp.dma_start(ks[r * WAYS:r * WAYS + WAYS, s:s + 2].bitcast(F32),
                                     kd[ds(b, 1), k:k + 2, part, g * DK:g * DK + DK].rearrange("o g d n -> d (o g) n")).then_inc(ks_in[s // 2], 16)

                def load_v(b, a):
                    hold(pv_done[a][0], VH // 2 * b)
                    hold(pv_done[a][1], VH // 2 * b)
                    sp.dma_start(vs[a][:].bitcast(F32).rearrange("p c h w -> p (c h w)"),
                                 vd[ds(b, 1), a].rearrange("o p n -> p (o n)")).then_inc(vs_in[a], 16)

                def stack_q(b, g):
                    hold(qlo_done, b + 1)
                    hold(*exp_at(b - 1, g * HG + HG - 1, KC // 2 - 1))
                    for r, part in ((0, q_hi), (1, q_hi), (2, q_lo)):
                        sp.dma_start(qs[r * WAYS:r * WAYS + WAYS, g * HG:g * HG + HG, :].bitcast(F32),
                                     part[g * DK:g * DK + DK].bitcast(F32)).then_inc(qs_in[g], 16)

                def load_x(b):
                    hold(xn_done, QC * b)
                    sp.dma_start(x_t[:], x[ds(b, 1)].rearrange("o p c n -> p (o c) n")).then_inc(x_in, 16)

                def load_mq(b):
                    hold(mq_done, b)
                    sp.dma_start(mq_raw[:], maskq[ds(b, 1)].rearrange("o p c n -> p (o c) n")).then_inc(mq_in, 16)

                def load_mt(b):
                    hold(mt_done, b)
                    sp.dma_start(mt_raw[:], maskt[ds(b, 1)].rearrange("o p c n -> p (o c) n")).then_inc(mt_in, 16)

                def load_res(b):
                    hold(rest_free, R_USES * b + 1)
                    sp.dma_start(x_res[:], x[ds(b, 1)].rearrange("o p c n -> p (o c) n")).then_inc(xres_in, 16)

                def start():
                    load_x(0)
                    load_mq(0)
                    load_k(0, 0)
                    load_k(0, 2)
                    load_mt(0)
                    load_k(0, 4)
                    load_v(0, 0)
                    sp.dma_start(wo_sb[:], wo).then_inc(att_in, 16)
                    sp.dma_start(gw_sb[:], gatew).then_inc(att_in, 16)
                    for g in range(NG):
                        stack_q(0, g)

                def body(b, j, first, last):
                    if not last:
                        load_x(b + 1)
                    if not first:
                        load_res(b - 1)
                    if not last:
                        load_mq(b + 1)
                    for t in range(0, H, 2):
                        if t + 6 < H:
                            load_k(b, t + 6)
                        elif not last:
                            load_k(b + 1, t + 6 - H)
                        if t == 0 and not first:
                            stack_q(b, NG - 1)
                        if t == 2:
                            load_v(b, 1)
                            if not last:
                                load_mt(b + 1)
                        if t == 8 and not last:
                            stack_q(b + 1, 0)
                            stack_q(b + 1, 1)
                        if t == 10 and not last:
                            load_v(b + 1, 0)
                        if t == 12 and not last:
                            stack_q(b + 1, 2)

                every_batch(sp, start, body, lambda: load_res(B - 1))

            @block.gpsimd
            def _(pool):
                def hold(s_, v_):
                    if not (isinstance(v_, int) and v_ <= 0):
                        pool.wait_ge(s_, v_)
                        pool.nop(nofuse=True)

                def root(b, which, before):
                    hold(mv_done[which], b + 1)
                    nc.gpsimd.tensor_scalar(var[:], mv[:, which, :, 1], EPS, None, ALU.add).then_inc(var_done, 1)
                    hold(var_done, before + 1)
                    nc.gpsimd.tensor_tensor(rstd[:, which], var[:], minus_half[:], ALU.pow).then_inc(rstd_done[which], 1)

                def sines(b):
                    hold(qrot_done, b + 1)
                    nc.gpsimd.tensor_tensor(q_rot[:], q_rot[:], sin[:, None, 0:S].broadcast_to((P, NG, S)), ALU.mult).then_inc(qsin_done, 1)

                def add_parts(b, a):
                    hold(copied, H // 2 * b + 4 * a + 4)
                    nc.gpsimd.tensor_tensor(c_a[:, a], c_a[:, a], c_b[:, a], ALU.add).then_inc(ab_done, 1)

                def split_low(b, h):
                    for pc in range(KC // 2):
                        hold(phi_done[pc], H * b + h + 1)
                        nc.gpsimd.tensor_tensor(p_lo[h % 2][:, pc], e_t[h % 2][pc][:], p_hi[h % 2][:, pc], ALU.subtract).then_inc(plo_done[pc], 1)

                def store_out(b):
                    hold(x2o_done, QC * b + QC)
                    pool.dma_start(out[ds(b, 1)].rearrange("o (c p) n -> p (o c) n", c=QC), x2o[:]).then_inc(out_stored, 16)

                def store_rows(b):
                    hold(xn2_done, QC * b + QC)
                    pool.dma_start(xn_rows.rearrange("(b c p) n -> b p c n", b=B, c=QC)[ds(b, 1)].rearrange("o p c n -> p (o c) n"),
                                   xn2[:]).then_inc(rows_stored, 16)

                def start():
                    nc.gpsimd.memset(minus_half[:], -0.5).then_inc(fill_set, 1)
                    nc.gpsimd.memset(mq[:, :, S2:SK], MASKED).then_inc(fill_set, 1)
                    nc.gpsimd.memset(mx[:], 0.0).then_inc(fill_set, 1)
                    hold(fill_set, 3)
                    root(0, 0, 0)
                    sines(0)

                def body(b, j, first, last):
                    for t in range(H):
                        split_low(b, t)
                        if not last:
                            if t == 0:
                                root(b + 1, 0, b + 1 if first else 2 * b)
                            if t == 6:
                                sines(b + 1)
                        if not first:
                            if t == 1:
                                add_parts(b - 1, 1)
                            if t == 7:
                                root(b - 1, 1, 2 * B - 2 if last else 2 * b + 1)
                                store_out(b - 1)
                            if t == 9:
                                store_rows(b - 1)
                        if t == 9:
                            add_parts(b, 0)

                def end():
                    add_parts(B - 1, 1)
                    root(B - 1, 1, 2 * B - 1)
                    store_out(B - 1)
                    store_rows(B - 1)
                    pool.wait_ge(out_stored, 16 * B)
                    pool.wait_ge(rows_stored, 16 * B)

                every_batch(pool, start, body, end)

            @block.scalar
            def _(act):
                def x_columns(b, n):
                    act.wait_ge(ahead_made, F_USES * b + F_XT + n + 1)
                    after(act, rest_free, R_USES * (b - 2) + 1)
                    nc.scalar.activation(xT[:, n], w_ps[:, 0:2 * S], ACT.Copy).then_inc(ahead_free, 1)

                def x2_columns(b, n):
                    act.wait_ge(rest_made, R_USES * b + R_XNT + n + 1)
                    nc.scalar.activation(xT[:, n], w_ps[:, 0:2 * S], ACT.Copy).then_inc(rest_free, 1)

                def queries(b, n):
                    act.wait_ge(ahead_made, F_USES * b + F_Q + n + 1)
                    nc.scalar.activation(q_raw[:, 2 * n:2 * n + 2].rearrange("p c s -> p (c s)"), w_ps[:, 0:2 * S], ACT.Copy).then_inc(ahead_free, 1)

                def high_q(b):
                    act.wait_ge(qsum_done, b + 1)
                    for g in range(NG):
                        after(act, qs_in[g], 48 * b)
                    nc.scalar.activation(q_hi[:], q_cos[:], ACT.Copy).then_inc(qhi_done, 1)

                def neg_max(b, g):
                    u = neg_use(g)
                    act.wait_ge(m_made, made(b, u))
                    nc.scalar.activation(qs[3 * WAYS:P, g * HG:g * HG + HG, :],
                                         m_ps[u % 2][3 * WAYS:P, 0:1, 0:S].broadcast_to((WAYS, HG, S)),
                                         ACT.Copy, scale=-1.0).then_inc(m_free[u % 2], 1)

                def exp(b, h, pc):
                    n = h * (KC // 2) + pc
                    act.wait_ge(s_made, NST * b + n + 1)
                    after(act, plo_done[pc], H * b + h - 1)
                    nc.scalar.activation(e_t[h % 2][pc][:], s_ps[n % 2][0:KP, 0:PAIR], ACT.Exp, scale=SCALE).then_inc(exp_at(b, h, pc)[0], 1)

                def high(b, h, pc):
                    act.wait_ge(*exp_at(b, h, pc))
                    after(act, *pv_at(b, h - 2))
                    nc.scalar.activation(p_hi[h % 2][:, pc], e_t[h % 2][pc][:], ACT.Copy).then_inc(phi_done[pc], 1)

                def copy_ctx(b, q):
                    a, j = q // 4, q % 4
                    act.wait_ge(*pv_at(b, 2 * q + 1))
                    if j == 0:
                        after(act, cx_done[a], b)
                    rows = slice(j * WAYS, j * WAYS + WAYS)
                    nc.scalar.activation(c_a[rows, a], o_ps[0:DK, 0:PAIR], ACT.Copy)
                    nc.scalar.activation(c_b[rows, a], o_ps[DK:2 * DK, 0:PAIR], ACT.Copy)
                    nc.scalar.activation(c_s[rows, a], o_ps[2 * DK:3 * DK, 0:PAIR], ACT.Copy).then_inc(copied, 1)

                def logit_exp(b):
                    act.wait_ge(lsub_done, b + 1)
                    nc.scalar.activation(ex[:], lg[:], ACT.Exp).then_inc(lexp_done, 1)

                def start():
                    for n in range(2):
                        x_columns(0, n)
                    nc.scalar.activation(ks[3 * WAYS:P, 0:HG], cst[3 * WAYS:P, C_KSEL:C_KSEL + HG, None].broadcast_to((WAYS, HG, SK)),
                                         ACT.Copy).then_inc(sel_set, 1)
                    nc.scalar.activation(identb[:], ident, ACT.Copy).then_inc(sel_set, 1)
                    queries(0, 0)
                    nc.scalar.activation(ks[3 * WAYS:P, HG:KSLOTS], cst[3 * WAYS:P, C_KSEL:C_KSEL + HG, None].broadcast_to((WAYS, HG, SK)),
                                         ACT.Copy).then_inc(sel_set, 1)
                    queries(0, 1)
                    high_q(0)
                    neg_max(0, 0)

                def body(b, j, first, last):
                    for t in range(H):
                        exp(b, t, 0)
                        if t == 1 and not first:
                            copy_ctx(b - 1, 7)
                        if t > 1 and t % 2:
                            copy_ctx(b, (t - 3) // 2)
                        exp(b, t, 1)
                        high(b, t, 0)
                        exp(b, t, 2)
                        high(b, t, 1)
                        high(b, t, 2)
                        if t % HG == HG - 1 and t < H - 1:
                            neg_max(b, t // HG + 1)
                        if t == H - 1 and not last:
                            neg_max(b + 1, 0)
                        if not last:
                            if t in (2, 3):
                                x_columns(b + 1, t - 2)
                            if t in (4, 5):
                                queries(b + 1, t - 4)
                            if t == 7:
                                high_q(b + 1)
                        if not first:
                            if t in (9, 10):
                                x2_columns(b - 1, t - 9)
                            if t == 11:
                                logit_exp(b - 1)

                def end():
                    copy_ctx(B - 1, 7)
                    for n in range(2):
                        x2_columns(B - 1, n)
                    logit_exp(B - 1)

                every_batch(act, start, body, end)

            @block.vector
            def _(dve):
                def hold(s_, v_):
                    if not (isinstance(v_, int) and v_ <= 0):
                        dve.wait_ge(s_, v_)
                        dve.nop(nofuse=True)

                def done(ins, s_, value, alone=False):
                    ins.then_inc(s_, 1)
                    dve.wait_ge(s_, value)
                    if alone:
                        dve.nop(nofuse=True)

                def moments(b, which, src):
                    for c in range(QC):
                        ins = nc.vector.bn_stats(stats[:, c], src[:, c])
                    done(ins, ahead_step if which == 0 else rest_step, b + 1, alone=True)
                    for c in range(QC):
                        ins = nc.vector.bn_aggr(mv[:, which, c], stats[:, c])
                    ins.then_inc(mv_done[which], 1)

                def norm(b, which, src, dst, s_):
                    dve.wait_ge(rstd_done[which], b + 1)
                    dve.wait_ge(mv_done[which], b + 1)
                    for c in range(QC):
                        nc.vector.tensor_scalar(dst[:, c], src[:, c], mv[:, which, c, 0:1], rstd[:, which, c:c + 1],
                                                ALU.subtract, ALU.mult).then_inc(s_, 1)

                def mask_queries(b):
                    dve.wait_ge(mq_in, 16 * b + 16)
                    for qc in range(QC):
                        u = max_use(H - 1, qc)
                        after(dve, m_free[u % 2], freed(b - 1, u))
                    nc.vector.tensor_scalar(mq[:, :, 0:S2], mq_raw[:], 0, MASKED, ALU.is_equal, ALU.mult).then_inc(mq_done, 1)

                def mask_keys(b, j):
                    dve.wait_ge(mt_in, 16 * b + 16)
                    after(dve, *exp_at(b - 2, H - 1, KC // 2 - 1))
                    nc.vector.tensor_scalar(mt[j][:], mt_raw[:], 0, MASKED, ALU.is_equal, ALU.mult).then_inc(mt_done, 1)

                def maxima(b, h):
                    if h == 0:
                        dve.wait_ge(mq_done, b + 1)
                    g, hh = h // HG, h % HG
                    if hh == 0:
                        g_, b_ = (g - 2, b) if g >= 2 else (g + 2, b - 1)
                        after(dve, m_made, made(b_, neg_use(g_)))
                    for qc in range(QC):
                        u = max_use(h, qc)
                        dve.wait_ge(m_made, made(b, u))
                        hold(m_free[u % 2], freed(b, u) - 1)
                        nc.vector.tensor_tensor_reduce(junk[u % 2][:].rearrange("p (a n) -> p a n", a=2), m_ps[u % 2][0:QP, :, 0:KN],
                                                       mq[:, qc].rearrange("p (a n) -> p a n", a=2), 1.0, -3e38, ALU.add, ALU.max,
                                                       mx[:, g % 2, qc, 3 * WAYS + hh:3 * WAYS + hh + 1]).then_inc(m_free[u % 2], 1)

                def recip_sums(b, a, n):
                    if n == 0:
                        hold(copied, H // 2 * b + 4 * a + 4)
                        done(nc.vector.stream_shuffle(cx[:, a], c_s[:, a], [0] * WAYS), spread_done, 2 * b + a + 1)
                    half = slice(n * S, n * S + S)
                    nc.vector.reciprocal(c_s[:, a, half], cx[:, a, half]).then_inc(recip_done, 1)

                def normalise(b, a):
                    dve.wait_ge(recip_done, 4 * b + 2 * a + 2)
                    dve.wait_ge(ab_done, 2 * b + a + 1)
                    nc.vector.tensor_tensor(cx[:, a], c_a[:, a], c_s[:, a], ALU.mult).then_inc(cx_done[a], 1)

                def rotate(b):
                    dve.wait_ge(ahead_free, F_USES * (b + 1))
                    nc.vector.tensor_tensor(q_cos[:], q_raw[:], cos[:, None, 0:S].broadcast_to((P, NG, S)), ALU.mult).then_inc(qcos_done, 1)
                    nc.vector.stream_shuffle(q_rot[:], q_raw[:], ROTATE).then_inc(qrot_done, 1)

                def sum_q(b):
                    dve.wait_ge(qcos_done, b + 1)
                    dve.wait_ge(qsin_done, b + 1)
                    nc.vector.tensor_tensor(q_cos[:], q_cos[:], q_rot[:], ALU.add).then_inc(qsum_done, 1)

                def low_q(b):
                    dve.wait_ge(qhi_done, b + 1)
                    nc.vector.tensor_tensor(q_lo[:], q_cos[:], q_hi[:], ALU.subtract).then_inc(qlo_done, 1)

                def flags(b):
                    for qc in range(QC):
                        u = max_use(H - 1, qc)
                        dve.wait_ge(m_free[u % 2], freed(b, u))
                    done(nc.vector.tensor_scalar(flag[:, 0], mx[:, (NG - 1) % 2, :, 3 * WAYS], MASKED / 2, None, ALU.is_lt), flag_step, 5 * b + 1)
                    done(nc.vector.tensor_scalar(flag[:, 1], flag[:, 0], -1.0, 1.0, ALU.mult, ALU.add), flag_step, 5 * b + 2)
                    done(nc.vector.reciprocal(flag[:, 2], flag[:, 1]), flag_step, 5 * b + 3)
                    done(nc.vector.tensor_scalar(flag[:, 3], flag[:, 2], 0.0, None, ALU.mult), flag_step, 5 * b + 4)
                    done(nc.vector.tensor_scalar(flag[:, 1], flag[:, 0], -4.0, None, ALU.mult), flag_step, 5 * b + 5)

                def residual(b, c):
                    dve.wait_ge(xres_in, 16 * b + 16)
                    dve.wait_ge(rest_made, R_USES * b + R_Y + c + 1)
                    nc.vector.scalar_tensor_tensor(out=x2[:, c], in0=w_ps[0:QP, :], scalar=gains[0:QP, 0:1], in1=x_res[:, c],
                                                   op0=ALU.mult, op1=ALU.add).then_inc(rest_free, 1)

                def x2_out(b):
                    dve.wait_ge(rest_free, R_USES * b + R_Y + 3)
                    for c in range(QC):
                        nc.vector.tensor_scalar(x2o[:, c], x2[:, c], flag[:, 3, c:c + 1], None, ALU.add).then_inc(x2o_done, 1)
                    dve.nop(nofuse=True)
                    moments(b, 1, x2)

                def norm_2(b):
                    norm(b, 1, x2, xn2, xn2_done)

                def logits(b):
                    dve.wait_ge(rest_made, R_USES * b + R_LOGIT + 1)
                    nc.vector.tensor_copy(lg[:], w_ps[0:QP, 0:QC * E].rearrange("p (c e) -> p c e", c=QC)).then_inc(rest_free, 1)
                    dve.wait_ge(rest_free, R_USES * b + R_LOGIT + 2)
                    done(nc.vector.tensor_reduce(lmax[:], lg[:], AX_X, ALU.max), soft_step, SOFT * b + 1)
                    nc.vector.tensor_tensor(lg[:], lg[:], lmax[:].rearrange("p (c o) -> p c o", o=1).broadcast_to((QP, QC, E)), ALU.subtract).then_inc(lsub_done, 1)

                def affinity(b):
                    dve.wait_ge(lexp_done, b + 1)
                    done(nc.vector.tensor_reduce(lsum[:], ex[:], AX_X, ALU.add), soft_step, SOFT * b + 2)
                    done(nc.vector.reciprocal(lsum[:], lsum[:]), soft_step, SOFT * b + 3)
                    done(nc.vector.tensor_tensor(aff[:], ex[:], lsum[:].rearrange("p (c o) -> p c o", o=1).broadcast_to((QP, QC, E)), ALU.mult), soft_step, SOFT * b + 4)
                    for c in range(QC):
                        nc.vector.tensor_scalar(aff[:, c], aff[:, c], flag[:, 1, c:c + 1], None, ALU.add).then_inc(aff_done, 1)

                def rounds(b, which):
                    if 0 in which:
                        dve.wait_ge(rest_made, R_USES * b + R_AFF + 1)
                        nc.vector.tensor_copy(aff8[0][:], w_ps[0:E, 0:S]).then_inc(rest_free, 1)
                        hold(rest_free, R_USES * b + R_AFF + 2)
                    for r in which:
                        v8, i8 = top_v[:, 8 * r:8 * r + 8], top_i[:, 8 * r:8 * r + 8]
                        done(nc.vector.max(v8, aff8[r % 2][:]), soft_step, SOFT * b + 5 + 2 * r, alone=True)
                        nc.vector.max_index(i8, v8, aff8[r % 2][:])
                        done(nc.vector.match_replace(aff8[(r + 1) % 2][:], v8, aff8[r % 2][:], -8.0), soft_step, SOFT * b + 6 + 2 * r, alone=True)
                    if ROUNDS - 1 in which:
                        dve.wait_ge(out_stored, 16 * (b + 1))
                        dve.wait_ge(rows_stored, 16 * (b + 1))
                        nc.vector.tensor_copy(gate_all[:, ds(b, 1), :].rearrange("e o k -> e (o k)"), top_v[:])
                        done(nc.vector.tensor_copy(row_all[:, ds(b, 1), :].rearrange("e o k -> e (o k)"), top_i[:]), soft_step, SOFT * (b + 1))

                SOFT = 5 + 2 * ROUNDS

                def start():
                    nc.vector.memset(o_ps[:], 1.0).then_inc(sel_set, 1)
                    nc.vector.memset(flag[:], 0.0).then_inc(rest_free, 1)
                    dve.wait_ge(x_in, 16)
                    moments(0, 0, x_t)
                    norm(0, 0, x_t, xn, xn_done)
                    rotate(0)
                    sum_q(0)
                    low_q(0)
                    dve.wait_ge(fill_set, 3)
                    mask_queries(0)
                    for h in range(MLEAD):
                        maxima(0, h)
                    mask_keys(0, 0)

                def body(b, j, first, last):
                    for t in range(H):
                        if not last:
                            if t == 0:
                                dve.wait_ge(x_in, 16 * (b + 2))
                                moments(b + 1, 0, x_t)
                            if t == 6:
                                rotate(b + 1)
                            if t == 7:
                                sum_q(b + 1)
                            if t + MLEAD == H:
                                mask_queries(b + 1)
                        if not first:
                            if t in (6, 7):
                                residual(b - 1, t - 6)
                            if t == 7:
                                x2_out(b - 1)
                            if t == 11:
                                logits(b - 1)
                        if t + MLEAD < H:
                            maxima(b, t + MLEAD)
                        elif not last:
                            maxima(b + 1, t + MLEAD - H)
                        if not last:
                            if t == 0:
                                dve.wait_ge(ahead_made, F_USES * (b + 1))
                                norm(b + 1, 0, x_t, xn, xn_done)
                            if t == 8:
                                low_q(b + 1)
                            if t == 9:
                                mask_keys(b + 1, 1 - j)
                        if not first:
                            if t in (2, 3):
                                recip_sums(b - 1, 1, t - 2)
                            if t == 4:
                                normalise(b - 1, 1)
                            if t == 7:
                                norm_2(b - 1)
                            if t == 11:
                                affinity(b - 1)
                            if t == 13:
                                rounds(b - 1, (0, 1))
                            if t == 14:
                                rounds(b - 1, (2, 3))
                            if t == 15:
                                rounds(b - 1, (4, 5, 6))
                        if t in (9, 10):
                            recip_sums(b, 0, t - 9)
                        if t == 12:
                            normalise(b, 0)
                            flags(b)

                def end():
                    b = B - 1
                    for n in range(2):
                        recip_sums(b, 1, n)
                    normalise(b, 1)
                    residual(b, 0)
                    residual(b, 1)
                    x2_out(b)
                    norm_2(b)
                    logits(b)
                    affinity(b)
                    rounds(b, range(ROUNDS))

                every_batch(dve, start, body, end)

            @block.tensor
            def _(pe):
                def take_slot(b, u):
                    after(pe, m_free[u % 2], freed(b, u) - 1)

                def turn(src, n, s_):
                    for c in range(2 * n, 2 * n + 2):
                        for qc in range(QC):
                            a = c % 2 * S + qc * QP
                            mm = nc.tensor.transpose(w_ps[:, a:a + QP], src[:, qc, c * P:c * P + P], ident[0:QP, 0:QP])
                    mm.then_inc(s_, 1)

                def turn_x(b, n):
                    if n == 0:
                        pe.wait_ge(rest_free, 1 if isinstance(b, int) and b < 2 else R_USES * (b - 2) + 1)
                    else:
                        pe.wait_ge(ahead_free, F_USES * b + F_XT + n)
                    pe.wait_ge(xn_done, QC * (b + 1))
                    turn(xn, n, ahead_made)

                def project_q(b, n):
                    pe.wait_ge(ahead_free, F_USES * b + F_Q + n)
                    for g in range(2 * n, 2 * n + 2):
                        for c in range(DC):
                            mm = nc.tensor.matmul(w_ps[:, g % 2 * S:g % 2 * S + S], wq_sb[:, c, g * P:g * P + P],
                                                  xT[:, c // 2, c % 2 * S:c % 2 * S + S], start=(c == 0), stop=(c == DC - 1))
                    mm.then_inc(ahead_made, 1)

                def project_out(b, qc, last):
                    if qc == 0:
                        pe.wait_ge(ahead_free, F_USES * (B if last else b + 3))
                    pe.wait_ge(rest_free, R_USES * b + R_Y + qc + 1)
                    for a in range(2):
                        pe.wait_ge(cx_done[a], b + 1)
                    for t in range(2):
                        for a in range(2):
                            mm = nc.tensor.matmul(w_ps[0:QP, :], cx[:, a, t * S + qc * QP:t * S + qc * QP + QP],
                                                  wo_sb[:, 2 * t + a, :], start=(t == 0 and a == 0), stop=(t == 1 and a == 1))
                    mm.then_inc(rest_made, 1)

                def turn_x2(b, n):
                    pe.wait_ge(rest_free, R_USES * b + R_XNT + n + 1)
                    pe.wait_ge(xn2_done, QC * (b + 1))
                    turn(xn2, n, rest_made)

                def logits(b):
                    pe.wait_ge(rest_free, R_USES * b + R_LOGIT + 1)
                    for qc in range(QC):
                        for c in range(DC):
                            mm = nc.tensor.matmul(w_ps[0:QP, qc * E:qc * E + E],
                                                  xT[:, c // 2, c % 2 * S + qc * QP:c % 2 * S + qc * QP + QP],
                                                  gw_sb[:, c, :], start=(c == 0), stop=(c == DC - 1))
                    mm.then_inc(rest_made, 1)

                def turn_affinity(b):
                    pe.wait_ge(rest_free, R_USES * b + R_AFF + 1)
                    pe.wait_ge(aff_done, QC * (b + 1))
                    for qc in range(QC):
                        mm = nc.tensor.transpose(w_ps[0:E, qc * QP:qc * QP + QP], aff[:, qc, :], ident[0:QP, 0:QP])
                    mm.then_inc(rest_made, 1)

                def scores(b, h, qc):
                    if h % HG == 0 and qc == 0:
                        pe.wait_ge(qs_in[h // HG], 48 * (b + 1))
                    if h % 2 == 0 and qc == 0:
                        pe.wait_ge(ks_in[h // 2 % HG], 48 * (2 * b + h // KSLOTS + 1))
                    u = max_use(h, qc)
                    take_slot(b, u)
                    for n in range(2):
                        mm = nc.tensor.matmul(m_ps[u % 2][0:QP, n, 0:KN], qs[0:3 * WAYS, h, qc * QP:qc * QP + QP],
                                              ks[0:3 * WAYS, h % KSLOTS, n * KN:n * KN + KN], start=True, stop=True)
                    mm.then_inc(m_made, 1)

                def transpose_max(b, g):
                    u = neg_use(g)
                    take_slot(b, u)
                    for j in range(2):
                        last = max_use(g * HG + HG - 1, QC - 1 - j)
                        pe.wait_ge(m_free[last % 2], freed(b, last))
                    for qc in range(QC):
                        mm = nc.tensor.transpose(m_ps[u % 2][:, 0, qc * QP:qc * QP + QP], mx[:, g % 2, qc, :], ident[0:QP, 0:QP])
                    mm.then_inc(m_made, 1)

                def scores_t(b, j, h, pc):
                    if h % HG == 0 and pc == 0:
                        u = neg_use(h // HG)
                        pe.wait_ge(m_free[u % 2], freed(b, u))
                    if h == 0 and pc == 0:
                        pe.wait_ge(mt_done, b + 1)
                    n = h * (KC // 2) + pc
                    after(pe, *exp_at(b, h, pc - 2))
                    o = s_ps[n % 2][0:KP, 0:PAIR]
                    nc.tensor.matmul(o, identb[0:KP, 0:KP], mt[j][:, 2 * pc:2 * pc + 2, :].rearrange("p c s -> p (c s)"), start=True, stop=False)
                    for k in range(2):
                        c = 2 * pc + k
                        mm = nc.tensor.matmul(o[:, k * S:k * S + S], ks[:, h % KSLOTS, c * KP:c * KP + KP], qs[:, h, :],
                                              start=False, stop=(k == 1))
                    mm.then_inc(s_made, 1)

                def values(b, h):
                    if h % VH == 0:
                        pe.wait_ge(vs_in[h // VH], 16 * b + 16)
                    if h % 2 == 0:
                        after(pe, copied, H // 2 * b + h // 2)
                    o = o_ps[0:VW, h % 2 * S:h % 2 * S + S]
                    for c in range(KC):
                        if c % 2 == 0:
                            pe.wait_ge(plo_done[c // 2], H * b + h + 1)
                        w = vs[h // VH][:, c, h % VH, :]
                        k = slice(c % 2 * S, c % 2 * S + S)
                        nc.tensor.matmul(o, w, p_hi[h % 2][:, c // 2, k], start=(c == 0), stop=False)
                        mm = nc.tensor.matmul(o, w, p_lo[h % 2][:, c // 2, k], start=False, stop=(c == KC - 1))
                    mm.then_inc(pv_done[h // VH][h % 2], 1)

                def start():
                    for n in range(2):
                        turn_x(0, n)
                    pe.wait_ge(wq_in, 16)
                    for n in range(2):
                        project_q(0, n)
                    for h in range(HG):
                        for qc in range(QC):
                            scores(0, h, qc)
                    transpose_max(0, 0)
                    for qc in range(QC):
                        scores(0, HG, qc)
                    pe.wait_ge(sel_set, 4)
                    pe.wait_ge(att_in, 32)
                    for pc in range(KC // 2):
                        scores_t(0, 0, 0, pc)

                def body(b, j, first, last):
                    for t in range(H):
                        def next_scores(pc):
                            if t + 1 < H:
                                scores_t(b, j, t + 1, pc)
                            elif not last:
                                scores_t(b + 1, 1 - j, 0, pc)

                        def last_values():
                            if t:
                                values(b, t - 1)
                            elif not first:
                                values(b - 1, H - 1)

                        def max_scores(qc):
                            if t + MLEAD < H:
                                scores(b, t + MLEAD, qc)
                            elif not last:
                                scores(b + 1, t + MLEAD - H, qc)

                        if (t + 1) % HG:
                            next_scores(0)
                            last_values()
                            next_scores(1)
                            max_scores(0)
                            max_scores(1)
                            next_scores(2)
                        else:
                            last_values()
                            if t + 1 < H:
                                transpose_max(b, (t + 1) // HG)
                            elif not last:
                                transpose_max(b + 1, 0)
                            max_scores(0)
                            next_scores(0)
                            max_scores(1)
                            next_scores(1)
                            next_scores(2)
                        if not last:
                            if t in (1, 2):
                                turn_x(b + 1, t - 1)
                            if t in (3, 4):
                                project_q(b + 1, t - 3)
                        if not first:
                            if t in (5, 6):
                                project_out(b - 1, t - 5, last)
                            if t in (8, 9):
                                turn_x2(b - 1, t - 8)
                            if t == 10:
                                logits(b - 1)
                            if t == 12:
                                turn_affinity(b - 1)

                def end():
                    b = B - 1
                    values(b, H - 1)
                    for qc in range(QC):
                        project_out(b, qc, True)
                    for n in range(2):
                        turn_x2(b, n)
                    logits(b)
                    turn_affinity(b)

                every_batch(pe, start, body, end)


def experts(nc, sem, sb, ps, wstream, xn_rows, out_rows, cst, ident, gains, gate_all, row_all):
    with ExitStack() as st:
        w_raw = [sb(st, f"w_raw{j}", [P, UNIT]) for j in range(NRAW)]
        w_hi = [sb(st, f"ws_hi{j}", [P, UNIT], F32R) for j in range(NRAW)]
        w_lo = [sb(st, f"ws_lo{j}", [P, UNIT], F32R) for j in range(NRAW)]
        rows_f = sb(st, "rows_f", [E, SLOTS])
        gate_t = sb(st, "gate_t", [RP, E, RG])
        idx_t = sb(st, "idx_t", [RP, E, RG], U32)
        gather_i, scatter_i = sb(st, "gather_i", [RP, RG], U32), sb(st, "scatter_i", [RP, RG], U32)
        xg = sb(st, "xg", [RP, RG, D])
        xs_hi, xs_lo = sb(st, "xs_hi", [P, DC, SLOTS], F32R), sb(st, "xs_lo", [P, DC, SLOTS], F32R)
        silu = [sb(st, f"silu{j}", [P, SLOTS]) for j in range(2)]
        hid = [sb(st, f"hid{j}", [P, SLOTS]) for j in range(2)]
        h_hi, h_lo = sb(st, "h_hi", [P, IC, SLOTS], F32R), sb(st, "h_lo", [P, IC, SLOTS], F32R)
        y_cols = sb(st, "y_cols", [P, DC, SLOTS])
        y_sb = sb(st, "y_sb", [RP, RG, D])
        gu_ps = [ps(st, f"gu_ps{j}", [P, 512]) for j in range(4)]
        y_ps = [ps(st, f"y_ps{j}", [P, 512]) for j in range(RG)]

        w_in = [sem(f"w_in{j}") for j in range(NRAW)]
        whi_done, wlo_done = sem("whi_done"), [sem(f"wlo_done{j}") for j in range(NRAW)]
        w_used = sem("w_used")
        rows_ready, turned, gates_ready, idx_ready = sem("rows_ready"), sem("turned"), sem("gates_ready"), sem("idx_ready")
        gidx_done, sidx_done = sem("gidx_done"), sem("sidx_done")
        gathered, x_turned, xhi_done, xlo_done = sem("gathered"), sem("x_turned"), sem("xhi_done"), sem("xlo_done")
        silu_done, hid_done = sem("silu_done"), [sem(f"hid_done{j}") for j in range(2)]
        hhi_done, hlo_done = sem("hhi_done"), sem("hlo_done")
        cols_act, cols_dve, y_turned = sem("cols_act"), sem("cols_dve"), sem("y_turned")
        y_act, y_dve, scattered = sem("y_act"), sem("y_dve"), sem("scattered")

        def ahead(e, u):
            return (e, u + LEAD) if u + LEAD < NU else (e + 1, u + LEAD - NU)

        def raw_uses(e, u):
            return NU // NRAW * e + u // NRAW

        with nc.Block() as block:
            @block.sync
            def _(sp):
                def hold(s_, v_):
                    sp.wait_ge(s_, v_)
                    sp.nop(nofuse=True)

                def load(e, u):
                    s = u % NRAW
                    if not (isinstance(e, int) and u < NRAW):
                        hold(wlo_done[s], raw_uses(e, u))
                    sp.dma_start(w_raw[s][:], wstream[ds(NU * e + u, 1)].rearrange("o p n -> p (o n)")).then_inc(w_in[s], 16)

                for u in range(NU):
                    load(0, u)
                with sp.Fori(1, E) as e:
                    for u in range(NU):
                        load(e, u)

            @block.gpsimd
            def _(pool):
                def hold(s_, v_):
                    if not (isinstance(v_, int) and v_ <= 0):
                        pool.wait_ge(s_, v_)
                        pool.nop(nofuse=True)

                def gather(e):
                    hold(x_turned, e)
                    hold(gathered, 16 * RG * e)
                    nc.gpsimd.tensor_copy(gather_i[:], idx_t[:, ds(e, 1), :].rearrange("p o g -> p (o g)")).then_inc(gidx_done, 1)
                    hold(gidx_done, e + 1)
                    for g in range(RG):
                        pool.indirect_dma_start(xg[:, g, :], None, xn_rows, bass.IndirectOffsetOnAxis(gather_i[:, g:g + 1], 0)).then_inc(gathered, 16)

                def scatter(e):
                    hold(scattered, 16 * RG * e)
                    nc.gpsimd.tensor_copy(scatter_i[:], idx_t[:, ds(e, 1), :].rearrange("p o g -> p (o g)")).then_inc(sidx_done, 1)
                    hold(sidx_done, e + 1)
                    hold(y_act, RG // 2 * (e + 1))
                    hold(y_dve, RG // 2 * (e + 1))
                    for g in range(RG):
                        pool.indirect_dma_start(out_rows, bass.IndirectOffsetOnAxis(scatter_i[:, g:g + 1], 0), y_sb[:, g, :], None,
                                                compute_op=ALU.add).then_inc(scattered, 16)

                pool.wait_ge(idx_ready, 1)
                gather(0)
                gather(1)
                scatter(0)
                with pool.Fori(1, E - 1) as e:
                    gather(e + 1)
                    scatter(e)
                scatter(E - 1)
                pool.wait_ge(scattered, 16 * RG * E)

            @block.scalar
            def _(act):
                def split_w(e, u):
                    s = u % NRAW
                    act.wait_ge(w_in[s], 16 * (raw_uses(e, u) + 1))
                    after(act, w_used, NU * e + u - NRAW + 1)
                    nc.scalar.activation(w_hi[s][:], w_raw[s][:], ACT.Copy).then_inc(whi_done, 1)

                def split_x(e):
                    act.wait_ge(x_turned, e + 1)
                    for c in range(DC):
                        nc.scalar.activation(xs_hi[:, c], gu_ps[c][:, 0:SLOTS], ACT.Copy).then_inc(xhi_done, 1)

                def scale_rows(e):
                    act.wait_ge(y_turned, e + 1)
                    act.nop(nofuse=True)
                    for g in range(RG // 2):
                        nc.scalar.activation(y_sb[:, g], y_ps[g][0:RP, :], ACT.Copy,
                                             scale=gate_t[:, ds(e, 1), g:g + 1].rearrange("p o g -> p (o g)")).then_inc(y_act, 1)

                def expert(e, first, last):
                    for u in range(NU):
                        if not (last and u + LEAD >= NU):
                            split_w(*ahead(e, u))
                        if u < GU:
                            act.wait_ge(w_used, NU * e + u + 1)
                            nc.scalar.activation(silu[u % 2][:], gu_ps[u % 2 * 2][:, 0:SLOTS], ACT.Silu).then_inc(silu_done, 1)
                            act.wait_ge(hid_done[u % 2], GU // 2 * e + u // 2 + 1)
                            nc.scalar.activation(h_hi[:, u], hid[u % 2][:], ACT.Copy).then_inc(hhi_done, 1)
                        if u == 3 and not first:
                            scale_rows(e - 1)
                        if u == GU + 1 and not last:
                            split_x(e + 1)
                    after(act, y_turned, e)
                    after(act, scattered, 16 * RG * e)
                    act.wait_ge(w_used, NU * (e + 1))
                    for d in range(DC // 2):
                        nc.scalar.activation(y_cols[:, d], y_ps[d][:, 0:SLOTS], ACT.Copy).then_inc(cols_act, 1)

                for u in range(LEAD):
                    split_w(0, u)
                split_x(0)
                act.wait_ge(gates_ready, 1)
                expert(0, True, False)
                with act.Fori(1, E - 1) as e:
                    expert(e, False, False)
                expert(E - 1, False, True)
                scale_rows(E - 1)

            @block.vector
            def _(dve):
                def split_w(e, u):
                    s = u % NRAW
                    dve.wait_ge(whi_done, NU * e + u + 1)
                    nc.vector.tensor_tensor(w_lo[s][:], w_raw[s][:], w_hi[s][:], ALU.subtract).then_inc(wlo_done[s], 1)

                def split_x(e):
                    for c in range(DC):
                        dve.wait_ge(xhi_done, DC * e + c + 1)
                        nc.vector.tensor_tensor(xs_lo[:, c], gu_ps[c][:, 0:SLOTS], xs_hi[:, c], ALU.subtract).then_inc(xlo_done, 1)

                def scale_rows(e):
                    dve.wait_ge(y_turned, e + 1)
                    for g in range(RG // 2, RG):
                        nc.vector.tensor_scalar(y_sb[:, g], y_ps[g][0:RP, :], gate_t[:, ds(e, 1), g:g + 1].rearrange("p o g -> p (o g)"),
                                                None, ALU.mult).then_inc(y_dve, 1)

                def expert(e, first, last):
                    for u in range(NU):
                        if not (last and u + LEAD >= NU):
                            split_w(*ahead(e, u))
                        if u < GU:
                            dve.wait_ge(silu_done, GU * e + u + 1)
                            nc.vector.tensor_tensor(hid[u % 2][:], silu[u % 2][:], gu_ps[u % 2 * 2 + 1][:, 0:SLOTS],
                                                    ALU.mult).then_inc(hid_done[u % 2], 1)
                            dve.wait_ge(hhi_done, GU * e + u + 1)
                            nc.vector.tensor_tensor(h_lo[:, u], hid[u % 2][:], h_hi[:, u], ALU.subtract).then_inc(hlo_done, 1)
                        if u == 3 and not first:
                            scale_rows(e - 1)
                        if u == GU + 1 and not last:
                            split_x(e + 1)
                    after(dve, y_turned, e)
                    after(dve, scattered, 16 * RG * e)
                    dve.wait_ge(w_used, NU * (e + 1))
                    for d in range(DC // 2, DC):
                        nc.vector.tensor_copy(y_cols[:, d], y_ps[d][:, 0:SLOTS]).then_inc(cols_dve, 1)

                nc.vector.tensor_tensor(rows_f[:], row_all[:].rearrange("e b k -> e (b k)"), cst[0:E, C_ROW:C_ROW + SLOTS],
                                        ALU.add).then_inc(rows_ready, 1)
                dve.wait_ge(turned, 1)
                nc.vector.tensor_scalar(gate_t[:].rearrange("p e g -> p g e"), gu_ps[0][0:RP, 0:RG * E].rearrange("p (g e) -> p g e", g=RG),
                                        gains[0:RP, 1:2], None, ALU.mult).then_inc(gates_ready, 1)
                nc.vector.tensor_copy(idx_t[:].rearrange("p e g -> p g e"),
                                      gu_ps[0][0:RP, RG * E:2 * RG * E].rearrange("p (g e) -> p g e", g=RG)).then_inc(idx_ready, 1)
                for u in range(LEAD):
                    split_w(0, u)
                split_x(0)
                dve.wait_ge(gates_ready, 1)
                expert(0, True, False)
                with dve.Fori(1, E - 1) as e:
                    expert(e, False, False)
                expert(E - 1, False, True)
                scale_rows(E - 1)

            @block.tensor
            def _(pe):
                def turn_rows(e):
                    pe.wait_ge(gathered, 16 * RG * (e + 1))
                    for c in range(DC):
                        for g in range(RG):
                            mm = nc.tensor.transpose(gu_ps[c][:, g * RP:g * RP + RP], xg[:, g, c * P:c * P + P], ident[0:RP, 0:RP])
                    mm.then_inc(x_turned, 1)

                def gate_up(e, u):
                    s = u % NRAW
                    pe.wait_ge(wlo_done[s], raw_uses(e, u) + 1)
                    after(pe, hid_done[u % 2], GU // 2 * e + u // 2)
                    if u == 0:
                        pe.wait_ge(xlo_done, DC * (e + 1))
                    for k in range(2):
                        o = gu_ps[u % 2 * 2 + k][:, 0:SLOTS]
                        for c in range(DC):
                            w = slice((k * DC + c) * P, (k * DC + c + 1) * P)
                            nc.tensor.matmul(o, w_hi[s][:, w], xs_hi[:, c], start=(c == 0), stop=False)
                            nc.tensor.matmul(o, w_hi[s][:, w], xs_lo[:, c], start=False, stop=False)
                            mm = nc.tensor.matmul(o, w_lo[s][:, w], xs_hi[:, c], start=False, stop=(c == DC - 1))
                    mm.then_inc(w_used, 1)

                def down(e, v):
                    s = (GU + v) % NRAW
                    pe.wait_ge(wlo_done[s], raw_uses(e, GU + v) + 1)
                    pe.wait_ge(hlo_done, GU * e + 2 * v + 2)
                    if v == 0:
                        after(pe, y_act, RG // 2 * e)
                        after(pe, y_dve, RG // 2 * e)
                    for k in range(2):
                        i = 2 * v + k
                        for d in range(DC):
                            o, w = y_ps[d][:, 0:SLOTS], slice(k * D + d * P, k * D + d * P + P)
                            nc.tensor.matmul(o, w_hi[s][:, w], h_hi[:, i], start=(i == 0), stop=False)
                            nc.tensor.matmul(o, w_hi[s][:, w], h_lo[:, i], start=False, stop=False)
                            mm = nc.tensor.matmul(o, w_lo[s][:, w], h_hi[:, i], start=False, stop=(i == IC - 1))
                    mm.then_inc(w_used, 1)

                def turn_out(e):
                    pe.wait_ge(cols_act, DC // 2 * (e + 1))
                    pe.wait_ge(cols_dve, DC // 2 * (e + 1))
                    for g in range(RG):
                        for d in range(DC):
                            mm = nc.tensor.transpose(y_ps[g][0:RP, d * P:d * P + P], y_cols[:, d, g * RP:g * RP + RP], ident)
                    mm.then_inc(y_turned, 1)

                def expert(e, first, last):
                    for u in range(GU):
                        gate_up(e, u)
                        if u == 1 and not first:
                            turn_out(e - 1)
                    for v in range(DU):
                        down(e, v)
                        if v == 1 and not last:
                            for j in range(2):
                                pe.wait_ge(hid_done[j], GU // 2 * (e + 1))
                            turn_rows(e + 1)

                pe.wait_ge(rows_ready, 1)
                for g in range(RG):
                    nc.tensor.transpose(gu_ps[0][0:RP, g * E:g * E + E], gate_all[:].rearrange("e b k -> e (b k)")[:, g * RP:g * RP + RP],
                                        ident[0:E, 0:E])
                for g in range(RG):
                    mm = nc.tensor.transpose(gu_ps[0][0:RP, (RG + g) * E:(RG + g) * E + E], rows_f[:, g * RP:g * RP + RP], ident[0:E, 0:E])
                mm.then_inc(turned, 1)
                pe.wait_ge(idx_ready, 1)
                turn_rows(0)
                expert(0, True, False)
                with pe.Fori(1, E - 1) as e:
                    expert(e, False, False)
                expert(E - 1, False, True)
                turn_out(E - 1)


def kernel(x, ctx_1024, mask_Bx1xSxS2_ik0, g_xattn, g_ffn, L0_xattn_W_q, L0_xattn_W_k, L0_xattn_W_v, L0_xattn_W_o,
           L0_ffn_gate_w, L0_ffn_w_gate, L0_ffn_w_up, L0_ffn_w_down):
    import numpy as np
    import concourse.bacc as bacc
    from concourse.bass_utils import run_bass_kernel_spmd

    f = np.float32
    arr = np.asarray

    consts = np.zeros((P, C_END), f)
    consts[:, C_ID:C_ID + P] = np.eye(P, dtype=f)
    inv_freq = (f(1.0) / f(10000.0) ** (np.arange(0, DK, 2, dtype=f) / f(DK))).astype(f)
    angles = np.outer(np.arange(S2, dtype=f), inv_freq).astype(f)
    angles = np.concatenate([angles, angles], axis=1).T
    sign = np.where(np.arange(DK) < DK // 2, f(-1), f(1))[:, None]
    rotations = np.zeros((P, 2, SK), f)
    rotations[:, 0, 0:S2] = np.tile(np.cos(angles), (P // DK, 1))
    rotations[:, 1, 0:S2] = np.tile(np.sin(angles) * sign, (P // DK, 1))
    consts[:, C_COS:C_SIN + S] = rotations[:, :, 0:S].reshape(P, 2 * S)
    consts[3 * WAYS:3 * WAYS + HG, C_KSEL:C_KSEL + HG] = np.eye(HG, dtype=f)
    consts[0:E, C_ROW:] = np.repeat(np.arange(B) * S, TOPK)[None]

    def columns(w):
        return arr(w).T.reshape(DC, P, -1).transpose(1, 0, 2)

    turns = [head_of(h) for h in range(H)]
    wv = arr(L0_xattn_W_v).reshape(H, DK, D)[turns].reshape(D, D)
    wo = arr(L0_xattn_W_o).T.reshape(H, DK, D)[turns].reshape(2, 4, 2, DK, D).transpose(1, 3, 2, 0, 4).reshape(P, DC, D)
    ctxT = arr(ctx_1024).transpose(0, 2, 1).reshape(B, DC, P, S2).transpose(0, 2, 1, 3)
    mask = arr(mask_Bx1xSxS2_ik0).reshape(B, S, S2)
    maskq = mask.reshape(B, QC, QP, S2).transpose(0, 2, 1, 3)
    maskt = mask.transpose(0, 2, 1).reshape(B, KC, KP, S).transpose(0, 2, 1, 3)
    wg, wu, wd = arr(L0_ffn_w_gate), arr(L0_ffn_w_up), arr(L0_ffn_w_down)
    wstream = np.empty((E, NU, P, UNIT), f)
    for k, w in ((0, wg), (1, wu)):
        wstream[:, 0:GU].reshape(E, GU, P, 2, DC, P)[:, :, :, k] = w.reshape(E, IC, P, DC, P).transpose(0, 1, 4, 3, 2)
    wstream[:, GU:] = wd.transpose(0, 2, 1).reshape(E, DU, 2, P, D).transpose(0, 1, 3, 2, 4).reshape(E, DU, P, UNIT)

    arrays = {
        "ctxT": ctxT, "x_rows": arr(x).reshape(B, QC, QP, D).transpose(0, 2, 1, 3), "maskq": maskq, "maskt": maskt,
        "wk": columns(L0_xattn_W_k), "wv": columns(wv), "wq": columns(L0_xattn_W_q), "wo": wo,
        "gatew": columns(L0_ffn_gate_w), "gx": np.broadcast_to(arr(g_xattn), (P, 1)), "gf": np.broadcast_to(arr(g_ffn), (P, 1)),
        "wstream": wstream.reshape(E * NU, P, UNIT), "consts": consts, "rotations": rotations,
    }
    arrays = {n: np.ascontiguousarray(a) for n, a in arrays.items()}
    nc = bacc.Bacc("TRN2", target_bir_lowering=False, num_devices=1)
    args = [nc.dram_tensor(n, a.shape, mybir.dt.from_np(a.dtype), kind="ExternalInput").ap() for n, a in arrays.items()]
    out = nc.dram_tensor("out", (B, S, D), F32, kind="ExternalOutput").ap()
    (ctxT_, x_, mq_, mt_, wk_, wv_, wq_, wo_, gw_, gx_, gf_, ws_, cs_, rt_) = args
    program(nc, ctxT_, x_, mq_, mt_, wk_, wv_, wq_, wo_, gw_, gx_, gf_, ws_, cs_, rt_, out)
    r = run_bass_kernel_spmd(nc, [arrays], core_ids=[0])
    return r.results[0]["out"]
```
